# Optimizing a Trainium2 kernel written in Bass

```python
import numpy as np
import jax
import jax.numpy as jnp

def _softmax(x, axis=-1):
    return jax.nn.softmax(x, axis=axis)
def _gelu(x):
    return jax.nn.gelu(x, approximate=True)
def _silu(x):
    return jax.nn.silu(x)
def _sigmoid(x):
    return jax.nn.sigmoid(x)
def _layernorm(x, axis=-1, eps=1e-5):
    m = jnp.mean(x, axis=axis, keepdims=True)
    v = jnp.var(x, axis=axis, keepdims=True)
    return (x - m) / jnp.sqrt(v + eps)
def _scatter_add(tgt, idx, src, axis=0):
    return tgt.at[idx].add(src)
def _segment_sum(src, seg, n):
    return jax.ops.segment_sum(src, seg, n)

kernel_name = 'mk_conv_attn_hybrid_d2_conv_nchw256_a6ef21'

def setup_inputs(seed: int = 0):
    np.random.seed(seed)
    _w = jnp.asarray
    def _rec_inputs():
        import jax
        import jax.numpy as jnp
        _gk = jax.random.key(seed)
        x = -0.0002928 + 1 * jax.random.normal(jax.random.fold_in(_gk, 1), (4, 256, 64, 64), jnp.float32)
        return x
    x = _rec_inputs()
    def _L0_conv_setup():
        import jax, jax.numpy as jnp
        import numpy as np
        K_SIZE = 3
        PAD = K_SIZE // 2
        EPS = 1e-05

        def _forward(x, Wq, bq, Wk, bk, Wv, bv, Wo, bo):
            B, C, H, W = x.shape
            mean = jnp.mean(x, axis=(2, 3), keepdims=True)
            var = jnp.var(x, axis=(2, 3), keepdims=True)
            xn = (x - mean) * jax.lax.rsqrt(var + EPS)
            p = jnp.pad(xn, ((0, 0), (0, 0), (PAD, PAD), (PAD, PAD)))
            p = jnp.transpose(p, (0, 2, 3, 1))
            xc = jnp.transpose(xn, (0, 2, 3, 1))
            scale = jnp.asarray(C, x.dtype) ** (-0.5)
            q = (xc @ Wq + bq) * scale
            kf = p @ Wk + bk
            vf = p @ Wv + bv
            Kw = jnp.stack([kf[:, dh:dh + H, dw:dw + W, :] for dh in range(K_SIZE) for dw in range(K_SIZE)], axis=3)
            Vw = jnp.stack([vf[:, dh:dh + H, dw:dw + W, :] for dh in range(K_SIZE) for dw in range(K_SIZE)], axis=3)
            logits = jnp.einsum('bhwc,bhwnc->bhwn', q, Kw)
            attn = jax.nn.softmax(logits, axis=-1)
            ctx = jnp.einsum('bhwn,bhwnc->bhwc', attn, Vw)
            out = ctx @ Wo + bo
            return jnp.transpose(out, (0, 3, 1, 2))
        key = jax.random.key(seed)
        ks = jax.random.split(key, 9)
        B, C, H, W = (4, 256, 64, 64)
        Cout = 256
        sc = 1.0 / np.sqrt(C)
        return {'x': jax.random.normal(ks[0], (B, C, H, W), dtype=jnp.float32), 'Wq': jax.random.normal(ks[1], (C, C), dtype=jnp.float32) * sc, 'bq': jax.random.normal(ks[2], (C,), dtype=jnp.float32) * 0.02, 'Wk': jax.random.normal(ks[3], (C, C), dtype=jnp.float32) * sc, 'bk': jax.random.normal(ks[4], (C,), dtype=jnp.float32) * 0.02, 'Wv': jax.random.normal(ks[5], (C, C), dtype=jnp.float32) * sc, 'bv': jax.random.normal(ks[6], (C,), dtype=jnp.float32) * 0.02, 'Wo': jax.random.normal(ks[7], (C, Cout), dtype=jnp.float32) * sc, 'bo': jax.random.normal(ks[8], (Cout,), dtype=jnp.float32) * 0.02}
    _L0_conv_all = _L0_conv_setup()
    _L0_conv_in = {k: v for k, v in _L0_conv_all.items() if k in ('Wq', 'bq', 'Wk', 'bk', 'Wv', 'bv', 'Wo', 'bo', )}
    del _L0_conv_all

    def _L1_attn_setup():
        import jax, jax.numpy as jnp
        import numpy as np
        ATTWSIZE = 64

        def _windowed_sum(v, w):
            cs = jnp.cumsum(v, axis=1)
            T = v.shape[1]
            shifted = jnp.pad(cs, ((0, 0), (w, 0), (0, 0)))[:, :T, :]
            return cs - shifted
        key = jax.random.key(seed)
        k1, k2, k3 = jax.random.split(key, 3)
        B, T, D, A = (32, 4096, 256, 128)
        x = jax.random.normal(k1, (B, T, D), dtype=jnp.float32)
        Wp = jax.random.normal(k2, (A, D), dtype=jnp.float32) / np.sqrt(D).astype(np.float32)
        bp = jnp.zeros((A,), dtype=jnp.float32)
        Wg = jax.random.normal(k3, (1, A), dtype=jnp.float32) / np.sqrt(A).astype(np.float32)
        return {'x': x, 'Wp': Wp, 'bp': bp, 'Wg': Wg}
    _L1_attn_all = _L1_attn_setup()
    _L1_attn_in = {k: v for k, v in _L1_attn_all.items() if k in ('Wp', 'bp', 'Wg', )}
    del _L1_attn_all

    def _L1_ffn_setup():
        import jax, jax.numpy as jnp
        import numpy as np
        NUM_EXPERTS = 8
        TOP_K = 2
        B, S, D = (8, 8192, 256)

        def _moe(tokens, router_w, w1, b1, w2, b2):
            N = tokens.shape[0]
            E = router_w.shape[0]
            logits = tokens.astype(jnp.float32) @ router_w.astype(jnp.float32).T
            probs = jax.nn.softmax(logits, axis=-1)
            rw, re = jax.lax.top_k(probs, TOP_K)
            if TOP_K > 1:
                rw = rw / jnp.maximum(rw.sum(-1, keepdims=True), 1e-12)
            rw = rw.astype(tokens.dtype)
            combine = jnp.zeros((N, E), tokens.dtype).at[jnp.arange(N)[:, None], re].set(rw)
            out = tokens
            for e in range(E):
                h = jax.nn.gelu(tokens @ w1[e] + b1[e], approximate=False)
                y = h @ w2[e] + b2[e]
                out = out + combine[:, e:e + 1] * y
            return out
        key = jax.random.key(seed)
        ks = jax.random.split(key, 4)
        scale = 1.0 / np.sqrt(D).astype(np.float32)
        return {'input_embeddings': jax.random.normal(ks[0], (B, S, D), jnp.float32), 'router_w': jax.random.normal(ks[1], (NUM_EXPERTS, D), jnp.float32) * scale, 'w1': jax.random.normal(ks[2], (NUM_EXPERTS, D, D), jnp.float32) * scale, 'b1': jnp.zeros((NUM_EXPERTS, D), jnp.float32), 'w2': jax.random.normal(ks[3], (NUM_EXPERTS, D, D), jnp.float32) * scale, 'b2': jnp.zeros((NUM_EXPERTS, D), jnp.float32)}
    _L1_ffn_all = _L1_ffn_setup()
    _L1_ffn_in = {k: v for k, v in _L1_ffn_all.items() if k in ('router_w', 'w1', 'b1', 'w2', 'b2', )}
    del _L1_ffn_all

    return {
        "x": x,
        "L0_conv_Wq": _L0_conv_in["Wq"],
        "L0_conv_bq": _L0_conv_in["bq"],
        "L0_conv_Wk": _L0_conv_in["Wk"],
        "L0_conv_bk": _L0_conv_in["bk"],
        "L0_conv_Wv": _L0_conv_in["Wv"],
        "L0_conv_bv": _L0_conv_in["bv"],
        "L0_conv_Wo": _L0_conv_in["Wo"],
        "L0_conv_bo": _L0_conv_in["bo"],
        "L1_attn_Wp": _L1_attn_in["Wp"],
        "L1_attn_bp": _L1_attn_in["bp"],
        "L1_attn_Wg": _L1_attn_in["Wg"],
        "L1_ffn_router_w": _L1_ffn_in["router_w"],
        "L1_ffn_w1": _L1_ffn_in["w1"],
        "L1_ffn_b1": _L1_ffn_in["b1"],
        "L1_ffn_w2": _L1_ffn_in["w2"],
        "L1_ffn_b2": _L1_ffn_in["b2"],
    }

def reference(x, L0_conv_Wq, L0_conv_bq, L0_conv_Wk, L0_conv_bk, L0_conv_Wv, L0_conv_bv, L0_conv_Wo, L0_conv_bo, L1_attn_Wp, L1_attn_bp, L1_attn_Wg, L1_ffn_router_w, L1_ffn_w1, L1_ffn_b1, L1_ffn_w2, L1_ffn_b2):
    import jax
    import jax.numpy as jnp
    def _L0_conv_ref(x, Wq, bq, Wk, bk, Wv, bv, Wo, bo):
        import jax, jax.numpy as jnp
        import numpy as np
        K_SIZE = 3
        PAD = K_SIZE // 2
        EPS = 1e-05

        def _forward(x, Wq, bq, Wk, bk, Wv, bv, Wo, bo):
            B, C, H, W = x.shape
            mean = jnp.mean(x, axis=(2, 3), keepdims=True)
            var = jnp.var(x, axis=(2, 3), keepdims=True)
            xn = (x - mean) * jax.lax.rsqrt(var + EPS)
            p = jnp.pad(xn, ((0, 0), (0, 0), (PAD, PAD), (PAD, PAD)))
            p = jnp.transpose(p, (0, 2, 3, 1))
            xc = jnp.transpose(xn, (0, 2, 3, 1))
            scale = jnp.asarray(C, x.dtype) ** (-0.5)
            q = (xc @ Wq + bq) * scale
            kf = p @ Wk + bk
            vf = p @ Wv + bv
            Kw = jnp.stack([kf[:, dh:dh + H, dw:dw + W, :] for dh in range(K_SIZE) for dw in range(K_SIZE)], axis=3)
            Vw = jnp.stack([vf[:, dh:dh + H, dw:dw + W, :] for dh in range(K_SIZE) for dw in range(K_SIZE)], axis=3)
            logits = jnp.einsum('bhwc,bhwnc->bhwn', q, Kw)
            attn = jax.nn.softmax(logits, axis=-1)
            ctx = jnp.einsum('bhwn,bhwnc->bhwc', attn, Vw)
            out = ctx @ Wo + bo
            return jnp.transpose(out, (0, 3, 1, 2))
        return _forward(x, Wq, bq, Wk, bk, Wv, bv, Wo, bo)

    def _L1_attn_ref(x, Wp, bp, Wg):
        import jax, jax.numpy as jnp
        import numpy as np
        ATTWSIZE = 64

        def _windowed_sum(v, w):
            cs = jnp.cumsum(v, axis=1)
            T = v.shape[1]
            shifted = jnp.pad(cs, ((0, 0), (w, 0), (0, 0)))[:, :T, :]
            return cs - shifted
        proj = jnp.tanh(jnp.einsum('btd,ad->bta', x, Wp) + bp)
        g = jax.nn.sigmoid(jnp.einsum('bta,oa->bto', proj, Wg))
        wx = g * x
        num = _windowed_sum(wx, ATTWSIZE)
        den = _windowed_sum(g, ATTWSIZE)
        return num / den

    def _L1_ffn_ref(input_embeddings, router_w, w1, b1, w2, b2):
        import jax, jax.numpy as jnp
        import numpy as np
        NUM_EXPERTS = 8
        TOP_K = 2
        B, S, D = (8, 8192, 256)

        def _moe(tokens, router_w, w1, b1, w2, b2):
            N = tokens.shape[0]
            E = router_w.shape[0]
            logits = tokens.astype(jnp.float32) @ router_w.astype(jnp.float32).T
            probs = jax.nn.softmax(logits, axis=-1)
            rw, re = jax.lax.top_k(probs, TOP_K)
            if TOP_K > 1:
                rw = rw / jnp.maximum(rw.sum(-1, keepdims=True), 1e-12)
            rw = rw.astype(tokens.dtype)
            combine = jnp.zeros((N, E), tokens.dtype).at[jnp.arange(N)[:, None], re].set(rw)
            out = tokens
            for e in range(E):
                h = jax.nn.gelu(tokens @ w1[e] + b1[e], approximate=False)
                y = h @ w2[e] + b2[e]
                out = out + combine[:, e:e + 1] * y
            return out
        b, s, d = input_embeddings.shape
        tokens = input_embeddings.reshape(b * s, d)
        return _moe(tokens, router_w, w1, b1, w2, b2).reshape(b, s, d)

    def _gn(v, G=32, eps=1e-5):
        B_, C_, H_, W_ = v.shape
        g = v.reshape(B_, G, C_ // G, H_, W_)
        m = jnp.mean(g, axis=(2, 3, 4), keepdims=True)
        s = jnp.var(g, axis=(2, 3, 4), keepdims=True)
        return ((g - m) / jnp.sqrt(s + eps)).reshape(v.shape)

    def _ln_c(v, eps=1e-6):
        m = jnp.mean(v, axis=1, keepdims=True)
        s = jnp.var(v, axis=1, keepdims=True)
        return (v - m) / jnp.sqrt(s + eps)

    def _ln_t(v, eps=1e-5):
        m = jnp.mean(v, axis=-1, keepdims=True)
        s = jnp.var(v, axis=-1, keepdims=True)
        return (v - m) / jnp.sqrt(s + eps)

    def _to_tokens(v):
        B_, C_, H_, W_ = v.shape
        return v.reshape(B_, C_, H_ * W_).transpose(0, 2, 1)
    def _from_tokens(t, like):
        B_, C_, H_, W_ = like.shape
        return t.transpose(0, 2, 1).reshape(B_, C_, H_, W_)

    x = x + _L0_conv_ref(_gn(x), L0_conv_Wq, L0_conv_bq, L0_conv_Wk, L0_conv_bk, L0_conv_Wv, L0_conv_bv, L0_conv_Wo, L0_conv_bo)
    t = _to_tokens(x)
    t = t + _L1_attn_ref(_ln_t(t), L1_attn_Wp, L1_attn_bp, L1_attn_Wg)
    t = t + _L1_ffn_ref(_ln_t(t), L1_ffn_router_w, L1_ffn_w1, L1_ffn_b1, L1_ffn_w2, L1_ffn_b2)
    x = _from_tokens(t, x)
    return x


_drawn_inputs = setup_inputs


def setup_inputs(seed=0):
    import zlib

    import numpy as np

    out = dict(_drawn_inputs(seed))
    spreads = {'L1_attn_bp': (0.0, 2.0), 'L1_ffn_b1': (0.0, 0.333), 'L1_ffn_b2': (0.0, 0.1)}
    factors = {'L0_conv_bq': 4.208, 'L0_conv_bk': 64.0}
    for name, (base, spread) in spreads.items():
        noise = np.random.default_rng([zlib.crc32(name.encode()), seed]).standard_normal(out[name].shape)
        drawn = base * np.exp(spread * noise) if base else spread * noise
        out[name] = jnp.asarray(drawn.astype(out[name].dtype))
    for name, factor in factors.items():
        out[name] = (out[name] * factor).astype(out[name].dtype)
    return out
```

```python
import concourse.bass as bass
from concourse import mybir
from contextlib import ExitStack

LAG = {"N": -2, "A": -1, "B": 0, "C": 1, "D": 2}


class Iteration:

    def __init__(self, base, off, blocks):
        self.base, self.off, self.blocks = base, off, blocks

    def runs(self, stage):
        if self.base is not None:
            return True
        return 0 <= self.off - LAG[stage] < self.blocks

    def block(self, stage):
        at = self.off - LAG[stage]
        return at if self.base is None else self.base * 2 + at

    def pair(self, stage, back=0):
        at = (self.off - LAG[stage] - back) // 2
        return at if self.base is None else self.base + at

    def parity(self, stage):
        return (self.off - LAG[stage]) % 2

    def before(self):
        return Iteration(self.base, self.off - 1, self.blocks)


class Signal:

    def __init__(self, sem, order):
        self.sem, self.order = sem, order.split()

    def count(self, it, event):
        n = 0
        for e in self.order:
            n += 1 if it.runs(e[0]) else 0
            if e == event:
                break
        else:
            raise KeyError(event)
        slope = 0
        for e in self.order:
            lag = LAG[e[0]]
            if it.base is None:
                n += min(max(it.off - lag, 0), it.blocks)
            else:
                n += it.off - lag
                slope += 2
        return n if it.base is None else it.base * slope + n

    def wait(self, eng, it, event):
        if it.runs(event[0]):
            eng.wait_ge(self.sem, self.count(it, event))

    def wait_before(self, eng, it, event):
        n = self.count(it, event) - 1
        if it.base is not None or n > 0:
            eng.wait_ge(self.sem, n)


def hybrid(nc, x, wqT, wkT, wvT, wo, bq, bk, bv, bo, wpT, bp, wg, rwT, w1, b1, w2, b2, out):
    f32 = mybir.dt.float32
    f32r = mybir.dt.float32r
    bf16 = mybir.dt.bfloat16
    i32 = mybir.dt.int32
    u32 = mybir.dt.uint32
    ALU = mybir.AluOpType
    ACT = mybir.ActivationFunctionType
    AX = mybir.AxisListType

    P = 128
    NI, C, H, W = x.shape
    CC = C // P
    HW = H * W
    NT = NI * HW
    ROWS = 8
    BT = ROWS * W
    KT = BT // P
    IB = H // ROWS
    NB = NI * IB
    PW = W + 2
    NBR = 4 * PW
    REAL = 4 * W
    VC = KT + 1
    A = wpT.shape[1]
    E = rwT.shape[1]
    WIN = 64
    SCALE = float(C) ** -0.5
    EPS, TOKEN_EPS = 1e-5, 1e-5
    FAR = 1e30
    CAP = NT + BT
    NJ = 2 * NT // BT + E
    NJ += NJ % 2
    SPARE = NJ - 2 * NT // BT
    ROOM = E * CAP + SPARE * BT

    xv = x.rearrange("i (c p) h w -> p c i (h w)", p=P)
    ov = out.rearrange("i (c p) h w -> p c i (h w)", p=P)

    ctx = ExitStack()
    with ctx:
        def sb(name, shape, dt=f32):
            return ctx.enter_context(nc.sbuf_tensor(name, shape, dt))

        def sem(name):
            return ctx.enter_context(nc.semaphore(name))

        def sig(name, order):
            return Signal(sem(name), order)

        residual_v = nc.dram_tensor("residual", [NB, P, KT * C], f32).ap()
        sent = nc.dram_tensor("sent", [ROOM, C], f32).ap()
        answers = nc.dram_tensor("answers", [NJ * BT, C], f32).ap()

        ident = sb("ident", [P, P])
        group = sb("group", [P, P])
        ones = sb("ones", [P, P])
        onesb = sb("onesb", [P, P], bf16)
        earlier = sb("earlier", [P, P], bf16)
        band_cur = sb("band_cur", [P, P])
        band_prev = sb("band_prev", [P, P])
        far2 = sb("far2", [P, NBR])
        edge = sb("edge", [P, 1])
        halves = sb("halves", [P, 2, 4])
        expert_ids = sb("expert_ids", [P, E])
        wqk = sb("wqk", [P, CC, C])
        wqb = sb("wqb", [P, CC, 1])
        wvo = sb("wvo", [P, CC, C])
        r_bias = sb("r_bias", [P, CC, 1])
        q_const = sb("q_const", [P, 1])
        o_bias = sb("o_bias", [P, CC, 1])
        wp_s = sb("wp_s", [P, CC, A])
        bp_s = sb("bp_s", [P, 1])
        wg_s = sb("wg_s", [P, 1])
        rw_s = sb("rw_s", [P, CC, E])
        tab = sb("tab", [P, 6, CC, NB])
        keep = sb("keep", [P, NB])
        w1_s = sb("w1_s", [P, E, CC, C])
        w2_s = sb("w2_s", [P, E, CC, C])
        slots = sb("slots", [P, NB * KT, 2])
        mix = sb("mix", [P, NB * KT, 2])
        base = sb("base", [P, 1, E])
        base0 = sb("base0", [P, 1, E])

        m_bank = [ctx.enter_context(nc.psum_tensor(f"m_bank{i}", [P, 512], f32)) for i in range(4)]
        s_bank = [ctx.enter_context(nc.psum_tensor(f"s_bank{i}", [P, 512], f32)) for i in range(2)]
        t_bank = ctx.enter_context(nc.psum_tensor("t_bank", [P, 512], f32))
        o_bank = ctx.enter_context(nc.psum_tensor("o_bank", [P, 512], f32))

        prep = ExitStack()

        def pb(name, shape, dt=f32):
            return prep.enter_context(nc.sbuf_tensor(name, shape, dt))

        far = pb("far", [P, 4, PW])
        wq_s = pb("wq_s", [P, CC, C])
        wk_s = pb("wk_s", [P, CC, C])
        wv_s = pb("wv_s", [P, CC, C])
        wo_s = pb("wo_s", [P, CC, C])
        bq_s = pb("bq_s", [P, CC, 1])
        bk_s = pb("bk_s", [P, CC, 1])
        bv_s = pb("bv_s", [P, CC, 1])
        bo_s = pb("bo_s", [P, CC, 1])
        bqb = pb("bqb", [P, CC, P])
        XR = 8
        xs = pb("xs", [P, XR, CC, BT])
        stats = pb("stats", [P, CC, NB, 6])
        mv = pb("mv", [P, CC, NI, 2])
        g1 = pb("g1", [P, CC, NI])
        g2 = pb("g2", [P, CC, NI])
        g3 = pb("g3", [P, CC, NI])
        s_all = pb("s_all", [P, CC, NI])
        b_all = pb("b_all", [P, CC, NI])

        w_in = sem("w_in")
        w_experts = sem("w_experts")
        x_seen = [sem(f"x_seen{i}") for i in range(XR)]
        x_done = [sem(f"x_done{i}") for i in range(XR)]
        pool_const = sem("pool_const")
        dve_const = sem("dve_const")
        fold = sem("fold")
        folded = sem("folded")
        d0 = sem("d0")
        g_sum = sem("g_sum")
        roots = sem("roots")
        prepared = sem("prepared")
        passed = sem("passed")

        with nc.Block() as block:
            @block.sync
            def _(eng):
                n = 0
                for dst, src in ((wq_s, wqT), (wk_s, wkT), (wv_s, wvT), (wo_s, wo), (wp_s, wpT), (rw_s, rwT)):
                    eng.dma_start(dst[:, :, :], src.rearrange("(c p) n -> p c n", p=P)).then_inc(w_in, 16)
                for dst, src in ((bq_s, bq), (bk_s, bk), (bv_s, bv), (bo_s, bo)):
                    eng.dma_start(dst[:, :, :], src.unsqueeze(2)).then_inc(w_in, 16)
                eng.dma_start(bp_s[:, :], bp).then_inc(w_in, 16)
                eng.dma_start(wg_s[:, :], wg).then_inc(w_in, 16)
                for i in range(XR):
                    eng.dma_start(xs[:, i, :, :], xv[:, :, i // IB, i % IB * BT:(i % IB + 1) * BT])\
                       .then_inc(x_seen[i], 16)
                if NI > 1:
                    with eng.Fori(1, NI) as img:
                        for i in range(XR):
                            eng.wait_ge(x_done[i], img)
                            eng.dma_start(xs[:, i, :, :],
                                          xv[:, :, bass.ds(img, 1), i * BT:(i + 1) * BT])\
                               .then_inc(x_seen[i], 16)

                for dst, src in ((w1_s, w1), (w2_s, w2)):
                    for c in range(CC):
                        eng.dma_start(dst[:, :, c, :], src[:, c * P:(c + 1) * P, :].rearrange("e p n -> p e n"))\
                           .then_inc(w_experts, 16)

            @block.gpsimd
            def _(eng):
                done = 0
                eng.memset(ident[:, :], 0.0).then_inc(pool_const, 1)
                done += 1
                eng.wait_ge(pool_const, done)
                eng.memset(group[:, :], 0.125).then_inc(pool_const, 1)
                done += 1
                eng.wait_ge(pool_const, done)
                eng.memset(halves[:, :, :], -0.5).then_inc(pool_const, 1)
                done += 1
                eng.wait_ge(pool_const, done)
                eng.memset(ones[:, :], 1.0).then_inc(pool_const, 1)
                done += 1
                eng.wait_ge(pool_const, done)
                eng.memset(onesb[:, :], 1.0).then_inc(pool_const, 1)
                done += 1
                eng.wait_ge(pool_const, done)
                eng.memset(far[:, :, :], 0.0).then_inc(pool_const, 1)
                done += 1
                eng.wait_ge(pool_const, done)
                eng.iota(expert_ids[:, :], pattern=[[1, E]], base=0, channel_multiplier=0,
                         allow_small_or_imprecise_dtypes=True).then_inc(pool_const, 1)
                done += 1
                eng.wait_ge(pool_const, done)
                eng.iota(base0[:, 0, :], pattern=[[1, E]], base=0, channel_multiplier=0,
                         allow_small_or_imprecise_dtypes=True).then_inc(pool_const, 1)
                done += 1
                eng.wait_ge(pool_const, done)
                eng.affine_select(out=ident[:, :], in_=ident[:, :], compare_op=ALU.not_equal, fill=1.0,
                                  base=0, pattern=[[-1, P]], channel_multiplier=1).then_inc(pool_const, 1)
                done += 1
                eng.wait_ge(pool_const, done)
                gv = group[:, :].rearrange("p (a b) -> p a b", b=8)
                eng.affine_select(out=gv, in_=gv, compare_op=ALU.is_ge, fill=0.0,
                                  base=0, pattern=[[-8, P // 8], [0, 8]], channel_multiplier=1).then_inc(pool_const, 1)
                done += 1
                eng.wait_ge(pool_const, done)
                eng.affine_select(out=earlier[:, :], in_=onesb[:, :], compare_op=ALU.is_gt, fill=0.0,
                                  base=0, pattern=[[1, P]], channel_multiplier=-1).then_inc(pool_const, 1)
                done += 1
                eng.wait_ge(pool_const, done)
                eng.affine_select(out=band_cur[:, :], in_=ones[:, :], compare_op=ALU.is_ge, fill=0.0,
                                  base=0, pattern=[[1, P]], channel_multiplier=-1).then_inc(pool_const, 1)
                done += 1
                eng.wait_ge(pool_const, done)
                eng.affine_select(out=band_prev[:, :], in_=ones[:, :], compare_op=ALU.is_ge, fill=0.0,
                                  base=WIN - 1 - P, pattern=[[-1, P]], channel_multiplier=1).then_inc(pool_const, 1)
                done += 1
                eng.wait_ge(pool_const, done)
                for h in range(2):
                    fv = far[W * h:W * h + W, :, :]
                    eng.affine_select(out=fv, in_=fv, compare_op=ALU.is_ge, fill=FAR, base=0,
                                      pattern=[[0, 4], [1, PW]], channel_multiplier=-1).then_inc(pool_const, 1)
                    done += 1
                    eng.wait_ge(pool_const, done)
                eng.affine_select(out=gv, in_=gv, compare_op=ALU.is_ge, fill=0.0,
                                  base=7, pattern=[[8, P // 8], [0, 8]], channel_multiplier=-1).then_inc(pool_const, 1)
                done += 1
                eng.wait_ge(pool_const, done)
                eng.affine_select(out=band_cur[:, :], in_=band_cur[:, :], compare_op=ALU.is_ge, fill=0.0,
                                  base=WIN - 1, pattern=[[-1, P]], channel_multiplier=1).then_inc(pool_const, 1)
                done += 1
                eng.wait_ge(pool_const, done)
                for h in range(2):
                    fv = far[W * h:W * h + W, :, :]
                    eng.affine_select(out=fv, in_=fv, compare_op=ALU.is_ge, fill=FAR, base=2,
                                      pattern=[[0, 4], [-1, PW]], channel_multiplier=1).then_inc(pool_const, 1)
                    done += 1
                    eng.wait_ge(pool_const, done)
                eng.memset(far[0:W, 3, :], FAR).then_inc(pool_const, 1)
                done += 1
                eng.wait_ge(pool_const, done)
                eng.memset(far[W:P, 0, :], FAR).then_inc(pool_const, 1)
                done += 1
                eng.wait_ge(pool_const, done)
                eng.wait_ge(d0, 6)
                eng.tensor_tensor(g2[:, :, :], g2[:, :, :], halves[:, :, 0:NI], ALU.pow).then_inc(roots, 1)
                eng.wait_ge(d0, 9)
                eng.tensor_tensor(g3[:, :, :], g3[:, :, :], halves[:, :, 0:NI], ALU.pow).then_inc(roots, 1)

            @block.tensor
            def _(eng):
                eng.wait_ge(w_in, 16 * 12)
                eng.wait_ge(dve_const, 1)

                def product(bank, cols, lhs, rhs):
                    for d in range(CC):
                        last = eng.matmul(bank[:, cols], lhs(d), rhs(d), start=(d == 0), stop=(d == CC - 1))
                    return last
                for c in range(CC):
                    cs = slice(c * P, c * P + P)
                    product(m_bank[c], slice(0, C), lambda d: wq_s[:, d, cs], lambda d: wk_s[:, d, :])
                    product(m_bank[c], slice(C, C + 1), lambda d: wk_s[:, d, cs], lambda d: bq_s[:, d, :])
                    product(m_bank[c], slice(C + 1, C + 2), lambda d: wq_s[:, d, cs], lambda d: bk_s[:, d, :])
                    product(m_bank[2 + c], slice(0, C), lambda d: wv_s[:, d, cs], lambda d: wo_s[:, d, :])
                    product(m_bank[2 + c], slice(C, C + 1), lambda d: wo_s[:, d, cs], lambda d: bv_s[:, d, :])
                product(s_bank[0], slice(0, 1), lambda d: bqb[:, d, :], lambda d: bk_s[:, d, :]).then_inc(fold, 1)
                eng.wait_ge(pool_const, 21)
                eng.wait_ge(d0, 2)
                eng.matmul(s_bank[1][:, 0:CC * NI], group[:, :], g1[:, :, :].rearrange("p a b -> p (a b)"),
                           start=True, stop=True).then_inc(g_sum, 1)
                eng.wait_ge(d0, 5)
                eng.matmul(s_bank[1][:, 32:32 + CC * NI], group[:, :], g3[:, :, :].rearrange("p a b -> p (a b)"),
                           start=True, stop=True).then_inc(g_sum, 1)

            @block.vector
            def _(eng):
                eng.memset(keep[:, :], 1.0).then_inc(folded, 1)
                eng.wait_ge(w_in, 16 * 12)
                eng.tensor_copy(bqb[:, :, :], bq_s[:, :, :].broadcast_to([P, CC, P])).then_inc(dve_const, 1)
                eng.wait_ge(fold, 1)
                for c in range(CC):
                    eng.tensor_scalar(wqk[:, c, :], m_bank[c][:, 0:C], -SCALE, None, ALU.mult)
                    eng.tensor_scalar(r_bias[:, c, :], m_bank[c][:, C:C + 1], -SCALE, None, ALU.mult)
                    eng.tensor_scalar(wqb[:, c, :], m_bank[c][:, C + 1:C + 2], -SCALE, None, ALU.mult)
                    eng.tensor_copy(wvo[:, c, :], m_bank[2 + c][:, 0:C])
                    eng.tensor_tensor(o_bias[:, c, :], m_bank[2 + c][:, C:C + 1], bo_s[:, c, :], ALU.add)
                eng.tensor_scalar(q_const[:, :], s_bank[0][:, 0:1], -SCALE, None, ALU.mult).then_inc(folded, 1)
                for i in range(XR):
                    eng.wait_ge(x_seen[i], 16)
                    for c in range(CC):
                        last = eng.bn_stats(stats[:, c, i, :], xs[:, i, c, :])
                    last.then_inc(x_done[i], 1)
                if NI > 1:
                    with eng.Fori(1, NI) as img:
                        for i in range(XR):
                            eng.wait_ge(x_seen[i], img * 16 + 16)
                            for c in range(CC):
                                last = eng.bn_stats(stats[:, c, bass.ds(img * IB + i, 1), :], xs[:, i, c, :])
                            last.then_inc(x_done[i], 1)
                eng.wait_ge(x_done[XR - 1], NI)
                for c in range(CC):
                    for i in range(NI):
                        last = eng.bn_aggr(mv[:, c, i, :], stats[:, c, i * IB:(i + 1) * IB, :].rearrange("p a b -> p (a b)"))
                last.then_inc(d0, 1)
                eng.wait_ge(d0, 1)
                eng.tensor_copy(g1[:, :, :], mv[:, :, :, 0]).then_inc(d0, 1)
                eng.wait_ge(g_sum, 1)
                gm = s_bank[1][:, 0:CC * NI].rearrange("p (a b) -> p a b", a=CC)
                gv = s_bank[1][:, 32:32 + CC * NI].rearrange("p (a b) -> p a b", a=CC)
                eng.tensor_tensor(g2[:, :, :], g1[:, :, :], gm, ALU.subtract).then_inc(d0, 1)
                eng.wait_ge(d0, 3)
                eng.tensor_tensor(g2[:, :, :], g2[:, :, :], g2[:, :, :], ALU.mult).then_inc(d0, 1)
                eng.wait_ge(d0, 4)
                eng.tensor_tensor(g3[:, :, :], g2[:, :, :], mv[:, :, :, 1], ALU.add).then_inc(d0, 1)
                eng.wait_ge(g_sum, 2)
                eng.tensor_scalar(g2[:, :, :], gv, EPS, None, ALU.add).then_inc(d0, 1)
                eng.wait_ge(roots, 1)
                eng.tensor_tensor(g3[:, :, :], g2[:, :, :], g2[:, :, :], ALU.mult).then_inc(d0, 1)
                eng.wait_ge(d0, 7)
                eng.tensor_tensor(g3[:, :, :], g3[:, :, :], mv[:, :, :, 1], ALU.mult).then_inc(d0, 1)
                eng.wait_ge(d0, 8)
                eng.tensor_scalar(g3[:, :, :], g3[:, :, :], EPS, None, ALU.add).then_inc(d0, 1)
                eng.wait_ge(roots, 2)
                eng.tensor_tensor(s_all[:, :, :], g3[:, :, :], g2[:, :, :], ALU.mult).then_inc(d0, 1)
                eng.wait_ge(d0, 10)
                eng.scalar_tensor_tensor(b_all[:, :, :], g1[:, :, :], -1.0, s_all[:, :, :], ALU.mult, ALU.mult).then_inc(d0, 1)
                eng.wait_ge(d0, 11)
                for c in range(CC):
                    for kind in range(3):
                        for half, src in ((0, s_all), (1, b_all)):
                            last = eng.tensor_copy(
                                tab[:, 2 * kind + half, c, :].rearrange("p (i b) -> p i b", b=IB),
                                src[:, c, :].unsqueeze(2).broadcast_to([P, NI, IB]))
                last.then_inc(d0, 1)
                eng.wait_ge(d0, 12)
                tv = tab[:, :, :, :].rearrange("p k c (i b) -> p k c i b", b=IB)
                for k in range(2):
                    for c in range(CC):
                        eng.memset(tv[:, 2 + k, c, :, 0], 0.0)
                        eng.memset(tv[:, 4 + k, c, :, IB - 1], 0.0)
                eng.wait_ge(folded, 1)
                eng.memset(keep[:, :].rearrange("p (i b) -> p i b", b=IB)[:, :, 0], 0.0)
                eng.wait_ge(pool_const, 21)
                eng.tensor_copy(far2[:, 0:REAL].rearrange("p (a b) -> p a b", b=W), far[:, :, 1:W + 1])
                eng.tensor_copy(far2[:, REAL:REAL + 4], far[:, :, 0])
                eng.tensor_copy(far2[:, REAL + 4:NBR], far[:, :, PW - 1])
                eng.tensor_reduce(edge[:, :], far[:, :, 0:PW:PW - 1], AX.XY, ALU.min)
                eng.tensor_scalar(base[:, 0, :], base0[:, 0, :], float(CAP), None, ALU.mult).then_inc(prepared, 1)

        prep.close()
        loop1 = ExitStack()

        def lb(name, shape, dt=f32):
            return loop1.enter_context(nc.sbuf_tensor(name, shape, dt))

        raw = lb("raw", [P, 2, CC, BT + 2 * W])
        band = lb("band", [P, 2, CC, (ROWS + 2) * W])
        xb = lb("xb", [P, 2, CC, BT])
        rT = lb("rT", [P, 2, CC, BT])
        vv = lb("vv", [P, 2, VC, C])
        sm = lb("sm", [P, 2, NBR])
        ex = lb("ex", [P, 2, NBR])
        at = lb("at", [P, 2, 2, P])
        xt = lb("xt", [P, KT, C])
        lowest = lb("lowest", [P, KT])
        qb = lb("qb", [P, KT])
        shift = lb("shift", [P, KT])
        den = lb("den", [P, KT])
        rden = lb("rden", [P, KT])
        tt = lb("tt", [P, 2, KT, C])
        bn6 = lb("bn6", [P, KT, 6])
        mv4 = lb("mv4", [P, KT, 2])
        ve = lb("ve", [P, KT])
        rs = lb("rs", [P, KT])
        xn1 = lb("xn1", [P, KT, C + 1])
        xn1T = lb("xn1T", [P, CC, BT])
        pT = lb("pT", [P, BT])
        eg = lb("eg", [P, KT])
        gg = lb("gg", [P, KT])
        wx = lb("wx", [P, 2, KT, C + 1])
        wprev = lb("wprev", [P, C + 1])
        wden = lb("wden", [P, KT])
        tn = lb("tn", [P, 2, KT, C])
        tnT = lb("tnT", [P, CC, BT])
        rsum = lb("rsum", [P, 2, KT, C])
        logit = lb("logit", [P, KT, E])
        best = lb("best", [P, KT, 8])
        besti = lb("besti", [P, KT, 8], u32)
        down = lb("down", [P, KT, 8])
        e8 = lb("e8", [P, KT, 8])
        zsum = lb("zsum", [P, KT, 1])
        p12 = lb("p12", [P, KT, 2])
        psum2 = lb("psum2", [P, KT, 1])
        idf = lb("idf", [P, KT, 2])
        hot = lb("hot", [P, 2, KT, E])
        chosen = lb("chosen", [P, KT, E], bf16)
        where = lb("where", [P, KT, E])
        prod = lb("prod", [P, 2, KT, E])
        slotf = lb("slotf", [P, 2, KT])
        slot_s = lb("slot_s", [P, 2, 2, KT], i32)

        JOBS = ("AV01 Ctr01 Ctr23 BX01 Cproj Cgate BX23 Dtr01 Dtr23 AV23 Drouter Cwin0 Cwin1 AV4 "
                "Cwin2 Cwin3 AR0 AR1 Dpos").split()
        bank_of = {job: i % 4 for i, job in enumerate(JOBS)}
        orders = [" ".join(j for j in JOBS if bank_of[j] == i) for i in range(4)]
        full = [sig(f"full{i}", orders[i]) for i in range(4)]
        taken = [sig(f"taken{i}", orders[i]) for i in range(4)]
        s_full = [sig(f"s_full{i}", f"BS{i} BS{i + 2}") for i in range(2)]
        s_taken = [sig(f"s_taken{i}", f"BS{i} BS{i + 2}") for i in range(2)]
        tiles = lambda s: " ".join(f"{s}{k}" for k in range(KT))
        at_full = sig("at_full", tiles("BAT"))
        at_taken = sig("at_taken", tiles("BAT"))
        o_full = sig("o_full", tiles("BAV"))
        t_ready = sig("t_ready", tiles("Bt"))
        exp_ready = sig("exp_ready", tiles("BE"))
        masked = sig("masked", tiles("BM"))
        rden_ready = sig("rden_ready", tiles("Brd"))
        ln_step = sig("ln_step", "Cst1 Cag1 Cve1 Cxn1 Cst2 Cag2 Cve2 Ctn")
        root = sig("root", "Crs1 Crs2")
        prev_ready = sig("prev_ready", "Cprev")
        gate_step = sig("gate_step", "Cg1 Cg")
        wx_ready = sig("wx_ready", tiles("Cwx"))
        wden_ready = sig("wden_ready", tiles("Cwd"))
        sum_ready = sig("sum_ready", "CR")
        route = sig("route", "Dbest Dbesti Ddown Dz Dzi Dp Dps Dpm Dpi Dmix Didf Dhot DM "
                             "Dwhere Dbase Dprod Dslotf Dsl")
        rexp = sig("rexp", "DE")
        main_ready = sig("main_ready", "Nmain")
        halo_ready = sig("halo_ready", "Nhalo")
        xb_ready = sig("xb_ready", "Nxb")
        x_in = [sem(f"x_in{i}") for i in range(2)]
        sum_out = [sem(f"sum_out{i}") for i in range(2)]
        scattered = [sem(f"scattered{i}") for i in range(2)]
        cleared = sem("cleared")

        def alone(eng, *waits):
            for s, v in waits:
                eng.wait_ge(s, v)
            eng.sem_inc(passed, 1)

        def iterations(eng, body):
            for off in range(-2, 2):
                body(Iteration(None, off, NB))
            with eng.Fori(1, NB // 2 - 1) as half:
                for off in range(2):
                    body(Iteration(half, off, NB))
            for off in range(NB - 2, NB + 2):
                body(Iteration(None, off, NB))

        def column(ap, at):
            return ap[:, at:at + 1] if isinstance(at, int) else ap[:, bass.ds(at, 1)]

        flat = "p a b -> p (a b)"

        with nc.Block() as block:
            @block.sync
            def _(eng):
                eng.wait_ge(prepared, 1)

                def body(it):
                    if it.runs("N"):
                        par, blk = it.parity("N"), it.block("N")
                        two = it.before().before()
                        main_ready.wait(eng, two, "Nmain")
                        halo_ready.wait(eng, two, "Nhalo")
                        xb_ready.wait(eng, two, "Nxb")
                        img, row = blk // IB, blk % IB
                        for at, n, r in ((W, BT, row * ROWS), (0, W, (row * ROWS + H - 1) % H),
                                         (W + BT, W, (row * ROWS + ROWS) % H)):
                            src = xv[:, :, bass.ds(img, 1), bass.ds(r * W, n)]
                            eng.dma_start(raw[:, par, :, at:at + n], src).then_inc(x_in[par], 16)
                    if it.runs("C"):
                        par, blk = it.parity("C"), it.block("C")
                        sum_ready.wait(eng, it, "CR")
                        eng.dma_start(residual_v[bass.ds(blk, 1), :, :], rsum[:, par, :, :].rearrange(flat))\
                           .then_inc(sum_out[par], 16)
                iterations(eng, body)
                for i in range(2):
                    eng.wait_ge(sum_out[i], 16 * (NB // 2))

            @block.tensor
            def _(eng):
                eng.wait_ge(prepared, 1)
                eng.wait_ge(cleared, 5)

                def begin(it, job):
                    taken[bank_of[job]].wait_before(eng, it, job)
                    return m_bank[bank_of[job]]

                def end(last, job):
                    last.then_inc(full[bank_of[job]].sem, 1)

                def moved(it, job):
                    taken[bank_of[job]].wait(eng, it, job)

                def logits(it, k):
                    par = it.parity("B")
                    if k == 0:
                        moved(it.before(), "AR0")
                        moved(it.before(), "AR1")
                    s_taken[k % 2].wait_before(eng, it, f"BS{k}")
                    bank = s_bank[k % 2]
                    for c in range(CC):
                        eng.matmul(bank[:, 0:REAL], rT[:, par, c, k * P:(k + 1) * P],
                                   band[:, par, c, k * P:k * P + REAL],
                                   start=(c == 0), stop=(c == CC - 1))
                    for c in range(CC):
                        last = eng.matmul(bank[:, REAL:REAL + 1], band[:, par, c, k * P + W:k * P + W + P],
                                          wqb[:, c, :], start=(c == 0), stop=(c == CC - 1))
                    last.then_inc(s_full[k % 2].sem, 1)

                def attend(it, k):
                    par = it.parity("B")
                    exp_ready.wait(eng, it, f"BE{k}")
                    at_taken.wait_before(eng, it, f"BAT{k}")
                    for j in range(2):
                        last = eng.transpose(t_bank[:, j * P:(j + 1) * P], ex[:, k % 2, j * P:(j + 1) * P],
                                             ident[:, :])
                    last.then_inc(at_full.sem, 1)

                def weigh(it, k):
                    par = it.parity("B")
                    at_taken.wait(eng, it, f"BAT{k}")
                    t_ready.wait_before(eng, it, f"Bt{k}")
                    if k == 0:
                        for job in ("AV01", "AV23", "AV4"):
                            moved(it.before(), job)
                    for j in range(2):
                        last = eng.matmul(o_bank[:, 0:C], at[:, k % 2, j, :], vv[:, par, k + j, :],
                                          start=(j == 0), stop=(j == 1))
                    last.then_inc(o_full.sem, 1)

                def transposed(it, job, src, k0, per_tile):
                    bank = begin(it, job)
                    for k in (k0, k0 + 1):
                        for c in range(CC):
                            col = (k - k0) * C + c * P if per_tile else c * 2 * P + (k - k0) * P
                            last = eng.transpose(bank[:, col:col + P], src(k, c), ident[:, :])
                    end(last, job)

                def values(it, job, chunks):
                    par = it.parity("A")
                    if job == "AV01":
                        main_ready.wait(eng, it.before(), "Nmain")
                        halo_ready.wait(eng, it.before(), "Nhalo")
                    bank = begin(it, job)
                    for j in chunks:
                        for c in range(CC):
                            last = eng.matmul(bank[:, (j - chunks[0]) * C:(j - chunks[0] + 1) * C],
                                              band[:, par, c, j * P:(j + 1) * P], wvo[:, c, :],
                                              start=(c == 0), stop=(c == CC - 1))
                    end(last, job)

                def queries(it, co):
                    par = it.parity("A")
                    bank = begin(it, f"AR{co}")
                    for c in range(CC):
                        last = eng.matmul(bank[:, :], wqk[:, c, co * P:(co + 1) * P],
                                          band[:, par, c, W:W + BT], start=(c == 0), stop=(c == CC - 1))
                    end(last, f"AR{co}")

                def window(it, k):
                    par, job = it.parity("C"), f"Cwin{k}"
                    wx_ready.wait(eng, it, f"Cwx{k}")
                    if k == 0:
                        prev_ready.wait(eng, it, "Cprev")
                    bank = begin(it, job)
                    before = wprev[:, :] if k == 0 else wx[:, par, k - 1, :]
                    eng.matmul(bank[:, 0:C + 1], band_cur[:, :], wx[:, par, k, :], start=True, stop=False)
                    end(eng.matmul(bank[:, 0:C + 1], band_prev[:, :], before, start=False, stop=True), job)

                def body(it):
                    a, b, c, d = (it.runs(s) for s in "ABCD")
                    if b:
                        logits(it, 0)
                        logits(it, 1)
                    if a:
                        values(it, "AV01", (0, 1))
                    if c:
                        ln_step.wait(eng, it, "Cxn1")
                        for k0 in (0, 2):
                            transposed(it, f"Ctr{k0}{k0 + 1}", lambda k, cc: xn1[:, k, cc * P:(cc + 1) * P], k0, False)
                    if b:
                        attend(it, 0)
                        xb_ready.wait(eng, it.before().before(), "Nxb")
                        src = lambda k, cc: xb[:, it.parity("B"), cc, k * P:(k + 1) * P]
                        transposed(it, "BX01", src, 0, True)
                        weigh(it, 0)
                    if c:
                        moved(it, "Ctr01")
                        moved(it, "Ctr23")
                        bank = begin(it, "Cproj")
                        for cc in range(CC):
                            last = eng.matmul(bank[:, :], wp_s[:, cc, :], xn1T[:, cc, :], start=(cc == 0),
                                              stop=(cc == CC - 1))
                        end(last, "Cproj")
                    if b:
                        logits(it, 2)
                        attend(it, 1)
                        weigh(it, 1)
                    if c:
                        moved(it, "Cproj")
                        bank = begin(it, "Cgate")
                        for k in range(KT):
                            last = eng.matmul(bank[:, k:k + 1], pT[:, k * P:(k + 1) * P], wg_s[:, :], start=True,
                                              stop=True)
                        end(last, "Cgate")
                    if b:
                        transposed(it, "BX23", src, 2, True)
                        logits(it, 3)
                        attend(it, 2)
                        weigh(it, 2)
                    if d:
                        par = it.parity("D")
                        ln_step.wait(eng, it.before(), "Ctn")
                        for k0 in (0, 2):
                            transposed(it, f"Dtr{k0}{k0 + 1}",
                                       lambda k, cc: tn[:, par, k, cc * P:(cc + 1) * P], k0, False)
                    if a:
                        values(it, "AV23", (2, 3))
                    if b:
                        attend(it, 3)
                        weigh(it, 3)
                    if d:
                        moved(it, "Dtr01")
                        moved(it, "Dtr23")
                        bank = begin(it, "Drouter")
                        for k in range(KT):
                            for cc in range(CC):
                                last = eng.matmul(bank[:, k * E:(k + 1) * E], tnT[:, cc, k * P:(k + 1) * P],
                                                  rw_s[:, cc, :], start=(cc == 0), stop=(cc == CC - 1))
                        end(last, "Drouter")
                    if c:
                        window(it, 0)
                        window(it, 1)
                    if a:
                        values(it, "AV4", (4,))
                    if c:
                        window(it, 2)
                        window(it, 3)
                    if a:
                        queries(it, 0)
                        queries(it, 1)
                    if d:
                        route.wait(eng, it, "DM")
                        bank = begin(it, "Dpos")
                        for k in range(KT):
                            for j in range(k + 1):
                                eng.matmul(bank[:, k * E:(k + 1) * E], (earlier if j == k else onesb)[:, :],
                                           chosen[:, j, :], start=(j == 0), stop=(j == k))
                        for k in range(KT):
                            last = eng.matmul(bank[:, KT * E:KT * E + E], onesb[:, :], chosen[:, k, :],
                                              start=(k == 0), stop=(k == KT - 1))
                        end(last, "Dpos")
                iterations(eng, body)

            @block.scalar
            def _(eng):
                eng.wait_ge(prepared, 1)
                eng.wait_ge(cleared, 5)

                def take(it, job, out_, in_=None, func=ACT.Copy, **k):
                    i = bank_of[job]
                    full[i].wait(eng, it, job)
                    src = m_bank[i][:, 0:out_.free_size()] if in_ is None else in_
                    eng.activation(out_, src, func, **k).then_inc(taken[i].sem, 1)

                def expo(it, k):
                    s_taken[k % 2].wait(eng, it, f"BS{k}")
                    eng.activation(ex[:, k % 2, :], sm[:, k % 2, :], ACT.Exp,
                                   bias=shift[:, k:k + 1], scale=-1.0,
                                   accum_out=den[:, k:k + 1]).then_inc(exp_ready.sem, 1)

                def take_at(it, k):
                    at_full.wait(eng, it, f"BAT{k}")
                    eng.activation(at[:, k % 2, :, :].rearrange(flat), t_bank[:, 0:2 * P], ACT.Copy)\
                       .then_inc(at_taken.sem, 1)

                def pair_of(dst, k0):
                    return dst[:, :, k0 * P:(k0 + 2) * P]

                def bank2(job):
                    return m_bank[bank_of[job]][:, :].rearrange("p (a b) -> p a b", a=CC)

                def body(it):
                    a, b, c, d, n = (it.runs(s) for s in "ABCDN")
                    pa = it.parity("A")
                    if b:
                        expo(it, 0)
                    if a:
                        take(it, "AV01", vv[:, pa, 0:2, :].rearrange(flat))
                    if b:
                        expo(it, 1)
                    if c:
                        take(it, "Ctr01", pair_of(xn1T, 0), bank2("Ctr01"))
                        take(it, "Ctr23", pair_of(xn1T, 2), bank2("Ctr23"))
                    if b:
                        take_at(it, 0)
                        t_ready.wait(eng, it.before(), "Bt3")
                        take(it, "BX01", xt[:, 0:2, :].rearrange(flat))
                    if c:
                        take(it, "Cproj", pT[:, :], func=ACT.Tanh, bias=bp_s[:, :])
                    if b:
                        take_at(it, 1)
                        expo(it, 2)
                    if c:
                        take(it, "Cgate", eg[:, :], func=ACT.Exp, scale=-1.0)
                    if b:
                        take(it, "BX23", xt[:, 2:4, :].rearrange(flat))
                        take_at(it, 2)
                        expo(it, 3)
                    if d:
                        take(it, "Dtr01", pair_of(tnT, 0), bank2("Dtr01"))
                        take(it, "Dtr23", pair_of(tnT, 2), bank2("Dtr23"))
                    if a:
                        take(it, "AV23", vv[:, pa, 2:4, :].rearrange(flat))
                    if b:
                        take_at(it, 3)
                    if a:
                        take(it, "AV4", vv[:, pa, 4, :])
                    if d:
                        route.wait(eng, it, "Ddown")
                        eng.activation(e8[:, :, :].rearrange(flat), down[:, :, :].rearrange(flat), ACT.Exp)\
                           .then_inc(rexp.sem, 1)
                    if a:
                        for co in range(CC):
                            take(it, f"AR{co}", rT[:, pa, co, :], func=ACT.Identity, bias=r_bias[:, co, :])
                    if n:
                        pn, blk = it.parity("N"), it.block("N")
                        eng.wait_ge(x_in[pn], it.pair("N") * 48 + 48)
                        for cc in range(CC):
                            last = eng.activation(
                                band[:, pn, cc, W:W + BT], raw[:, pn, cc, W:W + BT], ACT.Identity,
                                bias=column(tab[:, 1, cc, :], blk), scale=column(tab[:, 0, cc, :], blk))
                        last.then_inc(main_ready.sem, 1)
                iterations(eng, body)

            @block.vector
            def _(eng):
                eng.wait_ge(prepared, 1)
                for i in range(2):
                    eng.tensor_copy(sm[:, i, REAL:NBR], far2[:, REAL:NBR])
                    eng.memset(wx[:, i, :, :].rearrange(flat), 0.0).then_inc(cleared, 1)
                eng.memset(xn1[:, :, C:C + 1], 1.0).then_inc(cleared, 1)
                eng.memset(besti[:, :, :].rearrange(flat), 0).then_inc(cleared, 1)
                eng.memset(wprev[:, :], 0.0).then_inc(cleared, 1)

                def done(sgn, last):
                    last.then_inc(sgn.sem, 1)

                def step(it, sgn, event, last):
                    last.then_inc(sgn.sem, 1)
                    sgn.wait(eng, it, event)

                def normal(it, n, dst, after):
                    par = it.parity("C")
                    for k in range(KT):
                        last = eng.bn_stats(bn6[:, k, :], tt[:, par, k, :])
                    last.then_inc(ln_step.sem, 1)
                    alone(eng, (ln_step.sem, ln_step.count(it, f"Cst{n}")))
                    for k in range(KT):
                        last = eng.bn_aggr(mv4[:, k, :], bn6[:, k, :])
                    step(it, ln_step, f"Cag{n}", last)
                    done(ln_step, eng.tensor_scalar(ve[:, :], mv4[:, :, 1], TOKEN_EPS, None, ALU.add))

                def scaled(it, n, dst):
                    par = it.parity("C")
                    root.wait(eng, it, f"Crs{n}")
                    for k in range(KT):
                        last = eng.tensor_scalar(dst(k), tt[:, par, k, :], mv4[:, k, 0:1], rs[:, k:k + 1],
                                                 ALU.subtract, ALU.mult)
                    done(ln_step, last)

                def mask(it, k):
                    s_full[k % 2].wait(eng, it, f"BS{k}")
                    exp_ready.wait(eng, it if k >= 2 else it.before(), f"BE{(k - 2) % KT}")
                    bank = s_bank[k % 2]
                    eng.tensor_scalar(qb[:, k:k + 1], bank[:, REAL:REAL + 1], q_const[:, :], None, ALU.add)
                    step(it, masked, f"BM{k}",
                         eng.tensor_tensor_reduce(out=sm[:, k % 2, 0:REAL], in0=bank[:, 0:REAL],
                                                  in1=far2[:, 0:REAL], scale=1.0, scalar=edge[:, :],
                                                  op0=ALU.add, op1=ALU.min, accum_out=lowest[:, k:k + 1]))
                    eng.scalar_tensor_tensor(shift[:, k:k + 1], lowest[:, k:k + 1], qb[:, k:k + 1], qb[:, k:k + 1],
                                             ALU.add, ALU.subtract).then_inc(s_taken[k % 2].sem, 1)

                def tokens(it, k):
                    par = it.parity("B")
                    exp_ready.wait(eng, it, f"BE{k}")
                    step(it, rden_ready, f"Brd{k}", eng.reciprocal(rden[:, k:k + 1], den[:, k:k + 1]))
                    if k == 0:
                        sum_ready.wait(eng, it.before(), "CR")
                    if k % 2 == 0:
                        job = "BX01" if k == 0 else "BX23"
                        taken[bank_of[job]].wait(eng, it, job)
                    o_full.wait(eng, it, f"BAV{k}")
                    eng.scalar_tensor_tensor(tt[:, par, k, :], o_bank[:, 0:C], rden[:, k:k + 1], xt[:, k, :],
                                             ALU.mult, ALU.add).then_inc(t_ready.sem, 1)

                def windowed(it, k):
                    par, i = it.parity("C"), bank_of[f"Cwin{k}"]
                    full[i].wait(eng, it, f"Cwin{k}")
                    step(it, wden_ready, f"Cwd{k}", eng.reciprocal(wden[:, k:k + 1], m_bank[i][:, C:C + 1]))
                    eng.scalar_tensor_tensor(tt[:, par, k, :], m_bank[i][:, 0:C], wden[:, k:k + 1],
                                             tt[:, par, k, :], ALU.mult, ALU.add).then_inc(taken[i].sem, 1)

                def body(it):
                    a, b, c, d, n = (it.runs(s) for s in "ABCDN")
                    pc = it.parity("C")
                    if c:
                        t_ready.wait(eng, it.before(), "Bt3")
                        normal(it, 1, None, None)
                        wx_ready.wait(eng, it.before(), "Cwx3")
                        done(prev_ready, eng.tensor_scalar(wprev[:, :], wx[:, 1 - pc, KT - 1, :],
                                                           column(keep[:, :], it.block("C")), None, ALU.mult))
                    if b:
                        mask(it, 0)
                        mask(it, 1)
                    if c:
                        scaled(it, 1, lambda k: xn1[:, k, 0:C])
                    if b:
                        tokens(it, 0)
                        mask(it, 2)
                        tokens(it, 1)
                    if c:
                        taken[bank_of["Cgate"]].wait(eng, it, "Cgate")
                        step(it, gate_step, "Cg1", eng.tensor_scalar(gg[:, :], eg[:, :], 1.0, None, ALU.add))
                        done(gate_step, eng.reciprocal(gg[:, :], gg[:, :]))
                    if b:
                        mask(it, 3)
                        tokens(it, 2)
                        tokens(it, 3)
                    if d:
                        i = bank_of["Drouter"]
                        full[i].wait(eng, it, "Drouter")
                        eng.tensor_copy(logit[:, :, :].rearrange(flat), m_bank[i][:, 0:KT * E])\
                           .then_inc(taken[i].sem, 1)
                        alone(eng, (taken[i].sem, taken[i].count(it, "Drouter")))
                        for k in range(KT):
                            last = eng.max(best[:, k, :], logit[:, k, :])
                        last.then_inc(route.sem, 1)
                        alone(eng, (route.sem, route.count(it, "Dbest")))
                        for k in range(KT):
                            last = eng.max_index(besti[:, k, :], best[:, k, :], logit[:, k, :])
                        done(route, last)
                        done(route, eng.tensor_tensor(down[:, :, :], best[:, :, :],
                                                      best[:, :, 0:1].broadcast_to([P, KT, 8]), ALU.subtract))
                    if c:
                        for k in range(KT):
                            windowed(it, k)
                        taken[bank_of["Cwin3"]].wait(eng, it, "Cwin3")
                        normal(it, 2, None, None)
                    if d:
                        rexp.wait(eng, it, "DE")
                        step(it, route, "Dz", eng.reduce_sum(zsum[:, :, 0], e8[:, :, :], AX.X))
                        step(it, route, "Dzi", eng.reciprocal(zsum[:, :, :], zsum[:, :, :]))
                        step(it, route, "Dp", eng.tensor_tensor(p12[:, :, :], e8[:, :, 0:2],
                                                                zsum[:, :, :].broadcast_to([P, KT, 2]), ALU.mult))
                        step(it, route, "Dps", eng.tensor_tensor(psum2[:, :, :], p12[:, :, 0:1], p12[:, :, 1:2],
                                                                 ALU.add))
                        step(it, route, "Dpm", eng.tensor_scalar(psum2[:, :, :], psum2[:, :, :], 1e-12, None,
                                                                 ALU.max))
                        step(it, route, "Dpi", eng.reciprocal(psum2[:, :, :], psum2[:, :, :]))
                        at_ = it.block("D") * KT
                        done(route, eng.tensor_tensor(mix[:, bass.ds(at_, KT), :], p12[:, :, :],
                                                      psum2[:, :, :].broadcast_to([P, KT, 2]), ALU.mult))
                        step(it, route, "Didf", eng.tensor_copy(idf[:, :, :], besti[:, :, 0:2]))
                        for j in range(2):
                            last = eng.tensor_tensor(hot[:, j, :, :],
                                                     expert_ids[:, :].unsqueeze(1).broadcast_to([P, KT, E]),
                                                     idf[:, :, j:j + 1].broadcast_to([P, KT, E]), ALU.is_equal)
                        step(it, route, "Dhot", last)
                        done(route, eng.tensor_tensor(chosen[:, :, :], hot[:, 0, :, :], hot[:, 1, :, :], ALU.add))
                    if c:
                        if it.base is not None or it.block("C") >= 2:
                            eng.wait_ge(scattered[pc], it.pair("C") * (32 * KT))
                        scaled(it, 2, lambda k: tn[:, pc, k, :])
                    if n:
                        pn, blk = it.parity("N"), it.block("N")
                        eng.wait_ge(x_in[pn], it.pair("N") * 48 + 48)
                        for kind, at_ in ((2, 0), (4, W + BT)):
                            for cc in range(CC):
                                last = eng.tensor_scalar(
                                    band[:, pn, cc, at_:at_ + W], raw[:, pn, cc, at_:at_ + W],
                                    column(tab[:, kind, cc, :], blk), column(tab[:, kind + 1, cc, :], blk),
                                    ALU.mult, ALU.add)
                        done(halo_ready, last)
                    if d:
                        i = bank_of["Dpos"]
                        full[i].wait(eng, it, "Dpos")
                        step(it, route, "Dwhere", eng.tensor_tensor(where[:, :, :],
                                                      m_bank[i][:, 0:KT * E].rearrange("p (a b) -> p a b", b=E),
                                                      base[:, :, :].broadcast_to([P, KT, E]), ALU.add))
                        eng.tensor_tensor(base[:, 0, :], base[:, 0, :], m_bank[i][:, KT * E:KT * E + E],
                                          ALU.add).then_inc(route.sem, 1)
                        route.wait(eng, it, "Dbase")
                        eng.sem_inc(taken[i].sem, 1)
                        for j in range(2):
                            last = eng.tensor_tensor(prod[:, j, :, :], hot[:, j, :, :], where[:, :, :], ALU.mult)
                        step(it, route, "Dprod", last)
                        step(it, route, "Dslotf", eng.reduce_sum(slotf[:, :, :], prod[:, :, :, :], AX.X))
                        if it.base is not None or it.block("D") >= 2:
                            eng.wait_ge(scattered[it.parity("D")], it.pair("D") * (32 * KT))
                        eng.tensor_copy(slots[:, bass.ds(it.block("D") * KT, KT), :],
                                        slotf[:, :, :].rearrange("p j k -> p k j"))
                        done(route, eng.tensor_copy(slot_s[:, it.parity("D"), :, :], slotf[:, :, :]))
                iterations(eng, body)

            @block.gpsimd
            def _(eng):
                eng.wait_ge(prepared, 1)
                eng.wait_ge(cleared, 5)

                def power(it, n):
                    ln_step.wait(eng, it, f"Cve{n}")
                    eng.tensor_tensor(rs[:, :], ve[:, :], halves[:, 0, 0:KT], ALU.pow).then_inc(root.sem, 1)

                def body(it):
                    if it.runs("C"):
                        par = it.parity("C")
                        power(it, 1)
                        alone(eng, (gate_step.sem, gate_step.count(it, "Cg")),
                              (ln_step.sem, ln_step.count(it, "Cxn1")))
                        for k in range(KT):
                            eng.tensor_scalar(wx[:, par, k, :], xn1[:, k, :], gg[:, k:k + 1], None, ALU.mult)\
                               .then_inc(wx_ready.sem, 1)
                        power(it, 2)
                        if it.base is not None or it.block("C") >= 2:
                            eng.wait_ge(sum_out[par], it.pair("C") * 16)
                        ln_step.wait(eng, it, "Ctn")
                        eng.tensor_tensor(rsum[:, par, :, :].rearrange(flat), tt[:, par, :, :].rearrange(flat),
                                          tn[:, par, :, :].rearrange(flat), ALU.add).then_inc(sum_ready.sem, 1)
                    if it.runs("N"):
                        par = it.parity("N")
                        waits = [(x_in[par], it.pair("N") * 48 + 48)]
                        if it.runs("B"):
                            turned = full[bank_of["BX23"]]
                            waits.append((turned.sem, turned.count(it, "BX23")))
                        alone(eng, *waits)
                        for cc in range(CC):
                            last = eng.tensor_scalar(xb[:, par, cc, :], raw[:, par, cc, W:W + BT], o_bias[:, cc, :],
                                                     None, ALU.add)
                        last.then_inc(xb_ready.sem, 1)
                    if it.runs("D"):
                        par = it.parity("D")
                        alone(eng, (route.sem, route.count(it, "Dsl")))
                        for k in range(KT):
                            for j in range(2):
                                eng.indirect_dma_start(
                                    sent, bass.IndirectOffsetOnAxis(slot_s[:, par, j, k:k + 1], 0),
                                    tn[:, par, k, :], None).then_inc(scattered[par], 16)
                iterations(eng, body)
                for i in range(2):
                    eng.wait_ge(scattered[i], 32 * KT * (NB // 2))
        loop1.close()

        loop2 = ExitStack()

        def eb(name, shape, dt=f32):
            return loop2.enter_context(nc.sbuf_tensor(name, shape, dt))

        w1h = eb("w1h", [P, E, CC, C], f32r)
        w1l = eb("w1l", [P, E, CC, C], f32r)
        w2h = eb("w2h", [P, E, CC, C], f32r)
        w2l = eb("w2l", [P, E, CC, C], f32r)
        b2_all = eb("b2_all", [P, E, C])
        b1_all = eb("b1_all", [P, E, CC])
        jvec = eb("jvec", [P, NJ])
        count = eb("count", [P, E])
        counti = eb("counti", [P, E], i32)
        tiles_of = eb("tiles_of", [P, E])
        upto = eb("upto", [P, E, E])
        ends = eb("ends", [P, E])
        past = eb("past", [P, NJ, E])
        hop = eb("hop", [P, E])
        hops = eb("hops", [P, NJ, E])
        expert_f = eb("expert_f", [P, NJ])
        row_f = eb("row_f", [P, NJ])
        expert_i = eb("expert_i", [P, NJ], i32)
        row_i = eb("row_i", [P, NJ], i32)
        tail_i = eb("tail_i", [P, E], i32)
        lower = eb("lower", [P, NB * KT * 2])
        fall = eb("fall", [P, NB * KT * 2])
        xin = eb("xin", [P, 2, KT, C])
        xh = eb("xh", [P, CC, BT], f32r)
        xl = eb("xl", [P, CC, BT], f32r)
        hid = eb("hid", [P, CC, BT])
        hh = eb("hh", [P, 2, CC, BT], f32r)
        hl = eb("hl", [P, 2, CC, BT], f32r)
        yy = eb("yy", [P, 2, KT, C])
        w1hs = eb("w1hs", [P, 2, CC, C], f32r)
        w1ls = eb("w1ls", [P, 2, CC, C], f32r)
        b1s = eb("b1s", [P, 2, CC])

        tables = sem("tables")
        tails = sem("tails")
        zeroed = sem("zeroed")
        split = sem("split")
        split_h = sem("split_h")
        w_late = sem("w_late")
        jiota = sem("jiota")

        with nc.Block() as block:
            @block.sync
            def _(eng):
                eng.dma_start(b2_all[:, :, :].rearrange("p e c -> p (e c)"),
                              b2.rearrange("e c -> (e c)").partition_broadcast(P)).then_inc(w_late, 16)
                eng.dma_start(b1_all[:, :, :], b1).then_inc(w_late, 16)
                eng.wait_ge(zeroed, 1)
                eng.wait_ge(tables, 16)
                for e in range(E + SPARE):
                    row = E * CAP + (e - E) * BT if e >= E else \
                        eng.value_load(tail_i[0:1, e:e + 1], min_val=0, max_val=E * CAP)
                    eng.dma_start(sent[bass.ds(row, BT), :].rearrange("(p k) c -> p (k c)", k=KT),
                                  yy[:, 0, :, :].rearrange(flat)).then_inc(tails, 16)
                eng.wait_ge(tails, 16 * (E + SPARE))
                eng.wait_ge(w_late, 32)

            @block.gpsimd
            def _(eng):
                eng.iota(jvec[:, :], pattern=[[1, NJ]], base=0, channel_multiplier=0,
                         allow_small_or_imprecise_dtypes=True).then_inc(jiota, 1)

            @block.scalar
            def _(eng):
                eng.wait_ge(w_experts, 16 * 2 * CC)
                for e in range(E):
                    eng.activation(w1h[:, e, :, :].rearrange(flat), w1_s[:, e, :, :].rearrange(flat), ACT.Copy)
                    eng.activation(w2h[:, e, :, :].rearrange(flat), w2_s[:, e, :, :].rearrange(flat), ACT.Copy)\
                       .then_inc(split_h, 1)

            @block.vector
            def _(eng):
                n = [0]

                def step(ins):
                    n[0] += 1
                    ins.then_inc(tables, 1)
                    eng.wait_ge(tables, n[0])

                eng.memset(yy[:, 0, :, :].rearrange(flat), 0.0).then_inc(zeroed, 1)
                step(eng.tensor_copy(tail_i[:, :], base[:, 0, :]))
                step(eng.scalar_tensor_tensor(count[:, :], base0[:, 0, :], -float(CAP), base[:, 0, :],
                                              ALU.mult, ALU.add))
                step(eng.tensor_scalar(count[:, :], count[:, :], float(BT - 1), None, ALU.add))
                step(eng.tensor_copy(counti[:, :], count[:, :]))
                step(eng.tensor_scalar(counti[:, :], counti[:, :], BT.bit_length() - 1, None,
                                       ALU.arith_shift_right))
                step(eng.tensor_copy(tiles_of[:, :], counti[:, :]))
                step(eng.tensor_tensor(upto[:, :, :], expert_ids[:, :].unsqueeze(2).broadcast_to([P, E, E]),
                                       expert_ids[:, :].unsqueeze(1).broadcast_to([P, E, E]), ALU.is_ge))
                step(eng.tensor_tensor(upto[:, :, :], upto[:, :, :],
                                       tiles_of[:, :].unsqueeze(1).broadcast_to([P, E, E]), ALU.mult))
                step(eng.reduce_sum(ends[:, :], upto[:, :, :], AX.X))
                eng.wait_ge(jiota, 1)
                step(eng.tensor_tensor(past[:, :, :], jvec[:, :].unsqueeze(2).broadcast_to([P, NJ, E]),
                                       ends[:, :].unsqueeze(1).broadcast_to([P, NJ, E]), ALU.is_ge))
                step(eng.tensor_scalar(hop[:, :], tiles_of[:, :], -float(BT), float(CAP), ALU.mult, ALU.add))
                step(eng.tensor_tensor(hops[:, :, :], past[:, :, :],
                                       hop[:, :].unsqueeze(1).broadcast_to([P, NJ, E]), ALU.mult))
                eng.reduce_sum(expert_f[:, :], past[:, :, :], AX.X)
                step(eng.reduce_sum(row_f[:, :], hops[:, :, :], AX.X))
                step(eng.scalar_tensor_tensor(row_f[:, :], jvec[:, :], float(BT), row_f[:, :], ALU.mult, ALU.add))
                eng.tensor_scalar(expert_i[:, :], expert_f[:, :], float(E - 1), None, ALU.min)
                step(eng.tensor_copy(row_i[:, :], row_f[:, :]))
                for e in range(E - 1):
                    step(eng.tensor_scalar(lower[:, :], slots[:, :, :].rearrange("p a b -> p (a b)"),
                                           float((e + 1) * CAP), hop[:, e:e + 1], ALU.is_ge, ALU.mult))
                    step(eng.tensor_tensor(fall[:, :], lower[:, :], fall[:, :], ALU.add) if e else
                         eng.tensor_copy(fall[:, :], lower[:, :]))
                step(eng.tensor_tensor(slots[:, :, :].rearrange("p a b -> p (a b)"),
                                       slots[:, :, :].rearrange("p a b -> p (a b)"), fall[:, :], ALU.subtract))
                for e in range(E):
                    eng.wait_ge(split_h, e + 1)
                    eng.tensor_tensor(w1l[:, e, :, :].rearrange(flat), w1_s[:, e, :, :].rearrange(flat),
                                      w1h[:, e, :, :].rearrange(flat).bitcast(f32), ALU.subtract)
                    eng.tensor_tensor(w2l[:, e, :, :].rearrange(flat), w2_s[:, e, :, :].rearrange(flat),
                                      w2h[:, e, :, :].rearrange(flat).bitcast(f32), ALU.subtract)\
                       .then_inc(split, 1)

        LAG.update(L=-2, X=-1, H=0, Y=1)
        xT_full = [sig(f"xT_full{i}", f"Xt{i}") for i in range(2)]
        xh_ready = [sig(f"xh_ready{i}", f"Xh{i}") for i in range(2)]
        xl_ready = [sig(f"xl_ready{i}", f"Xl{i}") for i in range(2)]
        h_full = [sig(f"h_full{i}", f"Hf{i}") for i in range(2)]
        hid_ready = [sig(f"hid_ready{i}", f"Hg{i}") for i in range(2)]
        hh_ready = [sig(f"hh_ready{i}", f"Hh{i}") for i in range(2)]
        hl_ready = [sig(f"hl_ready{i}", f"Hl{i}") for i in range(2)]
        y_full = [sig(f"y_full{i}", f"Yf{i}") for i in range(2)]
        y_taken = [sig(f"y_taken{i}", f"Yt{i}") for i in range(2)]
        w_ready = sig("w_ready", "Xw")
        rows_in = [sem(f"rows_in{i}") for i in range(2)]
        rows_out = [sem(f"rows_out{i}") for i in range(2)]
        xT_bank, h_bank, y_bank = m_bank[0:2], m_bank[2:4], s_bank

        def tiles_loop(eng, n, body):
            for off in range(-2, 2):
                body(Iteration(None, off, n))
            with eng.Fori(1, n // 2 - 1) as half:
                for off in range(2):
                    body(Iteration(half, off, n))
            for off in range(n - 2, n + 2):
                body(Iteration(None, off, n))

        def entry(eng, table, at, top):
            src = table[0:1, at:at + 1] if isinstance(at, int) else table[0:1, bass.ds(at, 1)]
            return eng.value_load(src, min_val=0, max_val=top)

        def rows_of(dram, row):
            return dram[bass.ds(row, BT), :].rearrange("(p k) c -> p (k c)", k=KT)

        with nc.Block() as block:
            @block.sync
            def _(eng):
                def body(it):
                    if it.runs("L"):
                        par = it.parity("L")
                        row = entry(eng, row_i, it.block("L"), ROOM - BT)
                        xT_full[0].wait(eng, it.before(), "Xt0")
                        xT_full[1].wait(eng, it.before(), "Xt1")
                        eng.dma_start(xin[:, par, :, :].rearrange(flat), rows_of(sent, row))\
                           .then_inc(rows_in[par], 16)
                    if it.runs("Y"):
                        par = it.parity("Y")
                        row = it.block("Y") * BT
                        for i in range(2):
                            y_taken[i].wait(eng, it, f"Yt{i}")
                        eng.dma_start(rows_of(answers, row), yy[:, par, :, :].rearrange(flat))\
                           .then_inc(rows_out[par], 16)
                tiles_loop(eng, NJ, body)
                for i in range(2):
                    eng.wait_ge(rows_out[i], 16 * (NJ // 2))

            @block.gpsimd
            def _(eng):
                eng.wait_ge(split, E)
                eng.wait_ge(w_late, 32)

                def body(it):
                    if it.runs("X"):
                        par = it.parity("X")
                        e = entry(eng, expert_i, it.block("X"), E - 1)
                        if it.before().runs("H"):
                            alone(eng, (hid_ready[1].sem, hid_ready[1].count(it.before(), "Hg1")))
                        eng.tensor_copy(w1hs[:, par, :, :].rearrange(flat),
                                        w1h[:, bass.ds(e, 1), :, :].rearrange("p e a b -> p (e a b)"))
                        eng.tensor_copy(w1ls[:, par, :, :].rearrange(flat),
                                        w1l[:, bass.ds(e, 1), :, :].rearrange("p e a b -> p (e a b)"))
                        eng.tensor_copy(b1s[:, par, :], b1_all[:, bass.ds(e, 1), :].rearrange("p e a -> p (e a)"))\
                           .then_inc(w_ready.sem, 1)
                tiles_loop(eng, NJ, body)

            @block.tensor
            def _(eng):
                eng.wait_ge(split, E)

                def turn(it):
                    par = it.parity("X")
                    eng.wait_ge(rows_in[par], it.pair("X") * 16 + 16)
                    for c in range(CC):
                        xl_ready[c].wait_before(eng, it, f"Xl{c}")
                        for k in range(KT):
                            last = eng.transpose(xT_bank[c][:, k * P:(k + 1) * P],
                                                 xin[:, par, k, c * P:(c + 1) * P], ident[:, :])
                        last.then_inc(xT_full[c].sem, 1)

                def first(it, f):
                    par = it.parity("H")
                    if f == 0:
                        w_ready.wait(eng, it.before(), "Xw")
                        for c in range(CC):
                            xl_ready[c].wait(eng, it.before(), f"Xl{c}")
                    hid_ready[f].wait_before(eng, it, f"Hg{f}")
                    fs = slice(f * P, (f + 1) * P)
                    n = 0
                    for c in range(CC):
                        for w, xx in ((w1hs, xh), (w1hs, xl), (w1ls, xh)):
                            last = eng.matmul(h_bank[f][:, :], w[:, par, c, fs], xx[:, c, :],
                                              start=(n == 0), stop=(n == 3 * CC - 1))
                            n += 1
                    last.then_inc(h_full[f].sem, 1)

                def second(it, half, e):
                    par = it.parity("Y")
                    if half == 0:
                        for f in range(CC):
                            hl_ready[f].wait(eng, it.before(), f"Hl{f}")
                    y_taken[half].wait_before(eng, it, f"Yt{half}")
                    for k in range(2):
                        ts = slice((2 * half + k) * P, (2 * half + k + 1) * P)
                        n = 0
                        for f in range(CC):
                            for hx, w in ((hh, w2h), (hh, w2l), (hl, w2h)):
                                rhs = w[:, bass.ds(e, 1), f, :].rearrange("p e c -> p (e c)")
                                last = eng.matmul(y_bank[half][:, k * C:(k + 1) * C], hx[:, par, f, ts], rhs,
                                                  start=(n == 0), stop=(n == 3 * CC - 1))
                                n += 1
                    last.then_inc(y_full[half].sem, 1)

                def body(it):
                    h, y, x_ = it.runs("H"), it.runs("Y"), it.runs("X")
                    if h:
                        first(it, 0)
                        first(it, 1)
                    if x_:
                        turn(it)
                    if y:
                        e = entry(eng, expert_i, it.block("Y"), E - 1)
                        second(it, 0, e)
                        second(it, 1, e)
                tiles_loop(eng, NJ, body)

            @block.scalar
            def _(eng):
                eng.wait_ge(w_late, 32)

                def body(it):
                    if it.runs("H"):
                        par = it.parity("H")
                        w_ready.wait(eng, it.before(), "Xw")
                        for f in range(CC):
                            h_full[f].wait(eng, it, f"Hf{f}")
                            hl_ready[f].wait(eng, it.before(), f"Hl{f}")
                            eng.activation(hid[:, f, :], h_bank[f][:, :], ACT.Gelu, bias=b1s[:, par, f:f + 1])\
                               .then_inc(hid_ready[f].sem, 1)
                    if it.runs("X"):
                        for c in range(CC):
                            xT_full[c].wait(eng, it, f"Xt{c}")
                            eng.activation(xh[:, c, :], xT_bank[c][:, :], ACT.Copy).then_inc(xh_ready[c].sem, 1)
                    if it.runs("H"):
                        for f in range(CC):
                            hid_ready[f].wait(eng, it, f"Hg{f}")
                            eng.activation(hh[:, it.parity("H"), f, :], hid[:, f, :], ACT.Copy)\
                               .then_inc(hh_ready[f].sem, 1)
                tiles_loop(eng, NJ, body)

            @block.vector
            def _(eng):
                eng.wait_ge(w_late, 32)

                def body(it):
                    if it.runs("X"):
                        for c in range(CC):
                            xh_ready[c].wait(eng, it, f"Xh{c}")
                            eng.tensor_tensor(xl[:, c, :], xT_bank[c][:, :], xh[:, c, :].bitcast(f32),
                                              ALU.subtract).then_inc(xl_ready[c].sem, 1)
                    if it.runs("H"):
                        for f in range(CC):
                            hh_ready[f].wait(eng, it, f"Hh{f}")
                            eng.tensor_tensor(hl[:, it.parity("H"), f, :], hid[:, f, :],
                                              hh[:, it.parity("H"), f, :].bitcast(f32),
                                              ALU.subtract).then_inc(hl_ready[f].sem, 1)
                    if it.runs("Y"):
                        par = it.parity("Y")
                        e = entry(eng, expert_i, it.block("Y"), E - 1)
                        if it.base is not None or it.block("Y") >= 2:
                            eng.wait_ge(rows_out[par], it.pair("Y") * 16)
                        for half in range(2):
                            y_full[half].wait(eng, it, f"Yf{half}")
                            eng.tensor_tensor(yy[:, par, 2 * half:2 * half + 2, :],
                                              y_bank[half][:, :].rearrange("p (k c) -> p k c", k=2),
                                              b2_all[:, bass.ds(e, 1), :].broadcast_to([P, 2, C]),
                                              ALU.add).then_inc(y_taken[half].sem, 1)
                tiles_loop(eng, NJ, body)
        loop2.close()

        LAG.update(G=-1, K=0)
        loop3 = ExitStack()

        def cb(name, shape, dt=f32):
            return loop3.enter_context(nc.sbuf_tensor(name, shape, dt))

        pick = cb("pick", [P, 2, 2, KT], i32)
        share = cb("share", [P, 2, KT, 2])
        got = cb("got", [P, 2, 2, KT, C])
        res = cb("res", [P, 2, KT, C])
        part = cb("part", [P, KT, C])
        tot = cb("tot", [P, 2, KT, C])
        fin = cb("fin", [P, 2, CC, BT])
        pick_ready = sig("pick_ready", "Gp")
        part_ready = sig("part_ready", "Kp")
        tot_ready = sig("tot_ready", "Kt")
        f_full = [sig(f"f_full{i}", f"Kf{i}") for i in range(2)]
        f_taken = [sig(f"f_taken{i}", f"Kk{i}") for i in range(2)]
        gathered = [sem(f"gathered{i}") for i in range(2)]
        res_in = [sem(f"res_in{i}") for i in range(2)]
        fin_out = [sem(f"fin_out{i}") for i in range(2)]

        with nc.Block() as block:
            @block.sync
            def _(eng):
                def body(it):
                    if it.runs("G"):
                        par = it.parity("G")
                        part_ready.wait(eng, it.before(), "Kp")
                        eng.dma_start(res[:, par, :, :].rearrange(flat),
                                      residual_v[bass.ds(it.block("G"), 1), :, :]).then_inc(res_in[par], 16)
                    if it.runs("K"):
                        par, blk = it.parity("K"), it.block("K")
                        for i in range(CC):
                            f_taken[i].wait(eng, it, f"Kk{i}")
                        dst = ov[:, :, bass.ds(blk // IB, 1), bass.ds(blk % IB * BT, BT)]
                        eng.dma_start(dst, fin[:, par, :, :]).then_inc(fin_out[par], 16)
                tiles_loop(eng, NB, body)
                for i in range(2):
                    eng.wait_ge(fin_out[i], 16 * (NB // 2))

            @block.gpsimd
            def _(eng):
                def body(it):
                    if it.runs("G"):
                        par = it.parity("G")
                        waits = [(pick_ready.sem, pick_ready.count(it, "Gp"))]
                        if it.before().runs("K"):
                            waits.append((tot_ready.sem, tot_ready.count(it.before(), "Kt")))
                        alone(eng, *waits)
                        for k in range(KT):
                            for j in range(2):
                                eng.indirect_dma_start(
                                    got[:, par, j, k, :], None, answers,
                                    bass.IndirectOffsetOnAxis(pick[:, par, j, k:k + 1], 0))\
                                   .then_inc(gathered[par], 16)
                tiles_loop(eng, NB, body)

            @block.vector
            def _(eng):
                def body(it):
                    if it.runs("G"):
                        par, at_ = it.parity("G"), it.block("G") * KT
                        if it.base is not None or it.block("G") >= 2:
                            eng.wait_ge(gathered[par], it.pair("G") * (32 * KT))
                        tot_ready.wait(eng, it.before(), "Kt")
                        eng.tensor_copy(share[:, par, :, :], mix[:, bass.ds(at_, KT), :])
                        eng.tensor_copy(pick[:, par, :, :].rearrange("p j k -> p k j"),
                                        slots[:, bass.ds(at_, KT), :]).then_inc(pick_ready.sem, 1)
                    if it.runs("K"):
                        par = it.parity("K")
                        pick_ready.wait(eng, it.before(), "Gp")
                        tot_ready.wait(eng, it.before(), "Kt")
                        eng.wait_ge(res_in[par], it.pair("K") * 16 + 16)
                        eng.wait_ge(gathered[par], it.pair("K") * (32 * KT) + 32 * KT)
                        for k in range(KT):
                            last = eng.scalar_tensor_tensor(part[:, k, :], got[:, par, 0, k, :],
                                                            share[:, par, k, 0:1], res[:, par, k, :],
                                                            ALU.mult, ALU.add)
                        last.then_inc(part_ready.sem, 1)
                        part_ready.wait(eng, it, "Kp")
                        for i in range(CC):
                            f_full[i].wait(eng, it.before(), f"Kf{i}")
                        for k in range(KT):
                            last = eng.scalar_tensor_tensor(tot[:, par, k, :], got[:, par, 1, k, :],
                                                            share[:, par, k, 1:2], part[:, k, :],
                                                            ALU.mult, ALU.add)
                        last.then_inc(tot_ready.sem, 1)
                tiles_loop(eng, NB, body)

            @block.tensor
            def _(eng):
                def body(it):
                    if it.runs("K"):
                        par = it.parity("K")
                        tot_ready.wait(eng, it, "Kt")
                        for c in range(CC):
                            f_taken[c].wait_before(eng, it, f"Kk{c}")
                            for k in range(KT):
                                last = eng.transpose(m_bank[c][:, k * P:(k + 1) * P],
                                                     tot[:, par, k, c * P:(c + 1) * P], ident[:, :])
                            last.then_inc(f_full[c].sem, 1)
                tiles_loop(eng, NB, body)

            @block.scalar
            def _(eng):
                def body(it):
                    if it.runs("K"):
                        par = it.parity("K")
                        if it.base is not None or it.block("K") >= 2:
                            eng.wait_ge(fin_out[par], it.pair("K") * 16)
                        for c in range(CC):
                            f_full[c].wait(eng, it, f"Kf{c}")
                            eng.activation(fin[:, par, c, :], m_bank[c][:, :], ACT.Copy).then_inc(f_taken[c].sem, 1)
                tiles_loop(eng, NB, body)
        loop3.close()


_INS = ["x", "wqT", "wkT", "wvT", "wo", "bq", "bk", "bv", "bo", "wpT", "bp", "wg", "rwT", "w1", "b1", "w2", "b2"]


def kernel(x, L0_conv_Wq, L0_conv_bq, L0_conv_Wk, L0_conv_bk, L0_conv_Wv, L0_conv_bv, L0_conv_Wo, L0_conv_bo,
           L1_attn_Wp, L1_attn_bp, L1_attn_Wg, L1_ffn_router_w, L1_ffn_w1, L1_ffn_b1, L1_ffn_w2, L1_ffn_b2):
    import numpy as np
    import concourse.bacc as bacc
    from concourse.bass_utils import run_bass_kernel_spmd

    def turned(a):
        return np.asarray(a).T

    def by_partition(a):
        a = np.asarray(a)
        a = a.reshape(a.shape[:-1] + (-1, 128))
        return np.moveaxis(a, -1, 0)

    given = dict(
        x=x, wqT=turned(L0_conv_Wq), wkT=turned(L0_conv_Wk), wvT=turned(L0_conv_Wv), wo=L0_conv_Wo,
        bq=by_partition(L0_conv_bq), bk=by_partition(L0_conv_bk), bv=by_partition(L0_conv_bv),
        bo=by_partition(L0_conv_bo), wpT=turned(L1_attn_Wp), bp=by_partition(L1_attn_bp), wg=turned(L1_attn_Wg),
        rwT=turned(L1_ffn_router_w), w1=L1_ffn_w1, b1=by_partition(L1_ffn_b1), w2=L1_ffn_w2, b2=L1_ffn_b2)
    nc = bacc.Bacc("TRN2", target_bir_lowering=False, num_devices=1)
    arrays, args = {}, {}
    for name in _INS:
        a = np.ascontiguousarray(given[name])
        arrays[f"in_{name}"] = a
        args[name] = nc.dram_tensor(f"in_{name}", a.shape, mybir.dt.from_np(a.dtype), kind="ExternalInput").ap()
    shape = arrays["in_x"].shape
    args["out"] = nc.dram_tensor("out_x", shape, mybir.dt.float32, kind="ExternalOutput").ap()
    hybrid(nc, **args)
    r = run_bass_kernel_spmd(nc, [arrays], core_ids=[0])
    return r.results[0]["out_x"]
```

```python
import concourse.bass as bass
from concourse import mybir
from contextlib import ExitStack

LAG = {"N": -2, "A": -1, "B": 0, "C": 1, "D": 2, "S": 3}


class Iteration:

    def __init__(self, base, off, blocks):
        self.base, self.off, self.blocks = base, off, blocks

    def runs(self, stage):
        if self.base is not None:
            return True
        return 0 <= self.off - LAG[stage] < self.blocks

    def block(self, stage):
        at = self.off - LAG[stage]
        return at if self.base is None else self.base * 2 + at

    def pair(self, stage, back=0):
        at = (self.off - LAG[stage] - back) // 2
        return at if self.base is None else self.base + at

    def parity(self, stage):
        return (self.off - LAG[stage]) % 2

    def before(self):
        return Iteration(self.base, self.off - 1, self.blocks)


class Signal:

    def __init__(self, sem, order):
        self.sem, self.order = sem, order.split()

    def count(self, it, event):
        n = 0
        for e in self.order:
            n += 1 if it.runs(e[0]) else 0
            if e == event:
                break
        else:
            raise KeyError(event)
        slope = 0
        for e in self.order:
            lag = LAG[e[0]]
            if it.base is None:
                n += min(max(it.off - lag, 0), it.blocks)
            else:
                n += it.off - lag
                slope += 2
        return n if it.base is None else it.base * slope + n

    def wait(self, eng, it, event):
        if it.runs(event[0]):
            eng.wait_ge(self.sem, self.count(it, event))

    def wait_before(self, eng, it, event):
        n = self.count(it, event) - 1
        if it.base is not None or n > 0:
            eng.wait_ge(self.sem, n)


def hybrid(nc, x, wqT, wkT, wvT, wo, bq, bk, bv, bo, wpT, bp, wg, rwT, w1, b1, w2, b2, out):
    f32 = mybir.dt.float32
    f32r = mybir.dt.float32r
    bf16 = mybir.dt.bfloat16
    i32 = mybir.dt.int32
    u32 = mybir.dt.uint32
    ALU = mybir.AluOpType
    ACT = mybir.ActivationFunctionType
    AX = mybir.AxisListType

    P = 128
    NI, C, H, W = x.shape
    CC = C // P
    HW = H * W
    NT = NI * HW
    ROWS = 8
    BT = ROWS * W
    KT = BT // P
    IB = H // ROWS
    NB = NI * IB
    PW = W + 2
    NBR = 4 * PW
    REAL = 4 * W
    VC = KT + 1
    A = wpT.shape[1]
    E = rwT.shape[1]
    WIN = 64
    SCALE = float(C) ** -0.5
    EPS, TOKEN_EPS = 1e-5, 1e-5
    FAR = 1e30
    CAP = NT + BT
    NJ = 2 * NT // BT + E
    NJ += NJ % 2
    SPARE = NJ - 2 * NT // BT
    ROOM = E * CAP + SPARE * BT

    xv = x.rearrange("i (c p) h w -> p c i (h w)", p=P)
    ov = out.rearrange("i (c p) h w -> p c i (h w)", p=P)

    ctx = ExitStack()
    with ctx:
        def sb(name, shape, dt=f32):
            return ctx.enter_context(nc.sbuf_tensor(name, shape, dt))

        def sem(name):
            return ctx.enter_context(nc.semaphore(name))

        def sig(name, order):
            return Signal(sem(name), order)

        residual_v = nc.dram_tensor("residual", [NB, P, KT * C], f32).ap()
        sent = nc.dram_tensor("sent", [ROOM, C], f32).ap()
        answers = nc.dram_tensor("answers", [NJ * BT, C], f32).ap()

        ident = sb("ident", [P, P])
        group = sb("group", [P, P])
        ones = sb("ones", [P, P])
        onesb = sb("onesb", [P, P], bf16)
        earlier = sb("earlier", [P, P], bf16)
        far2 = sb("far2", [P, NBR])
        edge = sb("edge", [P, 1])
        halves = sb("halves", [P, 2, 4])
        expert_ids = sb("expert_ids", [P, E])
        wqk2 = sb("wqk2", [P, 2, CC, C], f32r)
        wqb2 = sb("wqb2", [P, CC, 2], f32r)
        wvo2 = sb("wvo2", [P, 2, CC, C], f32r)
        rw2 = sb("rw2", [P, CC, 2, E], f32r)
        band_cur = sb("band_cur", [P, P], f32r)
        band_prev = sb("band_prev", [P, P], f32r)
        r_bias = sb("r_bias", [P, CC, 1])
        q_const = sb("q_const", [P, 1])
        o_bias = sb("o_bias", [P, CC, 1])
        wp_s = sb("wp_s", [P, CC, A])
        bp_s = sb("bp_s", [P, 1])
        wg_s = sb("wg_s", [P, 1])
        tab = sb("tab", [P, 6, CC, NB])
        keep = sb("keep", [P, NB])
        w1_s = sb("w1_s", [P, E, CC, C])
        w2_s = sb("w2_s", [P, E, CC, C])
        slots = sb("slots", [P, NB * KT, 2])
        mix = sb("mix", [P, NB * KT, 2])
        base = sb("base", [P, 1, E])
        base0 = sb("base0", [P, 1, E])

        m_bank = [ctx.enter_context(nc.psum_tensor(f"m_bank{i}", [P, 512], f32)) for i in range(4)]
        s_bank = [ctx.enter_context(nc.psum_tensor(f"s_bank{i}", [P, 512], f32)) for i in range(2)]
        t_bank = ctx.enter_context(nc.psum_tensor("t_bank", [P, 512], f32))
        o_bank = ctx.enter_context(nc.psum_tensor("o_bank", [P, 512], f32))

        prep = ExitStack()

        def pb(name, shape, dt=f32):
            return prep.enter_context(nc.sbuf_tensor(name, shape, dt))

        far = pb("far", [P, 4, PW])
        cur_s = pb("cur_s", [P, P])
        prev_s = pb("prev_s", [P, P])
        rw_s = pb("rw_s", [P, CC, E])
        wqk = pb("wqk", [P, CC, C])
        wqb = pb("wqb", [P, CC, 1])
        wvo = pb("wvo", [P, CC, C])
        wq_s = pb("wq_s", [P, CC, C])
        wk_s = pb("wk_s", [P, CC, C])
        wv_s = pb("wv_s", [P, CC, C])
        wo_s = pb("wo_s", [P, CC, C])
        bq_s = pb("bq_s", [P, CC, 1])
        bk_s = pb("bk_s", [P, CC, 1])
        bv_s = pb("bv_s", [P, CC, 1])
        bo_s = pb("bo_s", [P, CC, 1])
        bqb = pb("bqb", [P, CC, P])
        XR = 8
        xs = pb("xs", [P, XR, CC, BT])
        stats = pb("stats", [P, CC, NB, 6])
        mv = pb("mv", [P, CC, NI, 2])
        g1 = pb("g1", [P, CC, NI])
        g2 = pb("g2", [P, CC, NI])
        g3 = pb("g3", [P, CC, NI])
        s_all = pb("s_all", [P, CC, NI])
        b_all = pb("b_all", [P, CC, NI])

        w_in = sem("w_in")
        w_experts = sem("w_experts")
        x_seen = [sem(f"x_seen{i}") for i in range(XR)]
        x_done = [sem(f"x_done{i}") for i in range(XR)]
        pool_const = sem("pool_const")
        dve_const = sem("dve_const")
        fold = sem("fold")
        folded = sem("folded")
        d0 = sem("d0")
        g_sum = sem("g_sum")
        roots = sem("roots")
        prepared = sem("prepared")
        passed = sem("passed")

        with nc.Block() as block:
            @block.sync
            def _(eng):
                n = 0
                for dst, src in ((wq_s, wqT), (wk_s, wkT), (wv_s, wvT), (wo_s, wo), (wp_s, wpT), (rw_s, rwT)):
                    eng.dma_start(dst[:, :, :], src.rearrange("(c p) n -> p c n", p=P)).then_inc(w_in, 16)
                for dst, src in ((bq_s, bq), (bk_s, bk), (bv_s, bv), (bo_s, bo)):
                    eng.dma_start(dst[:, :, :], src.unsqueeze(2)).then_inc(w_in, 16)
                eng.dma_start(bp_s[:, :], bp).then_inc(w_in, 16)
                eng.dma_start(wg_s[:, :], wg).then_inc(w_in, 16)
                for i in range(XR):
                    eng.dma_start(xs[:, i, :, :], xv[:, :, i // IB, i % IB * BT:(i % IB + 1) * BT])\
                       .then_inc(x_seen[i], 16)
                if NI > 1:
                    with eng.Fori(1, NI) as img:
                        for i in range(XR):
                            eng.wait_ge(x_done[i], img)
                            eng.dma_start(xs[:, i, :, :],
                                          xv[:, :, bass.ds(img, 1), i * BT:(i + 1) * BT])\
                               .then_inc(x_seen[i], 16)

                for dst, src in ((w1_s, w1), (w2_s, w2)):
                    for c in range(CC):
                        eng.dma_start(dst[:, :, c, :], src[:, c * P:(c + 1) * P, :].rearrange("e p n -> p e n"))\
                           .then_inc(w_experts, 16)

            @block.gpsimd
            def _(eng):
                done = 0
                eng.memset(ident[:, :], 0.0).then_inc(pool_const, 1)
                done += 1
                eng.wait_ge(pool_const, done)
                eng.memset(group[:, :], 0.125).then_inc(pool_const, 1)
                done += 1
                eng.wait_ge(pool_const, done)
                eng.memset(halves[:, :, :], -0.5).then_inc(pool_const, 1)
                done += 1
                eng.wait_ge(pool_const, done)
                eng.memset(ones[:, :], 1.0).then_inc(pool_const, 1)
                done += 1
                eng.wait_ge(pool_const, done)
                eng.memset(onesb[:, :], 1.0).then_inc(pool_const, 1)
                done += 1
                eng.wait_ge(pool_const, done)
                eng.memset(far[:, :, :], 0.0).then_inc(pool_const, 1)
                done += 1
                eng.wait_ge(pool_const, done)
                eng.iota(expert_ids[:, :], pattern=[[1, E]], base=0, channel_multiplier=0,
                         allow_small_or_imprecise_dtypes=True).then_inc(pool_const, 1)
                done += 1
                eng.wait_ge(pool_const, done)
                eng.iota(base0[:, 0, :], pattern=[[1, E]], base=0, channel_multiplier=0,
                         allow_small_or_imprecise_dtypes=True).then_inc(pool_const, 1)
                done += 1
                eng.wait_ge(pool_const, done)
                eng.affine_select(out=ident[:, :], in_=ident[:, :], compare_op=ALU.not_equal, fill=1.0,
                                  base=0, pattern=[[-1, P]], channel_multiplier=1).then_inc(pool_const, 1)
                done += 1
                eng.wait_ge(pool_const, done)
                gv = group[:, :].rearrange("p (a b) -> p a b", b=8)
                eng.affine_select(out=gv, in_=gv, compare_op=ALU.is_ge, fill=0.0,
                                  base=0, pattern=[[-8, P // 8], [0, 8]], channel_multiplier=1).then_inc(pool_const, 1)
                done += 1
                eng.wait_ge(pool_const, done)
                eng.affine_select(out=earlier[:, :], in_=onesb[:, :], compare_op=ALU.is_gt, fill=0.0,
                                  base=0, pattern=[[1, P]], channel_multiplier=-1).then_inc(pool_const, 1)
                done += 1
                eng.wait_ge(pool_const, done)
                eng.affine_select(out=cur_s[:, :], in_=ones[:, :], compare_op=ALU.is_ge, fill=0.0,
                                  base=0, pattern=[[1, P]], channel_multiplier=-1).then_inc(pool_const, 1)
                done += 1
                eng.wait_ge(pool_const, done)
                eng.affine_select(out=prev_s[:, :], in_=ones[:, :], compare_op=ALU.is_ge, fill=0.0,
                                  base=WIN - 1 - P, pattern=[[-1, P]], channel_multiplier=1).then_inc(pool_const, 1)
                done += 1
                eng.wait_ge(pool_const, done)
                for h in range(2):
                    fv = far[W * h:W * h + W, :, :]
                    eng.affine_select(out=fv, in_=fv, compare_op=ALU.is_ge, fill=FAR, base=0,
                                      pattern=[[0, 4], [1, PW]], channel_multiplier=-1).then_inc(pool_const, 1)
                    done += 1
                    eng.wait_ge(pool_const, done)
                eng.affine_select(out=gv, in_=gv, compare_op=ALU.is_ge, fill=0.0,
                                  base=7, pattern=[[8, P // 8], [0, 8]], channel_multiplier=-1).then_inc(pool_const, 1)
                done += 1
                eng.wait_ge(pool_const, done)
                eng.affine_select(out=cur_s[:, :], in_=cur_s[:, :], compare_op=ALU.is_ge, fill=0.0,
                                  base=WIN - 1, pattern=[[-1, P]], channel_multiplier=1).then_inc(pool_const, 1)
                done += 1
                eng.wait_ge(pool_const, done)
                for h in range(2):
                    fv = far[W * h:W * h + W, :, :]
                    eng.affine_select(out=fv, in_=fv, compare_op=ALU.is_ge, fill=FAR, base=2,
                                      pattern=[[0, 4], [-1, PW]], channel_multiplier=1).then_inc(pool_const, 1)
                    done += 1
                    eng.wait_ge(pool_const, done)
                eng.memset(far[0:W, 3, :], FAR).then_inc(pool_const, 1)
                done += 1
                eng.wait_ge(pool_const, done)
                eng.memset(far[W:P, 0, :], FAR).then_inc(pool_const, 1)
                done += 1
                eng.wait_ge(pool_const, done)
                eng.wait_ge(d0, 6)
                eng.tensor_tensor(g2[:, :, :], g2[:, :, :], halves[:, :, 0:NI], ALU.pow).then_inc(roots, 1)
                eng.wait_ge(d0, 9)
                eng.tensor_tensor(g3[:, :, :], g3[:, :, :], halves[:, :, 0:NI], ALU.pow).then_inc(roots, 1)

            @block.tensor
            def _(eng):
                eng.wait_ge(w_in, 16 * 12)
                eng.wait_ge(dve_const, 1)

                def product(bank, cols, lhs, rhs):
                    for d in range(CC):
                        last = eng.matmul(bank[:, cols], lhs(d), rhs(d), start=(d == 0), stop=(d == CC - 1))
                    return last
                for c in range(CC):
                    cs = slice(c * P, c * P + P)
                    product(m_bank[c], slice(0, C), lambda d: wq_s[:, d, cs], lambda d: wk_s[:, d, :])
                    product(m_bank[c], slice(C, C + 1), lambda d: wk_s[:, d, cs], lambda d: bq_s[:, d, :])
                    product(m_bank[c], slice(C + 1, C + 2), lambda d: wq_s[:, d, cs], lambda d: bk_s[:, d, :])
                    product(m_bank[2 + c], slice(0, C), lambda d: wv_s[:, d, cs], lambda d: wo_s[:, d, :])
                    product(m_bank[2 + c], slice(C, C + 1), lambda d: wo_s[:, d, cs], lambda d: bv_s[:, d, :])
                product(s_bank[0], slice(0, 1), lambda d: bqb[:, d, :], lambda d: bk_s[:, d, :]).then_inc(fold, 1)
                eng.wait_ge(pool_const, 21)
                eng.wait_ge(d0, 2)
                eng.matmul(s_bank[1][:, 0:CC * NI], group[:, :], g1[:, :, :].rearrange("p a b -> p (a b)"),
                           start=True, stop=True).then_inc(g_sum, 1)
                eng.wait_ge(d0, 5)
                eng.matmul(s_bank[1][:, 32:32 + CC * NI], group[:, :], g3[:, :, :].rearrange("p a b -> p (a b)"),
                           start=True, stop=True).then_inc(g_sum, 1)

            @block.vector
            def _(eng):
                eng.memset(keep[:, :], 1.0).then_inc(folded, 1)
                eng.wait_ge(w_in, 16 * 12)
                eng.tensor_copy(bqb[:, :, :], bq_s[:, :, :].broadcast_to([P, CC, P])).then_inc(dve_const, 1)
                eng.wait_ge(fold, 1)
                for c in range(CC):
                    eng.tensor_scalar(wqk[:, c, :], m_bank[c][:, 0:C], -SCALE, None, ALU.mult)
                    eng.tensor_scalar(r_bias[:, c, :], m_bank[c][:, C:C + 1], -SCALE, None, ALU.mult)
                    eng.tensor_scalar(wqb[:, c, :], m_bank[c][:, C + 1:C + 2], -SCALE, None, ALU.mult)
                    eng.tensor_copy(wvo[:, c, :], m_bank[2 + c][:, 0:C])
                    eng.tensor_tensor(o_bias[:, c, :], m_bank[2 + c][:, C:C + 1], bo_s[:, c, :], ALU.add)
                eng.tensor_scalar(q_const[:, :], s_bank[0][:, 0:1], -SCALE, None, ALU.mult).then_inc(folded, 1)
                parts = ((lambda h: wqk2[:, h, :, :], wqk), (lambda h: wqb2[:, :, h:h + 1], wqb),
                         (lambda h: wvo2[:, h, :, :], wvo), (lambda h: rw2[:, :, h, :], rw_s))
                eng.wait_ge(folded, 2)
                for part, whole in parts:
                    last = eng.tensor_copy(part(0), whole[:, :, :])
                last.then_inc(folded, 1)
                eng.wait_ge(folded, 3)
                for part, whole in parts:
                    last = eng.tensor_tensor(part(1), whole[:, :, :], part(0).bitcast(f32), ALU.subtract)
                last.then_inc(folded, 1)
                for i in range(XR):
                    eng.wait_ge(x_seen[i], 16)
                    for c in range(CC):
                        last = eng.bn_stats(stats[:, c, i, :], xs[:, i, c, :])
                    last.then_inc(x_done[i], 1)
                if NI > 1:
                    with eng.Fori(1, NI) as img:
                        for i in range(XR):
                            eng.wait_ge(x_seen[i], img * 16 + 16)
                            for c in range(CC):
                                last = eng.bn_stats(stats[:, c, bass.ds(img * IB + i, 1), :], xs[:, i, c, :])
                            last.then_inc(x_done[i], 1)
                eng.wait_ge(x_done[XR - 1], NI)
                for c in range(CC):
                    for i in range(NI):
                        last = eng.bn_aggr(mv[:, c, i, :], stats[:, c, i * IB:(i + 1) * IB, :].rearrange("p a b -> p (a b)"))
                last.then_inc(d0, 1)
                eng.wait_ge(d0, 1)
                eng.tensor_copy(g1[:, :, :], mv[:, :, :, 0]).then_inc(d0, 1)
                eng.wait_ge(g_sum, 1)
                gm = s_bank[1][:, 0:CC * NI].rearrange("p (a b) -> p a b", a=CC)
                gv = s_bank[1][:, 32:32 + CC * NI].rearrange("p (a b) -> p a b", a=CC)
                eng.tensor_tensor(g2[:, :, :], g1[:, :, :], gm, ALU.subtract).then_inc(d0, 1)
                eng.wait_ge(d0, 3)
                eng.tensor_tensor(g2[:, :, :], g2[:, :, :], g2[:, :, :], ALU.mult).then_inc(d0, 1)
                eng.wait_ge(d0, 4)
                eng.tensor_tensor(g3[:, :, :], g2[:, :, :], mv[:, :, :, 1], ALU.add).then_inc(d0, 1)
                eng.wait_ge(g_sum, 2)
                eng.tensor_scalar(g2[:, :, :], gv, EPS, None, ALU.add).then_inc(d0, 1)
                eng.wait_ge(roots, 1)
                eng.tensor_tensor(g3[:, :, :], g2[:, :, :], g2[:, :, :], ALU.mult).then_inc(d0, 1)
                eng.wait_ge(d0, 7)
                eng.tensor_tensor(g3[:, :, :], g3[:, :, :], mv[:, :, :, 1], ALU.mult).then_inc(d0, 1)
                eng.wait_ge(d0, 8)
                eng.tensor_scalar(g3[:, :, :], g3[:, :, :], EPS, None, ALU.add).then_inc(d0, 1)
                eng.wait_ge(roots, 2)
                eng.tensor_tensor(s_all[:, :, :], g3[:, :, :], g2[:, :, :], ALU.mult).then_inc(d0, 1)
                eng.wait_ge(d0, 10)
                eng.scalar_tensor_tensor(b_all[:, :, :], g1[:, :, :], -1.0, s_all[:, :, :], ALU.mult, ALU.mult).then_inc(d0, 1)
                eng.wait_ge(d0, 11)
                for c in range(CC):
                    for kind in range(3):
                        for half, src in ((0, s_all), (1, b_all)):
                            last = eng.tensor_copy(
                                tab[:, 2 * kind + half, c, :].rearrange("p (i b) -> p i b", b=IB),
                                src[:, c, :].unsqueeze(2).broadcast_to([P, NI, IB]))
                last.then_inc(d0, 1)
                eng.wait_ge(d0, 12)
                tv = tab[:, :, :, :].rearrange("p k c (i b) -> p k c i b", b=IB)
                for k in range(2):
                    for c in range(CC):
                        eng.memset(tv[:, 2 + k, c, :, 0], 0.0)
                        eng.memset(tv[:, 4 + k, c, :, IB - 1], 0.0)
                eng.wait_ge(folded, 1)
                eng.memset(keep[:, :].rearrange("p (i b) -> p i b", b=IB)[:, :, 0], 0.0)
                eng.wait_ge(pool_const, 21)
                eng.tensor_copy(band_cur[:, :], cur_s[:, :])
                eng.tensor_copy(band_prev[:, :], prev_s[:, :])
                eng.tensor_copy(far2[:, 0:REAL].rearrange("p (a b) -> p a b", b=W), far[:, :, 1:W + 1])
                eng.tensor_copy(far2[:, REAL:REAL + 4], far[:, :, 0])
                eng.tensor_copy(far2[:, REAL + 4:NBR], far[:, :, PW - 1])
                eng.tensor_reduce(edge[:, :], far[:, :, 0:PW:PW - 1], AX.XY, ALU.min)
                eng.tensor_scalar(base[:, 0, :], base0[:, 0, :], float(CAP), None, ALU.mult).then_inc(prepared, 1)

        prep.close()
        loop1 = ExitStack()

        def lb(name, shape, dt=f32):
            return loop1.enter_context(nc.sbuf_tensor(name, shape, dt))

        raw = lb("raw", [P, 2, CC, BT + 2 * W])
        normed = lb("normed", [P, CC, (ROWS + 2) * W])
        band = lb("band", [P, 2, 2, CC, (ROWS + 2) * W], f32r)
        xb = lb("xb", [P, 2, CC, BT])
        rT = lb("rT", [P, 2, 2, CC, BT], f32r)
        vv = lb("vv", [P, 2, VC, C])
        sm = lb("sm", [P, 2, NBR])
        ex = lb("ex", [P, 2, NBR])
        at = lb("at", [P, 2, 2, P])
        xt = lb("xt", [P, KT, C])
        lowest = lb("lowest", [P, KT])
        qb = lb("qb", [P, KT])
        shift = lb("shift", [P, KT])
        den = lb("den", [P, KT])
        rden = lb("rden", [P, KT])
        tt = lb("tt", [P, 2, KT, C])
        bn6 = lb("bn6", [P, KT, 6])
        mv4 = lb("mv4", [P, KT, 2])
        ve = lb("ve", [P, KT])
        rs = lb("rs", [P, KT])
        xn1 = lb("xn1", [P, KT, C + 2])
        xn1T = lb("xn1T", [P, CC, BT])
        pT = lb("pT", [P, BT])
        eg = lb("eg", [P, KT])
        gg = lb("gg", [P, KT])
        wx = lb("wx", [P, KT, C + 2])
        wx2 = lb("wx2", [P, 2, 2, KT, C + 2], f32r)
        wprev = lb("wprev", [P, 2, C + 2], f32r)
        wden = lb("wden", [P, KT])
        tn = lb("tn", [P, 2, KT, C])
        tnT = lb("tnT", [P, 2, CC, BT], f32r)
        rsum = lb("rsum", [P, 2, KT, C])
        logit = lb("logit", [P, KT, E])
        best = lb("best", [P, KT, 8])
        besti = lb("besti", [P, KT, 8], u32)
        down = lb("down", [P, KT, 8])
        e8 = lb("e8", [P, KT, 8])
        zsum = lb("zsum", [P, KT, 1])
        p12 = lb("p12", [P, KT, 2])
        psum2 = lb("psum2", [P, KT, 1])
        idf = lb("idf", [P, KT, 2])
        hot = lb("hot", [P, 2, KT, E])
        chosen = lb("chosen", [P, KT, E], bf16)
        where = lb("where", [P, KT, E])
        prod = lb("prod", [P, 2, KT, E])
        slotf = lb("slotf", [P, 2, KT])
        slot_s = lb("slot_s", [P, 2, 2, KT], i32)

        JOBS = ("AV01 AV23 AR0 Dtr01 Dtr23 BX01 AR1 Ctr01 Ctr23 Drouter BX23 Cproj Cgate AV4 Dpos "
                "Cwin0 Cwin1 Cwin2 Cwin3").split()
        bank_of = {job: i % 4 for i, job in enumerate(JOBS)}
        orders = [" ".join(j for j in JOBS if bank_of[j] == i) for i in range(4)]
        full = [sig(f"full{i}", orders[i]) for i in range(4)]
        taken = [sig(f"taken{i}", orders[i]) for i in range(4)]
        s_full = [sig(f"s_full{i}", f"BS{i} BS{i + 2}") for i in range(2)]
        s_taken = [sig(f"s_taken{i}", f"BS{i} BS{i + 2}") for i in range(2)]
        tiles = lambda s: " ".join(f"{s}{k}" for k in range(KT))
        at_full = sig("at_full", tiles("BAT"))
        at_taken = sig("at_taken", tiles("BAT"))
        o_full = sig("o_full", tiles("BAV"))
        t_ready = sig("t_ready", tiles("Bt"))
        exp_ready = sig("exp_ready", tiles("BE"))
        masked = sig("masked", tiles("BM"))
        rden_ready = sig("rden_ready", tiles("Brd"))
        ln_step = sig("ln_step", "Cst1 Cag1 Cve1 Cxn1 Cst2 Cag2 Cve2 Ctn")
        root = sig("root", "Crs1 Crs2")
        prev_ready = sig("prev_ready", "Cprev")
        gate_step = sig("gate_step", "Cg1 Cg")
        wx_first = sig("wx_first", tiles("Cwf"))
        wx_high = sig("wx_high", tiles("Cwh"))
        wx_ready = sig("wx_ready", tiles("Cwx"))
        high = sig("high", "Ah0 Dh01 Dh23 Ah1")
        band_high = sig("band_high", "Nbh")
        band_ready = sig("band_ready", "Nbl")
        wden_ready = sig("wden_ready", tiles("Cwd"))
        sum_ready = sig("sum_ready", "CR")
        route = sig("route", "Dbest Dbesti Ddown Didf Dhot DM Dz Dzi Dp Dps Dpm Dpi Dmix "
                             "Dwhere Dbase Dprod Dslotf Dsl")
        rexp = sig("rexp", "DE")
        main_ready = sig("main_ready", "Nmain")
        halo_ready = sig("halo_ready", "Nhalo")
        xb_ready = sig("xb_ready", "Nxb")
        x_in = [sem(f"x_in{i}") for i in range(2)]
        sum_out = [sem(f"sum_out{i}") for i in range(2)]
        scattered = [sem(f"scattered{i}") for i in range(2)]
        cleared = sem("cleared")

        def alone(eng, *waits):
            for s, v in waits:
                eng.wait_ge(s, v)
            eng.sem_inc(passed, 1)

        def iterations(eng, body):
            for off in range(-2, 4):
                body(Iteration(None, off, NB))
            with eng.Fori(2, NB // 2 - 1) as half:
                for off in range(2):
                    body(Iteration(half, off, NB))
            for off in range(NB - 2, NB + 3):
                body(Iteration(None, off, NB))

        def column(ap, at):
            return ap[:, at:at + 1] if isinstance(at, int) else ap[:, bass.ds(at, 1)]

        flat = "p a b -> p (a b)"

        with nc.Block() as block:
            @block.sync
            def _(eng):
                eng.wait_ge(prepared, 1)

                def body(it):
                    if it.runs("N"):
                        par, blk = it.parity("N"), it.block("N")
                        two = it.before().before()
                        main_ready.wait(eng, two, "Nmain")
                        halo_ready.wait(eng, two, "Nhalo")
                        xb_ready.wait(eng, two, "Nxb")
                        img, row = blk // IB, blk % IB
                        for at, n, r in ((W, BT, row * ROWS), (0, W, (row * ROWS + H - 1) % H),
                                         (W + BT, W, (row * ROWS + ROWS) % H)):
                            src = xv[:, :, bass.ds(img, 1), bass.ds(r * W, n)]
                            eng.dma_start(raw[:, par, :, at:at + n], src).then_inc(x_in[par], 16)
                    prior = it.before()
                    if prior.runs("C"):
                        par, blk = prior.parity("C"), prior.block("C")
                        sum_ready.wait(eng, prior, "CR")
                        eng.dma_start(residual_v[bass.ds(blk, 1), :, :], rsum[:, par, :, :].rearrange(flat))\
                           .then_inc(sum_out[par], 16)
                iterations(eng, body)
                for i in range(2):
                    eng.wait_ge(sum_out[i], 16 * (NB // 2))

            @block.tensor
            def _(eng):
                eng.wait_ge(prepared, 1)
                eng.wait_ge(cleared, 5)

                def begin(it, job):
                    taken[bank_of[job]].wait_before(eng, it, job)
                    return m_bank[bank_of[job]]

                def end(last, job):
                    last.then_inc(full[bank_of[job]].sem, 1)

                def moved(it, job):
                    taken[bank_of[job]].wait(eng, it, job)

                def exact(dst, lhs, rhs):
                    passes = [(c, i, j) for c in range(CC) for i, j in ((0, 0), (0, 1), (1, 0))]
                    for n, (c, i, j) in enumerate(passes):
                        last = eng.matmul(dst, lhs(i, c), rhs(j, c), start=(n == 0), stop=(n == len(passes) - 1))
                    return last

                def logits(it, k):
                    par = it.parity("B")
                    if k == 0:
                        moved(it.before(), "AR0")
                        moved(it.before(), "AR1")
                    s_taken[k % 2].wait_before(eng, it, f"BS{k}")
                    bank = s_bank[k % 2]
                    exact(bank[:, 0:REAL], lambda h, c: rT[:, par, h, c, k * P:(k + 1) * P],
                          lambda h, c: band[:, par, h, c, k * P:k * P + REAL])
                    for n, (c, h) in enumerate((c, h) for c in range(CC) for h in range(2)):
                        last = eng.matmul(bank[:, REAL:REAL + 2], band[:, par, h, c, k * P + W:k * P + W + P],
                                          wqb2[:, c, :], start=(n == 0), stop=(n == 2 * CC - 1))
                    last.then_inc(s_full[k % 2].sem, 1)

                def attend(it, k):
                    par = it.parity("B")
                    exp_ready.wait(eng, it, f"BE{k}")
                    at_taken.wait_before(eng, it, f"BAT{k}")
                    for j in range(2):
                        last = eng.transpose(t_bank[:, j * P:(j + 1) * P], ex[:, k % 2, j * P:(j + 1) * P],
                                             ident[:, :])
                    last.then_inc(at_full.sem, 1)

                def weigh(it, k):
                    par = it.parity("B")
                    at_taken.wait(eng, it, f"BAT{k}")
                    t_ready.wait_before(eng, it, f"Bt{k}")
                    if k == 0:
                        for job in ("AV01", "AV23", "AV4"):
                            moved(it.before(), job)
                    for j in range(2):
                        last = eng.matmul(o_bank[:, 0:C], at[:, k % 2, j, :], vv[:, par, k + j, :],
                                          start=(j == 0), stop=(j == 1))
                    last.then_inc(o_full.sem, 1)

                def transposed(it, job, src, k0, per_tile):
                    bank = begin(it, job)
                    for k in (k0, k0 + 1):
                        for c in range(CC):
                            col = (k - k0) * C + c * P if per_tile else c * 2 * P + (k - k0) * P
                            last = eng.transpose(bank[:, col:col + P], src(k, c), ident[:, :])
                    end(last, job)

                def values(it, job, chunks):
                    par = it.parity("A")
                    if job == "AV01":
                        band_ready.wait(eng, it.before(), "Nbl")
                    bank = begin(it, job)
                    for j in chunks:
                        last = exact(bank[:, (j - chunks[0]) * C:(j - chunks[0] + 1) * C],
                                     lambda h, c: band[:, par, h, c, j * P:(j + 1) * P],
                                     lambda h, c: wvo2[:, h, c, :])
                    end(last, job)

                def queries(it, co):
                    par = it.parity("A")
                    bank = begin(it, f"AR{co}")
                    end(exact(bank[:, :], lambda h, c: wqk2[:, h, c, co * P:(co + 1) * P],
                              lambda h, c: band[:, par, h, c, W:W + BT]), f"AR{co}")

                def window(it, k):
                    par, job = it.parity("C"), f"Cwin{k}"
                    wx_ready.wait(eng, it, f"Cwx{k}")
                    if k == 0:
                        prev_ready.wait(eng, it, "Cprev")
                    bank = begin(it, job)
                    for h in range(2):
                        eng.matmul(bank[:, 0:C + 2], band_cur[:, :], wx2[:, par, h, k, :], start=(h == 0), stop=False)
                    for h in range(2):
                        before = wprev[:, h, :] if k == 0 else wx2[:, par, h, k - 1, :]
                        last = eng.matmul(bank[:, 0:C + 2], band_prev[:, :], before, start=False, stop=(h == 1))
                    end(last, job)

                def rows_turned(it, k0):
                    transposed(it, "BX01" if k0 == 0 else "BX23",
                               lambda k, cc: xb[:, it.parity("B"), cc, k * P:(k + 1) * P], k0, True)

                def gate_product(it):
                    moved(it, "Ctr01")
                    moved(it, "Ctr23")
                    bank = begin(it, "Cproj")
                    for cc in range(CC):
                        last = eng.matmul(bank[:, :], wp_s[:, cc, :], xn1T[:, cc, :], start=(cc == 0),
                                          stop=(cc == CC - 1))
                    end(last, "Cproj")

                def gates(it):
                    moved(it, "Cproj")
                    bank = begin(it, "Cgate")
                    for k in range(KT):
                        last = eng.matmul(bank[:, k:k + 1], pT[:, k * P:(k + 1) * P], wg_s[:, :], start=True,
                                          stop=True)
                    end(last, "Cgate")

                def router(it):
                    moved(it, "Dtr01")
                    moved(it, "Dtr23")
                    bank = begin(it, "Drouter")
                    for k in range(KT):
                        for n, (cc, h) in enumerate((cc, h) for cc in range(CC) for h in range(2)):
                            last = eng.matmul(bank[:, k * 2 * E:(k + 1) * 2 * E],
                                              tnT[:, h, cc, k * P:(k + 1) * P],
                                              rw2[:, cc, :, :].rearrange(flat),
                                              start=(n == 0), stop=(n == 2 * CC - 1))
                    end(last, "Drouter")

                def positions(it):
                    route.wait(eng, it, "DM")
                    bank = begin(it, "Dpos")
                    for k in range(KT):
                        for j in range(k + 1):
                            eng.matmul(bank[:, k * E:(k + 1) * E], (earlier if j == k else onesb)[:, :],
                                       chosen[:, j, :], start=(j == 0), stop=(j == k))
                    for k in range(KT):
                        last = eng.matmul(bank[:, KT * E:KT * E + E], onesb[:, :], chosen[:, k, :],
                                          start=(k == 0), stop=(k == KT - 1))
                    end(last, "Dpos")

                def x_turned(it, k0):
                    xb_ready.wait(eng, it.before().before(), "Nxb")
                    transposed(it, "BX01" if k0 == 0 else "BX23",
                               lambda k, cc: xb[:, it.parity("B"), cc, k * P:(k + 1) * P], k0, True)

                def gated_turned(it):
                    ln_step.wait(eng, it, "Cxn1")
                    for k0 in (0, 2):
                        transposed(it, f"Ctr{k0}{k0 + 1}", lambda k, cc: xn1[:, k, cc * P:(cc + 1) * P], k0, False)

                def tokens_turned(it):
                    ln_step.wait(eng, it.before(), "Ctn")
                    for k0 in (0, 2):
                        transposed(it, f"Dtr{k0}{k0 + 1}",
                                   lambda k, cc: tn[:, it.parity("D"), k, cc * P:(cc + 1) * P], k0, False)

                def body(it):
                    a, b, c, d = (it.runs(s) for s in "ABCD")
                    if b:
                        logits(it, 0)
                    if a:
                        values(it, "AV01", (0, 1))
                    if b:
                        logits(it, 1)
                    if a:
                        values(it, "AV23", (2, 3))
                    if b:
                        attend(it, 0)
                    if a:
                        queries(it, 0)
                    if d:
                        tokens_turned(it)
                    if b:
                        weigh(it, 0)
                        x_turned(it, 0)
                        logits(it, 2)
                        attend(it, 1)
                    if a:
                        queries(it, 1)
                    if b:
                        weigh(it, 1)
                    if c:
                        gated_turned(it)
                    if d:
                        router(it)
                    if b:
                        logits(it, 3)
                        attend(it, 2)
                        x_turned(it, 2)
                    if c:
                        gate_product(it)
                    if b:
                        weigh(it, 2)
                        attend(it, 3)
                    if c:
                        gates(it)
                    if a:
                        values(it, "AV4", (4,))
                    if d:
                        positions(it)
                    if b:
                        weigh(it, 3)
                    if c:
                        window(it, 0)
                        window(it, 1)
                        window(it, 2)
                        window(it, 3)
                iterations(eng, body)

            @block.scalar
            def _(eng):
                eng.wait_ge(prepared, 1)
                eng.wait_ge(cleared, 5)

                def take(it, job, out_, in_=None, func=ACT.Copy, **k):
                    i = bank_of[job]
                    full[i].wait(eng, it, job)
                    src = m_bank[i][:, 0:out_.free_size()] if in_ is None else in_
                    eng.activation(out_, src, func, **k).then_inc(taken[i].sem, 1)

                def upper(it, job, event, out_, in_=None, func=ACT.Copy, **k):
                    i = bank_of[job]
                    full[i].wait(eng, it, job)
                    eng.activation(out_, m_bank[i][:, :] if in_ is None else in_, func, **k).then_inc(high.sem, 1)

                def expo(it, k):
                    s_taken[k % 2].wait(eng, it, f"BS{k}")
                    eng.activation(ex[:, k % 2, :], sm[:, k % 2, :], ACT.Exp,
                                   bias=shift[:, k:k + 1], scale=-1.0,
                                   accum_out=den[:, k:k + 1]).then_inc(exp_ready.sem, 1)

                def take_at(it, k):
                    at_full.wait(eng, it, f"BAT{k}")
                    eng.activation(at[:, k % 2, :, :].rearrange(flat), t_bank[:, 0:2 * P], ACT.Copy)\
                       .then_inc(at_taken.sem, 1)

                def pair_of(dst, k0):
                    return dst[:, :, k0 * P:(k0 + 2) * P]

                def bank2(job):
                    return m_bank[bank_of[job]][:, :].rearrange("p (a b) -> p a b", a=CC)

                def body(it):
                    a, b, c, d, n = (it.runs(s) for s in "ABCDN")
                    pa, pn, par = it.parity("A"), it.parity("N"), it.parity("C")
                    if b:
                        expo(it, 0)
                    if a:
                        take(it, "AV01", vv[:, pa, 0:2, :].rearrange(flat))
                        take(it, "AV23", vv[:, pa, 2:4, :].rearrange(flat))
                    if b:
                        expo(it, 1)
                        take_at(it, 0)
                    if a:
                        upper(it, "AR0", "Ah0", rT[:, pa, 0, 0, :], func=ACT.Identity, bias=r_bias[:, 0, :])
                    if d:
                        upper(it, "Dtr01", "Dh01", pair_of(tnT[:, 0, :, :], 0), bank2("Dtr01"))
                        upper(it, "Dtr23", "Dh23", pair_of(tnT[:, 0, :, :], 2), bank2("Dtr23"))
                    if b:
                        t_ready.wait(eng, it.before(), "Bt3")
                        take(it, "BX01", xt[:, 0:2, :].rearrange(flat))
                        take_at(it, 1)
                    if n:
                        blk = it.block("N")
                        eng.wait_ge(x_in[pn], it.pair("N") * 48 + 48)
                        band_ready.wait(eng, it.before(), "Nbl")
                        for cc in range(CC):
                            last = eng.activation(
                                normed[:, cc, W:W + BT], raw[:, pn, cc, W:W + BT], ACT.Identity,
                                bias=column(tab[:, 1, cc, :], blk), scale=column(tab[:, 0, cc, :], blk))
                        last.then_inc(main_ready.sem, 1)
                    if a:
                        upper(it, "AR1", "Ah1", rT[:, pa, 0, 1, :], func=ACT.Identity, bias=r_bias[:, 1, :])
                    if b:
                        expo(it, 2)
                    if c:
                        take(it, "Ctr01", pair_of(xn1T, 0), bank2("Ctr01"))
                        take(it, "Ctr23", pair_of(xn1T, 2), bank2("Ctr23"))
                    if b:
                        take_at(it, 2)
                        expo(it, 3)
                        take(it, "BX23", xt[:, 2:4, :].rearrange(flat))
                    if n:
                        if b:
                            s_taken[1].wait(eng, it, "BS3")
                        main_ready.wait(eng, it, "Nmain")
                        halo_ready.wait(eng, it, "Nhalo")
                        eng.activation(band[:, pn, 0, :, :], normed[:, :, :], ACT.Copy).then_inc(band_high.sem, 1)
                    if c:
                        take(it, "Cproj", pT[:, :], func=ACT.Tanh, bias=bp_s[:, :])
                    if b:
                        take_at(it, 3)
                    if d:
                        route.wait(eng, it, "Ddown")
                        eng.activation(e8[:, :, :].rearrange(flat), down[:, :, :].rearrange(flat), ACT.Exp)\
                           .then_inc(rexp.sem, 1)
                    if c:
                        take(it, "Cgate", eg[:, :], func=ACT.Exp, scale=-1.0)
                    if a:
                        take(it, "AV4", vv[:, pa, 4, :])
                    if c:
                        gate_step.wait(eng, it, "Cg")
                        wx_ready.wait(eng, it.before(), "Cwx3")
                        for k in range(KT):
                            eng.activation(wx[:, k, :], xn1[:, k, :], ACT.Copy, scale=gg[:, k:k + 1])\
                               .then_inc(wx_first.sem, 1)
                            if k > 0:
                                wx_first.wait(eng, it, f"Cwf{k - 1}")
                                eng.activation(wx2[:, par, 0, k - 1, :], wx[:, k - 1, :], ACT.Copy)\
                                   .then_inc(wx_high.sem, 1)
                        wx_first.wait(eng, it, f"Cwf{KT - 1}")
                        eng.activation(wx2[:, par, 0, KT - 1, :], wx[:, KT - 1, :], ACT.Copy).then_inc(wx_high.sem, 1)
                    if n:
                        for cc in range(CC):
                            last = eng.activation(xb[:, pn, cc, :], raw[:, pn, cc, W:W + BT], ACT.Identity,
                                                  bias=o_bias[:, cc, :])
                        last.then_inc(xb_ready.sem, 1)
                iterations(eng, body)

            @block.vector
            def _(eng):
                eng.wait_ge(prepared, 1)
                eng.memset(xn1[:, :, :], 0.0).then_inc(cleared, 1)
                eng.wait_ge(cleared, 1)
                for i in range(2):
                    eng.tensor_copy(sm[:, i, REAL:NBR], far2[:, REAL:NBR])
                    eng.tensor_scalar(wx2[:, i, :, KT - 1, :], xn1[:, 0:2, :], 0.0, None, ALU.mult).then_inc(cleared, 1)
                eng.wait_ge(cleared, 3)
                eng.memset(xn1[:, :, C:C + 1], 1.0).then_inc(cleared, 1)
                eng.memset(besti[:, :, :].rearrange(flat), 0).then_inc(cleared, 1)

                def done(sgn, last):
                    last.then_inc(sgn.sem, 1)

                def step(it, sgn, event, last):
                    last.then_inc(sgn.sem, 1)
                    sgn.wait(eng, it, event)

                def normal(it, n, dst, after):
                    par = it.parity("C")
                    for k in range(KT):
                        last = eng.bn_stats(bn6[:, k, :], tt[:, par, k, :])
                    last.then_inc(ln_step.sem, 1)
                    alone(eng, (ln_step.sem, ln_step.count(it, f"Cst{n}")))
                    for k in range(KT):
                        last = eng.bn_aggr(mv4[:, k, :], bn6[:, k, :])
                    step(it, ln_step, f"Cag{n}", last)
                    done(ln_step, eng.tensor_scalar(ve[:, :], mv4[:, :, 1], TOKEN_EPS, None, ALU.add))

                def scaled(it, n, dst):
                    par = it.parity("C")
                    root.wait(eng, it, f"Crs{n}")
                    for k in range(KT):
                        last = eng.tensor_scalar(dst(k), tt[:, par, k, :], mv4[:, k, 0:1], rs[:, k:k + 1],
                                                 ALU.subtract, ALU.mult)
                    done(ln_step, last)

                def mask(it, k):
                    s_full[k % 2].wait(eng, it, f"BS{k}")
                    exp_ready.wait(eng, it if k >= 2 else it.before(), f"BE{(k - 2) % KT}")
                    bank = s_bank[k % 2]
                    eng.tensor_reduce(qb[:, k:k + 1], bank[:, REAL:REAL + 2], AX.X, ALU.add)
                    step(it, masked, f"BM{k}",
                         eng.tensor_tensor_reduce(out=sm[:, k % 2, 0:REAL], in0=bank[:, 0:REAL],
                                                  in1=far2[:, 0:REAL], scale=1.0, scalar=edge[:, :],
                                                  op0=ALU.add, op1=ALU.min, accum_out=lowest[:, k:k + 1]))
                    eng.scalar_tensor_tensor(shift[:, k:k + 1], lowest[:, k:k + 1], qb[:, k:k + 1], qb[:, k:k + 1],
                                             ALU.add, ALU.subtract).then_inc(s_taken[k % 2].sem, 1)

                def tokens(it, k):
                    par = it.parity("B")
                    exp_ready.wait(eng, it, f"BE{k}")
                    step(it, rden_ready, f"Brd{k}", eng.reciprocal(rden[:, k:k + 1], den[:, k:k + 1]))
                    if k == 0:
                        sum_ready.wait(eng, it.before(), "CR")
                    if k % 2 == 0:
                        job = "BX01" if k == 0 else "BX23"
                        taken[bank_of[job]].wait(eng, it, job)
                    o_full.wait(eng, it, f"BAV{k}")
                    eng.scalar_tensor_tensor(tt[:, par, k, :], o_bank[:, 0:C], rden[:, k:k + 1], xt[:, k, :],
                                             ALU.mult, ALU.add).then_inc(t_ready.sem, 1)

                def lower_part(it, job, event, dst, upper_, src, bias=None):
                    high.wait(eng, it, event)
                    if bias is None:
                        last = eng.tensor_tensor(dst, src, upper_.bitcast(f32), ALU.subtract)
                    else:
                        last = eng.scalar_tensor_tensor(dst, src, bias, upper_.bitcast(f32), ALU.add, ALU.subtract)
                    last.then_inc(taken[bank_of[job]].sem, 1)

                def query_part(it, co):
                    pa, job = it.parity("A"), f"AR{co}"
                    lower_part(it, job, f"Ah{co}", rT[:, pa, 1, co, :], rT[:, pa, 0, co, :],
                               m_bank[bank_of[job]][:, :], r_bias[:, co, :])

                def token_part(it, k0):
                    job = f"Dtr{k0}{k0 + 1}"
                    ts = slice(k0 * P, (k0 + 2) * P)
                    lower_part(it, job, f"Dh{k0}{k0 + 1}", tnT[:, 1, :, ts], tnT[:, 0, :, ts],
                               m_bank[bank_of[job]][:, :].rearrange("p (a b) -> p a b", a=CC))

                def windowed(it, k):
                    par, i = it.parity("C"), bank_of[f"Cwin{k}"]
                    full[i].wait(eng, it, f"Cwin{k}")
                    step(it, wden_ready, f"Cwd{k}", eng.reciprocal(wden[:, k:k + 1], m_bank[i][:, C:C + 1]))
                    eng.scalar_tensor_tensor(tt[:, par, k, :], m_bank[i][:, 0:C], wden[:, k:k + 1],
                                             tt[:, par, k, :], ALU.mult, ALU.add).then_inc(taken[i].sem, 1)

                def body(it):
                    a, b, c, d, n = (it.runs(s) for s in "ABCDN")
                    pc = it.parity("C")
                    if b:
                        mask(it, 0)
                    prior = it.before()
                    if prior.runs("C"):
                        pp = prior.parity("C")
                        if prior.base is not None or prior.block("C") >= 2:
                            eng.wait_ge(scattered[pp], prior.pair("C") * (32 * KT))
                        scaled(prior, 2, lambda k: tn[:, pp, k, :])
                    if b:
                        mask(it, 1)
                    if c:
                        t_ready.wait(eng, it.before(), "Bt3")
                        normal(it, 1, None, None)
                    if a:
                        query_part(it, 0)
                    if d:
                        token_part(it, 0)
                        token_part(it, 2)
                    if c:
                        wx_ready.wait(eng, it.before(), "Cwx3")
                        done(prev_ready, eng.tensor_scalar(wprev[:, :, :], wx2[:, 1 - pc, :, KT - 1, :].bitcast(f32),
                                                           column(keep[:, :], it.block("C")), None, ALU.mult))
                        scaled(it, 1, lambda k: xn1[:, k, 0:C])
                    if b:
                        tokens(it, 0)
                        mask(it, 2)
                    if n:
                        pn, blk = it.parity("N"), it.block("N")
                        eng.wait_ge(x_in[pn], it.pair("N") * 48 + 48)
                        band_ready.wait(eng, it.before(), "Nbl")
                        for kind, at_ in ((2, 0), (4, W + BT)):
                            for cc in range(CC):
                                last = eng.tensor_scalar(
                                    normed[:, cc, at_:at_ + W], raw[:, pn, cc, at_:at_ + W],
                                    column(tab[:, kind, cc, :], blk), column(tab[:, kind + 1, cc, :], blk),
                                    ALU.mult, ALU.add)
                        done(halo_ready, last)
                    if a:
                        query_part(it, 1)
                    if b:
                        tokens(it, 1)
                    if d:
                        i = bank_of["Drouter"]
                        full[i].wait(eng, it, "Drouter")
                        eng.reduce_sum(logit[:, :, :], m_bank[i][:, 0:KT * 2 * E].rearrange(
                            "p (k h e) -> p k e h", h=2, e=E), AX.X).then_inc(taken[i].sem, 1)
                        alone(eng, (taken[i].sem, taken[i].count(it, "Drouter")))
                        for k in range(KT):
                            last = eng.max(best[:, k, :], logit[:, k, :])
                        last.then_inc(route.sem, 1)
                        alone(eng, (route.sem, route.count(it, "Dbest")))
                        for k in range(KT):
                            last = eng.max_index(besti[:, k, :], best[:, k, :], logit[:, k, :])
                        done(route, last)
                        done(route, eng.tensor_tensor(down[:, :, :], best[:, :, :],
                                                      best[:, :, 0:1].broadcast_to([P, KT, 8]), ALU.subtract))
                    if b:
                        mask(it, 3)
                    if d:
                        route.wait(eng, it, "Dbesti")
                        step(it, route, "Didf", eng.tensor_copy(idf[:, :, :], besti[:, :, 0:2]))
                        for j in range(2):
                            last = eng.tensor_tensor(hot[:, j, :, :],
                                                     expert_ids[:, :].unsqueeze(1).broadcast_to([P, KT, E]),
                                                     idf[:, :, j:j + 1].broadcast_to([P, KT, E]), ALU.is_equal)
                        step(it, route, "Dhot", last)
                        done(route, eng.tensor_tensor(chosen[:, :, :], hot[:, 0, :, :], hot[:, 1, :, :], ALU.add))
                    if b:
                        tokens(it, 2)
                    if d:
                        rexp.wait(eng, it, "DE")
                        step(it, route, "Dz", eng.reduce_sum(zsum[:, :, 0], e8[:, :, :], AX.X))
                        step(it, route, "Dzi", eng.reciprocal(zsum[:, :, :], zsum[:, :, :]))
                        step(it, route, "Dp", eng.tensor_tensor(p12[:, :, :], e8[:, :, 0:2],
                                                                zsum[:, :, :].broadcast_to([P, KT, 2]), ALU.mult))
                        step(it, route, "Dps", eng.tensor_tensor(psum2[:, :, :], p12[:, :, 0:1], p12[:, :, 1:2],
                                                                 ALU.add))
                        step(it, route, "Dpm", eng.tensor_scalar(psum2[:, :, :], psum2[:, :, :], 1e-12, None,
                                                                 ALU.max))
                        step(it, route, "Dpi", eng.reciprocal(psum2[:, :, :], psum2[:, :, :]))
                        at_ = it.block("D") * KT
                        done(route, eng.tensor_tensor(mix[:, bass.ds(at_, KT), :], p12[:, :, :],
                                                      psum2[:, :, :].broadcast_to([P, KT, 2]), ALU.mult))
                    if c:
                        taken[bank_of["Cgate"]].wait(eng, it, "Cgate")
                        step(it, gate_step, "Cg1", eng.tensor_scalar(gg[:, :], eg[:, :], 1.0, None, ALU.add))
                        done(gate_step, eng.reciprocal(gg[:, :], gg[:, :]))
                    if d:
                        i = bank_of["Dpos"]
                        full[i].wait(eng, it, "Dpos")
                        step(it, route, "Dwhere", eng.tensor_tensor(where[:, :, :],
                                                      m_bank[i][:, 0:KT * E].rearrange("p (a b) -> p a b", b=E),
                                                      base[:, :, :].broadcast_to([P, KT, E]), ALU.add))
                        eng.tensor_tensor(base[:, 0, :], base[:, 0, :], m_bank[i][:, KT * E:KT * E + E],
                                          ALU.add).then_inc(route.sem, 1)
                        route.wait(eng, it, "Dbase")
                        eng.sem_inc(taken[i].sem, 1)
                    if b:
                        tokens(it, 3)
                    if c:
                        for k in range(KT):
                            wx_high.wait(eng, it, f"Cwh{k}")
                            eng.tensor_tensor(wx2[:, pc, 1, k, :], wx[:, k, :], wx2[:, pc, 0, k, :].bitcast(f32),
                                              ALU.subtract).then_inc(wx_ready.sem, 1)
                        for k in range(KT):
                            windowed(it, k)
                        taken[bank_of["Cwin3"]].wait(eng, it, "Cwin3")
                        normal(it, 2, None, None)
                    if d:
                        for j in range(2):
                            last = eng.tensor_tensor(prod[:, j, :, :], hot[:, j, :, :], where[:, :, :], ALU.mult)
                        step(it, route, "Dprod", last)
                        step(it, route, "Dslotf", eng.reduce_sum(slotf[:, :, :], prod[:, :, :, :], AX.X))
                        if it.base is not None or it.block("D") >= 2:
                            eng.wait_ge(scattered[it.parity("D")], it.pair("D") * (32 * KT))
                        eng.tensor_copy(slots[:, bass.ds(it.block("D") * KT, KT), :],
                                        slotf[:, :, :].rearrange("p j k -> p k j"))
                        done(route, eng.tensor_copy(slot_s[:, it.parity("D"), :, :], slotf[:, :, :]))
                iterations(eng, body)

            @block.gpsimd
            def _(eng):
                eng.wait_ge(prepared, 1)
                eng.wait_ge(cleared, 5)

                def power(it, n):
                    ln_step.wait(eng, it, f"Cve{n}")
                    eng.tensor_tensor(rs[:, :], ve[:, :], halves[:, 0, 0:KT], ALU.pow).then_inc(root.sem, 1)

                def body(it):
                    prior = it.before()
                    if prior.runs("C"):
                        par = prior.parity("C")
                        if prior.base is not None or prior.block("C") >= 2:
                            eng.wait_ge(sum_out[par], prior.pair("C") * 16)
                        ln_step.wait(eng, prior, "Ctn")
                        eng.tensor_tensor(rsum[:, par, :, :].rearrange(flat), tt[:, par, :, :].rearrange(flat),
                                          tn[:, par, :, :].rearrange(flat), ALU.add).then_inc(sum_ready.sem, 1)
                    if it.runs("C"):
                        power(it, 1)
                    if it.runs("S"):
                        par = it.parity("S")
                        alone(eng, (route.sem, route.count(it.before(), "Dsl")))
                        for k in range(KT):
                            for j in range(2):
                                eng.indirect_dma_start(
                                    sent, bass.IndirectOffsetOnAxis(slot_s[:, par, j, k:k + 1], 0),
                                    tn[:, par, k, :], None).then_inc(scattered[par], 16)
                    if it.runs("N"):
                        pn = it.parity("N")
                        band_high.wait(eng, it, "Nbh")
                        for cc in range(CC):
                            last = eng.tensor_tensor(band[:, pn, 1, cc, :], normed[:, cc, :],
                                                     band[:, pn, 0, cc, :].bitcast(f32), ALU.subtract)
                        last.then_inc(band_ready.sem, 1)
                    if it.runs("C"):
                        power(it, 2)
                iterations(eng, body)
                for i in range(2):
                    eng.wait_ge(scattered[i], 32 * KT * (NB // 2))
        loop1.close()

        loop2 = ExitStack()

        def eb(name, shape, dt=f32):
            return loop2.enter_context(nc.sbuf_tensor(name, shape, dt))

        w1h = eb("w1h", [P, E, CC, C], f32r)
        w1l = eb("w1l", [P, E, CC, C], f32r)
        w2h = eb("w2h", [P, E, CC, C], f32r)
        w2l = eb("w2l", [P, E, CC, C], f32r)
        b2_all = eb("b2_all", [P, E, C])
        b1_all = eb("b1_all", [P, E, CC])
        jvec = eb("jvec", [P, NJ])
        count = eb("count", [P, E])
        counti = eb("counti", [P, E], i32)
        tiles_of = eb("tiles_of", [P, E])
        upto = eb("upto", [P, E, E])
        ends = eb("ends", [P, E])
        past = eb("past", [P, NJ, E])
        hop = eb("hop", [P, E])
        hops = eb("hops", [P, NJ, E])
        expert_f = eb("expert_f", [P, NJ])
        row_f = eb("row_f", [P, NJ])
        expert_i = eb("expert_i", [P, NJ], i32)
        row_i = eb("row_i", [P, NJ], i32)
        tail_i = eb("tail_i", [P, E], i32)
        lower = eb("lower", [P, NB * KT * 2])
        fall = eb("fall", [P, NB * KT * 2])
        xin = eb("xin", [P, 2, KT, C])
        xh = eb("xh", [P, CC, BT], f32r)
        xl = eb("xl", [P, CC, BT], f32r)
        hid = eb("hid", [P, CC, BT])
        hh = eb("hh", [P, 2, CC, BT], f32r)
        hl = eb("hl", [P, 2, CC, BT], f32r)
        yy = eb("yy", [P, 2, KT, C])
        w1hs = eb("w1hs", [P, 2, CC, C], f32r)
        w1ls = eb("w1ls", [P, 2, CC, C], f32r)
        b1s = eb("b1s", [P, 2, CC])

        tables = sem("tables")
        tails = sem("tails")
        zeroed = sem("zeroed")
        split = sem("split")
        split_h = sem("split_h")
        w_late = sem("w_late")
        jiota = sem("jiota")

        with nc.Block() as block:
            @block.sync
            def _(eng):
                eng.dma_start(b2_all[:, :, :].rearrange("p e c -> p (e c)"),
                              b2.rearrange("e c -> (e c)").partition_broadcast(P)).then_inc(w_late, 16)
                eng.dma_start(b1_all[:, :, :], b1).then_inc(w_late, 16)
                eng.wait_ge(zeroed, 1)
                eng.wait_ge(tables, 16)
                for e in range(E + SPARE):
                    row = E * CAP + (e - E) * BT if e >= E else \
                        eng.value_load(tail_i[0:1, e:e + 1], min_val=0, max_val=E * CAP)
                    eng.dma_start(sent[bass.ds(row, BT), :].rearrange("(p k) c -> p (k c)", k=KT),
                                  yy[:, 0, :, :].rearrange(flat)).then_inc(tails, 16)
                eng.wait_ge(tails, 16 * (E + SPARE))
                eng.wait_ge(w_late, 32)

            @block.gpsimd
            def _(eng):
                eng.iota(jvec[:, :], pattern=[[1, NJ]], base=0, channel_multiplier=0,
                         allow_small_or_imprecise_dtypes=True).then_inc(jiota, 1)

            @block.scalar
            def _(eng):
                eng.wait_ge(w_experts, 16 * 2 * CC)
                for e in range(E):
                    eng.activation(w1h[:, e, :, :].rearrange(flat), w1_s[:, e, :, :].rearrange(flat), ACT.Copy)
                    eng.activation(w2h[:, e, :, :].rearrange(flat), w2_s[:, e, :, :].rearrange(flat), ACT.Copy)\
                       .then_inc(split_h, 1)

            @block.vector
            def _(eng):
                n = [0]

                def step(ins):
                    n[0] += 1
                    ins.then_inc(tables, 1)
                    eng.wait_ge(tables, n[0])

                eng.memset(yy[:, 0, :, :].rearrange(flat), 0.0).then_inc(zeroed, 1)
                step(eng.tensor_copy(tail_i[:, :], base[:, 0, :]))
                step(eng.scalar_tensor_tensor(count[:, :], base0[:, 0, :], -float(CAP), base[:, 0, :],
                                              ALU.mult, ALU.add))
                step(eng.tensor_scalar(count[:, :], count[:, :], float(BT - 1), None, ALU.add))
                step(eng.tensor_copy(counti[:, :], count[:, :]))
                step(eng.tensor_scalar(counti[:, :], counti[:, :], BT.bit_length() - 1, None,
                                       ALU.arith_shift_right))
                step(eng.tensor_copy(tiles_of[:, :], counti[:, :]))
                step(eng.tensor_tensor(upto[:, :, :], expert_ids[:, :].unsqueeze(2).broadcast_to([P, E, E]),
                                       expert_ids[:, :].unsqueeze(1).broadcast_to([P, E, E]), ALU.is_ge))
                step(eng.tensor_tensor(upto[:, :, :], upto[:, :, :],
                                       tiles_of[:, :].unsqueeze(1).broadcast_to([P, E, E]), ALU.mult))
                step(eng.reduce_sum(ends[:, :], upto[:, :, :], AX.X))
                eng.wait_ge(jiota, 1)
                step(eng.tensor_tensor(past[:, :, :], jvec[:, :].unsqueeze(2).broadcast_to([P, NJ, E]),
                                       ends[:, :].unsqueeze(1).broadcast_to([P, NJ, E]), ALU.is_ge))
                step(eng.tensor_scalar(hop[:, :], tiles_of[:, :], -float(BT), float(CAP), ALU.mult, ALU.add))
                step(eng.tensor_tensor(hops[:, :, :], past[:, :, :],
                                       hop[:, :].unsqueeze(1).broadcast_to([P, NJ, E]), ALU.mult))
                eng.reduce_sum(expert_f[:, :], past[:, :, :], AX.X)
                step(eng.reduce_sum(row_f[:, :], hops[:, :, :], AX.X))
                step(eng.scalar_tensor_tensor(row_f[:, :], jvec[:, :], float(BT), row_f[:, :], ALU.mult, ALU.add))
                eng.tensor_scalar(expert_i[:, :], expert_f[:, :], float(E - 1), None, ALU.min)
                step(eng.tensor_copy(row_i[:, :], row_f[:, :]))
                for e in range(E - 1):
                    step(eng.tensor_scalar(lower[:, :], slots[:, :, :].rearrange("p a b -> p (a b)"),
                                           float((e + 1) * CAP), hop[:, e:e + 1], ALU.is_ge, ALU.mult))
                    step(eng.tensor_tensor(fall[:, :], lower[:, :], fall[:, :], ALU.add) if e else
                         eng.tensor_copy(fall[:, :], lower[:, :]))
                step(eng.tensor_tensor(slots[:, :, :].rearrange("p a b -> p (a b)"),
                                       slots[:, :, :].rearrange("p a b -> p (a b)"), fall[:, :], ALU.subtract))
                for e in range(E):
                    eng.wait_ge(split_h, e + 1)
                    eng.tensor_tensor(w1l[:, e, :, :].rearrange(flat), w1_s[:, e, :, :].rearrange(flat),
                                      w1h[:, e, :, :].rearrange(flat).bitcast(f32), ALU.subtract)
                    eng.tensor_tensor(w2l[:, e, :, :].rearrange(flat), w2_s[:, e, :, :].rearrange(flat),
                                      w2h[:, e, :, :].rearrange(flat).bitcast(f32), ALU.subtract)\
                       .then_inc(split, 1)

        LAG.update(L=-2, X=-1, H=0, Y=1)
        xT_full = [sig(f"xT_full{i}", f"Xt{i}") for i in range(2)]
        xh_ready = [sig(f"xh_ready{i}", f"Xh{i}") for i in range(2)]
        xl_ready = [sig(f"xl_ready{i}", f"Xl{i}") for i in range(2)]
        h_full = [sig(f"h_full{i}", f"Hf{i}") for i in range(2)]
        hid_ready = [sig(f"hid_ready{i}", f"Hg{i}") for i in range(2)]
        hh_ready = [sig(f"hh_ready{i}", f"Hh{i}") for i in range(2)]
        hl_ready = [sig(f"hl_ready{i}", f"Hl{i}") for i in range(2)]
        y_full = [sig(f"y_full{i}", f"Yf{i}") for i in range(2)]
        y_taken = [sig(f"y_taken{i}", f"Yt{i}") for i in range(2)]
        w_ready = sig("w_ready", "Xw")
        rows_in = [sem(f"rows_in{i}") for i in range(2)]
        rows_out = [sem(f"rows_out{i}") for i in range(2)]
        xT_bank, h_bank, y_bank = m_bank[0:2], m_bank[2:4], s_bank

        def tiles_loop(eng, n, body):
            for off in range(-2, 4):
                body(Iteration(None, off, n))
            with eng.Fori(2, n // 2 - 1) as half:
                for off in range(2):
                    body(Iteration(half, off, n))
            for off in range(n - 2, n + 2):
                body(Iteration(None, off, n))

        def entry(eng, table, at, top):
            src = table[0:1, at:at + 1] if isinstance(at, int) else table[0:1, bass.ds(at, 1)]
            return eng.value_load(src, min_val=0, max_val=top)

        def rows_of(dram, row):
            return dram[bass.ds(row, BT), :].rearrange("(p k) c -> p (k c)", k=KT)

        with nc.Block() as block:
            @block.sync
            def _(eng):
                def body(it):
                    if it.runs("L"):
                        par = it.parity("L")
                        row = entry(eng, row_i, it.block("L"), ROOM - BT)
                        xT_full[0].wait(eng, it.before(), "Xt0")
                        xT_full[1].wait(eng, it.before(), "Xt1")
                        eng.dma_start(xin[:, par, :, :].rearrange(flat), rows_of(sent, row))\
                           .then_inc(rows_in[par], 16)
                    if it.runs("Y"):
                        par = it.parity("Y")
                        row = it.block("Y") * BT
                        for i in range(2):
                            y_taken[i].wait(eng, it, f"Yt{i}")
                        eng.dma_start(rows_of(answers, row), yy[:, par, :, :].rearrange(flat))\
                           .then_inc(rows_out[par], 16)
                tiles_loop(eng, NJ, body)
                for i in range(2):
                    eng.wait_ge(rows_out[i], 16 * (NJ // 2))

            @block.gpsimd
            def _(eng):
                eng.wait_ge(split, E)
                eng.wait_ge(w_late, 32)

                def body(it):
                    if it.runs("X"):
                        par = it.parity("X")
                        e = entry(eng, expert_i, it.block("X"), E - 1)
                        if it.before().runs("H"):
                            alone(eng, (hid_ready[1].sem, hid_ready[1].count(it.before(), "Hg1")))
                        eng.tensor_copy(w1hs[:, par, :, :].rearrange(flat),
                                        w1h[:, bass.ds(e, 1), :, :].rearrange("p e a b -> p (e a b)"))
                        eng.tensor_copy(w1ls[:, par, :, :].rearrange(flat),
                                        w1l[:, bass.ds(e, 1), :, :].rearrange("p e a b -> p (e a b)"))
                        eng.tensor_copy(b1s[:, par, :], b1_all[:, bass.ds(e, 1), :].rearrange("p e a -> p (e a)"))\
                           .then_inc(w_ready.sem, 1)
                tiles_loop(eng, NJ, body)

            @block.tensor
            def _(eng):
                eng.wait_ge(split, E)

                def turn(it):
                    par = it.parity("X")
                    eng.wait_ge(rows_in[par], it.pair("X") * 16 + 16)
                    for c in range(CC):
                        xl_ready[c].wait_before(eng, it, f"Xl{c}")
                        for k in range(KT):
                            last = eng.transpose(xT_bank[c][:, k * P:(k + 1) * P],
                                                 xin[:, par, k, c * P:(c + 1) * P], ident[:, :])
                        last.then_inc(xT_full[c].sem, 1)

                def first(it, f):
                    par = it.parity("H")
                    if f == 0:
                        w_ready.wait(eng, it.before(), "Xw")
                        for c in range(CC):
                            xl_ready[c].wait(eng, it.before(), f"Xl{c}")
                    hid_ready[f].wait_before(eng, it, f"Hg{f}")
                    fs = slice(f * P, (f + 1) * P)
                    n = 0
                    for c in range(CC):
                        for w, xx in ((w1hs, xh), (w1hs, xl), (w1ls, xh)):
                            last = eng.matmul(h_bank[f][:, :], w[:, par, c, fs], xx[:, c, :],
                                              start=(n == 0), stop=(n == 3 * CC - 1))
                            n += 1
                    last.then_inc(h_full[f].sem, 1)

                def second(it, half, e):
                    par = it.parity("Y")
                    if half == 0:
                        for f in range(CC):
                            hl_ready[f].wait(eng, it.before(), f"Hl{f}")
                    y_taken[half].wait_before(eng, it, f"Yt{half}")
                    for k in range(2):
                        ts = slice((2 * half + k) * P, (2 * half + k + 1) * P)
                        n = 0
                        for f in range(CC):
                            for hx, w in ((hh, w2h), (hh, w2l), (hl, w2h)):
                                rhs = w[:, bass.ds(e, 1), f, :].rearrange("p e c -> p (e c)")
                                last = eng.matmul(y_bank[half][:, k * C:(k + 1) * C], hx[:, par, f, ts], rhs,
                                                  start=(n == 0), stop=(n == 3 * CC - 1))
                                n += 1
                    last.then_inc(y_full[half].sem, 1)

                def body(it):
                    h, y, x_ = it.runs("H"), it.runs("Y"), it.runs("X")
                    if h:
                        first(it, 0)
                        first(it, 1)
                    if x_:
                        turn(it)
                    if y:
                        e = entry(eng, expert_i, it.block("Y"), E - 1)
                        second(it, 0, e)
                        second(it, 1, e)
                tiles_loop(eng, NJ, body)

            @block.scalar
            def _(eng):
                eng.wait_ge(w_late, 32)

                def body(it):
                    if it.runs("H"):
                        par = it.parity("H")
                        w_ready.wait(eng, it.before(), "Xw")
                        for f in range(CC):
                            h_full[f].wait(eng, it, f"Hf{f}")
                            hl_ready[f].wait(eng, it.before(), f"Hl{f}")
                            eng.activation(hid[:, f, :], h_bank[f][:, :], ACT.Gelu, bias=b1s[:, par, f:f + 1])\
                               .then_inc(hid_ready[f].sem, 1)
                    if it.runs("X"):
                        for c in range(CC):
                            xT_full[c].wait(eng, it, f"Xt{c}")
                            eng.activation(xh[:, c, :], xT_bank[c][:, :], ACT.Copy).then_inc(xh_ready[c].sem, 1)
                    if it.runs("H"):
                        for f in range(CC):
                            hid_ready[f].wait(eng, it, f"Hg{f}")
                            eng.activation(hh[:, it.parity("H"), f, :], hid[:, f, :], ACT.Copy)\
                               .then_inc(hh_ready[f].sem, 1)
                tiles_loop(eng, NJ, body)

            @block.vector
            def _(eng):
                eng.wait_ge(w_late, 32)

                def body(it):
                    if it.runs("X"):
                        for c in range(CC):
                            xh_ready[c].wait(eng, it, f"Xh{c}")
                            eng.tensor_tensor(xl[:, c, :], xT_bank[c][:, :], xh[:, c, :].bitcast(f32),
                                              ALU.subtract).then_inc(xl_ready[c].sem, 1)
                    if it.runs("H"):
                        for f in range(CC):
                            hh_ready[f].wait(eng, it, f"Hh{f}")
                            eng.tensor_tensor(hl[:, it.parity("H"), f, :], hid[:, f, :],
                                              hh[:, it.parity("H"), f, :].bitcast(f32),
                                              ALU.subtract).then_inc(hl_ready[f].sem, 1)
                    if it.runs("Y"):
                        par = it.parity("Y")
                        e = entry(eng, expert_i, it.block("Y"), E - 1)
                        if it.base is not None or it.block("Y") >= 2:
                            eng.wait_ge(rows_out[par], it.pair("Y") * 16)
                        for half in range(2):
                            y_full[half].wait(eng, it, f"Yf{half}")
                            eng.tensor_tensor(yy[:, par, 2 * half:2 * half + 2, :],
                                              y_bank[half][:, :].rearrange("p (k c) -> p k c", k=2),
                                              b2_all[:, bass.ds(e, 1), :].broadcast_to([P, 2, C]),
                                              ALU.add).then_inc(y_taken[half].sem, 1)
                tiles_loop(eng, NJ, body)
        loop2.close()

        LAG.update(G=-1, K=0)
        loop3 = ExitStack()

        def cb(name, shape, dt=f32):
            return loop3.enter_context(nc.sbuf_tensor(name, shape, dt))

        pick = cb("pick", [P, 2, 2, KT], i32)
        share = cb("share", [P, 2, KT, 2])
        got = cb("got", [P, 2, 2, KT, C])
        res = cb("res", [P, 2, KT, C])
        part = cb("part", [P, KT, C])
        tot = cb("tot", [P, 2, KT, C])
        fin = cb("fin", [P, 2, CC, BT])
        pick_ready = sig("pick_ready", "Gp")
        part_ready = sig("part_ready", "Kp")
        tot_ready = sig("tot_ready", "Kt")
        f_full = [sig(f"f_full{i}", f"Kf{i}") for i in range(2)]
        f_taken = [sig(f"f_taken{i}", f"Kk{i}") for i in range(2)]
        gathered = [sem(f"gathered{i}") for i in range(2)]
        res_in = [sem(f"res_in{i}") for i in range(2)]
        fin_out = [sem(f"fin_out{i}") for i in range(2)]

        with nc.Block() as block:
            @block.sync
            def _(eng):
                def body(it):
                    if it.runs("G"):
                        par = it.parity("G")
                        part_ready.wait(eng, it.before(), "Kp")
                        eng.dma_start(res[:, par, :, :].rearrange(flat),
                                      residual_v[bass.ds(it.block("G"), 1), :, :]).then_inc(res_in[par], 16)
                    if it.runs("K"):
                        par, blk = it.parity("K"), it.block("K")
                        for i in range(CC):
                            f_taken[i].wait(eng, it, f"Kk{i}")
                        dst = ov[:, :, bass.ds(blk // IB, 1), bass.ds(blk % IB * BT, BT)]
                        eng.dma_start(dst, fin[:, par, :, :]).then_inc(fin_out[par], 16)
                tiles_loop(eng, NB, body)
                for i in range(2):
                    eng.wait_ge(fin_out[i], 16 * (NB // 2))

            @block.gpsimd
            def _(eng):
                def body(it):
                    if it.runs("G"):
                        par = it.parity("G")
                        waits = [(pick_ready.sem, pick_ready.count(it, "Gp"))]
                        if it.before().runs("K"):
                            waits.append((tot_ready.sem, tot_ready.count(it.before(), "Kt")))
                        alone(eng, *waits)
                        for k in range(KT):
                            for j in range(2):
                                eng.indirect_dma_start(
                                    got[:, par, j, k, :], None, answers,
                                    bass.IndirectOffsetOnAxis(pick[:, par, j, k:k + 1], 0))\
                                   .then_inc(gathered[par], 16)
                tiles_loop(eng, NB, body)

            @block.vector
            def _(eng):
                def body(it):
                    if it.runs("G"):
                        par, at_ = it.parity("G"), it.block("G") * KT
                        if it.base is not None or it.block("G") >= 2:
                            eng.wait_ge(gathered[par], it.pair("G") * (32 * KT))
                        tot_ready.wait(eng, it.before(), "Kt")
                        eng.tensor_copy(share[:, par, :, :], mix[:, bass.ds(at_, KT), :])
                        eng.tensor_copy(pick[:, par, :, :].rearrange("p j k -> p k j"),
                                        slots[:, bass.ds(at_, KT), :]).then_inc(pick_ready.sem, 1)
                    if it.runs("K"):
                        par = it.parity("K")
                        pick_ready.wait(eng, it.before(), "Gp")
                        tot_ready.wait(eng, it.before(), "Kt")
                        eng.wait_ge(res_in[par], it.pair("K") * 16 + 16)
                        eng.wait_ge(gathered[par], it.pair("K") * (32 * KT) + 32 * KT)
                        for k in range(KT):
                            last = eng.scalar_tensor_tensor(part[:, k, :], got[:, par, 0, k, :],
                                                            share[:, par, k, 0:1], res[:, par, k, :],
                                                            ALU.mult, ALU.add)
                        last.then_inc(part_ready.sem, 1)
                        part_ready.wait(eng, it, "Kp")
                        for i in range(CC):
                            f_full[i].wait(eng, it.before(), f"Kf{i}")
                        for k in range(KT):
                            last = eng.scalar_tensor_tensor(tot[:, par, k, :], got[:, par, 1, k, :],
                                                            share[:, par, k, 1:2], part[:, k, :],
                                                            ALU.mult, ALU.add)
                        last.then_inc(tot_ready.sem, 1)
                tiles_loop(eng, NB, body)

            @block.tensor
            def _(eng):
                def body(it):
                    if it.runs("K"):
                        par = it.parity("K")
                        tot_ready.wait(eng, it, "Kt")
                        for c in range(CC):
                            f_taken[c].wait_before(eng, it, f"Kk{c}")
                            for k in range(KT):
                                last = eng.transpose(m_bank[c][:, k * P:(k + 1) * P],
                                                     tot[:, par, k, c * P:(c + 1) * P], ident[:, :])
                            last.then_inc(f_full[c].sem, 1)
                tiles_loop(eng, NB, body)

            @block.scalar
            def _(eng):
                def body(it):
                    if it.runs("K"):
                        par = it.parity("K")
                        if it.base is not None or it.block("K") >= 2:
                            eng.wait_ge(fin_out[par], it.pair("K") * 16)
                        for c in range(CC):
                            f_full[c].wait(eng, it, f"Kf{c}")
                            eng.activation(fin[:, par, c, :], m_bank[c][:, :], ACT.Copy).then_inc(f_taken[c].sem, 1)
                tiles_loop(eng, NB, body)
        loop3.close()


_INS = ["x", "wqT", "wkT", "wvT", "wo", "bq", "bk", "bv", "bo", "wpT", "bp", "wg", "rwT", "w1", "b1", "w2", "b2"]


def kernel(x, L0_conv_Wq, L0_conv_bq, L0_conv_Wk, L0_conv_bk, L0_conv_Wv, L0_conv_bv, L0_conv_Wo, L0_conv_bo,
           L1_attn_Wp, L1_attn_bp, L1_attn_Wg, L1_ffn_router_w, L1_ffn_w1, L1_ffn_b1, L1_ffn_w2, L1_ffn_b2):
    import numpy as np
    import concourse.bacc as bacc
    from concourse.bass_utils import run_bass_kernel_spmd

    def turned(a):
        return np.asarray(a).T

    def by_partition(a):
        a = np.asarray(a)
        a = a.reshape(a.shape[:-1] + (-1, 128))
        return np.moveaxis(a, -1, 0)

    given = dict(
        x=x, wqT=turned(L0_conv_Wq), wkT=turned(L0_conv_Wk), wvT=turned(L0_conv_Wv), wo=L0_conv_Wo,
        bq=by_partition(L0_conv_bq), bk=by_partition(L0_conv_bk), bv=by_partition(L0_conv_bv),
        bo=by_partition(L0_conv_bo), wpT=turned(L1_attn_Wp), bp=by_partition(L1_attn_bp), wg=turned(L1_attn_Wg),
        rwT=turned(L1_ffn_router_w), w1=L1_ffn_w1, b1=by_partition(L1_ffn_b1), w2=L1_ffn_w2, b2=L1_ffn_b2)
    nc = bacc.Bacc("TRN2", target_bir_lowering=False, num_devices=1)
    arrays, args = {}, {}
    for name in _INS:
        a = np.ascontiguousarray(given[name])
        arrays[f"in_{name}"] = a
        args[name] = nc.dram_tensor(f"in_{name}", a.shape, mybir.dt.from_np(a.dtype), kind="ExternalInput").ap()
    shape = arrays["in_x"].shape
    args["out"] = nc.dram_tensor("out_x", shape, mybir.dt.float32, kind="ExternalOutput").ap()
    hybrid(nc, **args)
    r = run_bass_kernel_spmd(nc, [arrays], core_ids=[0])
    return r.results[0]["out_x"]
```

```python
import concourse.bass as bass
from concourse import mybir
from contextlib import ExitStack

LAG = {"N": -2, "A": -1, "B": 0, "C": 1, "D": 2, "S": 3}


class Iteration:

    def __init__(self, base, off, blocks):
        self.base, self.off, self.blocks = base, off, blocks

    def runs(self, stage):
        if self.base is not None:
            return True
        return 0 <= self.off - LAG[stage] < self.blocks

    def block(self, stage):
        at = self.off - LAG[stage]
        return at if self.base is None else self.base * 2 + at

    def pair(self, stage, back=0):
        at = (self.off - LAG[stage] - back) // 2
        return at if self.base is None else self.base + at

    def parity(self, stage):
        return (self.off - LAG[stage]) % 2

    def before(self):
        return Iteration(self.base, self.off - 1, self.blocks)


class Signal:

    def __init__(self, sem, order):
        self.sem, self.order = sem, order.split()

    def count(self, it, event):
        n = 0
        for e in self.order:
            n += 1 if it.runs(e[0]) else 0
            if e == event:
                break
        else:
            raise KeyError(event)
        slope = 0
        for e in self.order:
            lag = LAG[e[0]]
            if it.base is None:
                n += min(max(it.off - lag, 0), it.blocks)
            else:
                n += it.off - lag
                slope += 2
        return n if it.base is None else it.base * slope + n

    def wait(self, eng, it, event):
        if it.runs(event[0]):
            eng.wait_ge(self.sem, self.count(it, event))

    def wait_before(self, eng, it, event):
        n = self.count(it, event) - 1
        if it.base is not None or n > 0:
            eng.wait_ge(self.sem, n)


def hybrid(nc, x, wqT, wkT, wvT, wo, bq, bk, bv, bo, wpT, bp, wg, rwT, w1, b1, w2, b2, out):
    f32 = mybir.dt.float32
    f32r = mybir.dt.float32r
    bf16 = mybir.dt.bfloat16
    i32 = mybir.dt.int32
    u32 = mybir.dt.uint32
    ALU = mybir.AluOpType
    ACT = mybir.ActivationFunctionType
    AX = mybir.AxisListType

    P = 128
    NI, C, H, W = x.shape
    CC = C // P
    HW = H * W
    NT = NI * HW
    ROWS = 8
    BT = ROWS * W
    KT = BT // P
    IB = H // ROWS
    NB = NI * IB
    PW = W + 2
    NBR = 4 * PW
    REAL = 4 * W
    VC = KT + 1
    A = wpT.shape[1]
    E = rwT.shape[1]
    WIN = 64
    SCALE = float(C) ** -0.5
    EPS, TOKEN_EPS = 1e-5, 1e-5
    FAR = 1e30
    CAP = NT + BT
    NJ = 2 * NT // BT + E
    NJ += NJ % 2
    SPARE = NJ - 2 * NT // BT
    ROOM = E * CAP + SPARE * BT

    xv = x.rearrange("i (c p) h w -> p c i (h w)", p=P)
    ov = out.rearrange("i (c p) h w -> p c i (h w)", p=P)

    ctx = ExitStack()
    with ctx:
        def sb(name, shape, dt=f32):
            return ctx.enter_context(nc.sbuf_tensor(name, shape, dt))

        def sem(name):
            return ctx.enter_context(nc.semaphore(name))

        def sig(name, order):
            return Signal(sem(name), order)

        residual_v = nc.dram_tensor("residual", [NB, P, KT * C], f32).ap()
        sent = nc.dram_tensor("sent", [ROOM, C + 2], f32).ap()
        answers = nc.dram_tensor("answers", [2 * NT + 2 * (E + SPARE) * BT, C], f32).ap()

        ident = sb("ident", [P, P])
        group = sb("group", [P, P])
        ones = sb("ones", [P, P])
        onesb = sb("onesb", [P, P], bf16)
        earlier = sb("earlier", [P, P], bf16)
        far2 = sb("far2", [P, NBR])
        edge = sb("edge", [P, 1])
        halves = sb("halves", [P, 2, 4])
        expert_ids = sb("expert_ids", [P, E])
        wqk2 = sb("wqk2", [P, 2, CC, C], f32r)
        wvo2 = sb("wvo2", [P, 2, CC, C + 2], f32r)
        rw_s = sb("rw_s", [P, CC, E])
        band_cur = sb("band_cur", [P, P], f32r)
        band_prev = sb("band_prev", [P, P], f32r)
        r_bias = sb("r_bias", [P, CC, 1])
        q_const = sb("q_const", [P, 1])
        o_bias = sb("o_bias", [P, CC, 1])
        wp_s = sb("wp_s", [P, CC, A])
        bp_s = sb("bp_s", [P, 1])
        wg_s = sb("wg_s", [P, 1])
        tab = sb("tab", [P, 6, CC, NB])
        keep = sb("keep", [P, NB])
        w1_s = sb("w1_s", [P, E, CC, C])
        w2_s = sb("w2_s", [P, E, CC, C])
        places = sb("places", [P, NB * KT])
        raw = sb("raw", [P, 2, CC, BT + 2 * W])
        expert_f = sb("expert_f", [P, NJ])
        expert_i = sb("expert_i", [P, NJ], i32)
        row_i = sb("row_i", [P, NJ], i32)
        tail_i = sb("tail_i", [P, E], i32)
        tail_id = sb("tail_id", [P, E + SPARE, KT, 2])
        mix = sb("mix", [P, NB * KT, 2])
        base = sb("base", [P, 1, E])
        base0 = sb("base0", [P, 1, E])

        m_bank = [ctx.enter_context(nc.psum_tensor(f"m_bank{i}", [P, 512], f32)) for i in range(4)]
        s_bank = [ctx.enter_context(nc.psum_tensor(f"s_bank{i}", [P, 512], f32)) for i in range(2)]
        t_bank = ctx.enter_context(nc.psum_tensor("t_bank", [P, 512], f32))
        o_bank = ctx.enter_context(nc.psum_tensor("o_bank", [P, 512], f32))

        prep = ExitStack()

        def pb(name, shape, dt=f32):
            return prep.enter_context(nc.sbuf_tensor(name, shape, dt))

        far = pb("far", [P, 4, PW])
        cur_s = pb("cur_s", [P, P])
        prev_s = pb("prev_s", [P, P])
        wqk = pb("wqk", [P, CC, C])
        wvo = pb("wvo", [P, CC, C + 2])
        wq_s = pb("wq_s", [P, CC, C])
        wk_s = pb("wk_s", [P, CC, C])
        wv_s = pb("wv_s", [P, CC, C])
        wo_s = pb("wo_s", [P, CC, C])
        bq_s = pb("bq_s", [P, CC, 1])
        bk_s = pb("bk_s", [P, CC, 1])
        bv_s = pb("bv_s", [P, CC, 1])
        bo_s = pb("bo_s", [P, CC, 1])
        bqb = pb("bqb", [P, CC, P])
        XR = 8
        xs = pb("xs", [P, XR, CC, BT])
        stats = pb("stats", [P, CC, NB, 6])
        mv = pb("mv", [P, CC, NI, 2])
        g1 = pb("g1", [P, CC, NI])
        g2 = pb("g2", [P, CC, NI])
        g3 = pb("g3", [P, CC, NI])
        s_all = pb("s_all", [P, CC, NI])
        b_all = pb("b_all", [P, CC, NI])

        w_in = sem("w_in")
        x_in = [sem(f"x_in{i}") for i in range(2)]
        w_experts = sem("w_experts")
        x_seen = [sem(f"x_seen{i}") for i in range(XR)]
        x_done = [sem(f"x_done{i}") for i in range(XR)]
        pool_const = sem("pool_const")
        dve_const = sem("dve_const")
        fold = sem("fold")
        folded = sem("folded")
        kept = sem("kept")
        d0 = sem("d0")
        g_sum = sem("g_sum")
        roots = sem("roots")
        prepared = sem("prepared")
        passed = sem("passed")

        def load_rows(eng, par, blk):
            img, row = blk // IB, blk % IB
            for at, n, r in ((W, BT, row * ROWS), (0, W, (row * ROWS + H - 1) % H),
                             (W + BT, W, (row * ROWS + ROWS) % H)):
                src = xv[:, :, bass.ds(img, 1), bass.ds(r * W, n)]
                eng.dma_start(raw[:, par, :, at:at + n], src).then_inc(x_in[par], 16)

        with nc.Block() as block:
            @block.sync
            def _(eng):
                for dst, src in ((wq_s, wqT), (wk_s, wkT), (wv_s, wvT), (wo_s, wo), (wp_s, wpT), (rw_s, rwT)):
                    eng.dma_start(dst[:, :, :], src.rearrange("(c p) n -> p c n", p=P)).then_inc(w_in, 16)
                for dst, src in ((bq_s, bq), (bk_s, bk), (bv_s, bv), (bo_s, bo)):
                    eng.dma_start(dst[:, :, :], src.unsqueeze(2)).then_inc(w_in, 16)
                eng.dma_start(bp_s[:, :], bp).then_inc(w_in, 16)
                eng.dma_start(wg_s[:, :], wg).then_inc(w_in, 16)
                for i in range(XR):
                    eng.dma_start(xs[:, i, :, :], xv[:, :, i // IB, i % IB * BT:(i % IB + 1) * BT])\
                       .then_inc(x_seen[i], 16)
                if NI > 1:
                    with eng.Fori(1, NI) as img:
                        for i in range(XR):
                            eng.wait_ge(x_done[i], img)
                            eng.dma_start(xs[:, i, :, :],
                                          xv[:, :, bass.ds(img, 1), i * BT:(i + 1) * BT])\
                               .then_inc(x_seen[i], 16)

                for blk in range(2):
                    load_rows(eng, blk, blk)

            @block.gpsimd
            def _(eng):
                done = 0
                eng.memset(ident[:, :], 0.0).then_inc(pool_const, 1)
                done += 1
                eng.wait_ge(pool_const, done)
                eng.memset(group[:, :], 0.125).then_inc(pool_const, 1)
                done += 1
                eng.wait_ge(pool_const, done)
                eng.memset(halves[:, :, :], -0.5).then_inc(pool_const, 1)
                done += 1
                eng.wait_ge(pool_const, done)
                eng.memset(ones[:, :], 1.0).then_inc(pool_const, 1)
                done += 1
                eng.wait_ge(pool_const, done)
                eng.memset(onesb[:, :], 1.0).then_inc(pool_const, 1)
                done += 1
                eng.wait_ge(pool_const, done)
                eng.memset(far[:, :, :], 0.0).then_inc(pool_const, 1)
                done += 1
                eng.wait_ge(pool_const, done)
                eng.iota(expert_ids[:, :], pattern=[[1, E]], base=0, channel_multiplier=0,
                         allow_small_or_imprecise_dtypes=True).then_inc(pool_const, 1)
                done += 1
                eng.wait_ge(pool_const, done)
                eng.iota(places[:, :], pattern=[[2 * BT, NB], [2, KT]], base=0, channel_multiplier=2 * KT,
                         allow_small_or_imprecise_dtypes=True).then_inc(pool_const, 1)
                done += 1
                eng.wait_ge(pool_const, done)
                eng.iota(base0[:, 0, :], pattern=[[1, E]], base=0, channel_multiplier=0,
                         allow_small_or_imprecise_dtypes=True).then_inc(pool_const, 1)
                done += 1
                eng.wait_ge(pool_const, done)
                eng.affine_select(out=ident[:, :], in_=ident[:, :], compare_op=ALU.not_equal, fill=1.0,
                                  base=0, pattern=[[-1, P]], channel_multiplier=1).then_inc(pool_const, 1)
                done += 1
                eng.wait_ge(pool_const, done)
                gv = group[:, :].rearrange("p (a b) -> p a b", b=8)
                eng.affine_select(out=gv, in_=gv, compare_op=ALU.is_ge, fill=0.0,
                                  base=0, pattern=[[-8, P // 8], [0, 8]], channel_multiplier=1).then_inc(pool_const, 1)
                done += 1
                eng.wait_ge(pool_const, done)
                eng.affine_select(out=earlier[:, :], in_=onesb[:, :], compare_op=ALU.is_gt, fill=0.0,
                                  base=0, pattern=[[1, P]], channel_multiplier=-1).then_inc(pool_const, 1)
                done += 1
                eng.wait_ge(pool_const, done)
                eng.affine_select(out=cur_s[:, :], in_=ones[:, :], compare_op=ALU.is_ge, fill=0.0,
                                  base=0, pattern=[[1, P]], channel_multiplier=-1).then_inc(pool_const, 1)
                done += 1
                eng.wait_ge(pool_const, done)
                eng.affine_select(out=prev_s[:, :], in_=ones[:, :], compare_op=ALU.is_ge, fill=0.0,
                                  base=WIN - 1 - P, pattern=[[-1, P]], channel_multiplier=1).then_inc(pool_const, 1)
                done += 1
                eng.wait_ge(pool_const, done)
                for h in range(2):
                    fv = far[W * h:W * h + W, :, :]
                    eng.affine_select(out=fv, in_=fv, compare_op=ALU.is_ge, fill=FAR, base=0,
                                      pattern=[[0, 4], [1, PW]], channel_multiplier=-1).then_inc(pool_const, 1)
                    done += 1
                    eng.wait_ge(pool_const, done)
                eng.affine_select(out=gv, in_=gv, compare_op=ALU.is_ge, fill=0.0,
                                  base=7, pattern=[[8, P // 8], [0, 8]], channel_multiplier=-1).then_inc(pool_const, 1)
                done += 1
                eng.wait_ge(pool_const, done)
                eng.affine_select(out=cur_s[:, :], in_=cur_s[:, :], compare_op=ALU.is_ge, fill=0.0,
                                  base=WIN - 1, pattern=[[-1, P]], channel_multiplier=1).then_inc(pool_const, 1)
                done += 1
                eng.wait_ge(pool_const, done)
                for h in range(2):
                    fv = far[W * h:W * h + W, :, :]
                    eng.affine_select(out=fv, in_=fv, compare_op=ALU.is_ge, fill=FAR, base=2,
                                      pattern=[[0, 4], [-1, PW]], channel_multiplier=1).then_inc(pool_const, 1)
                    done += 1
                    eng.wait_ge(pool_const, done)
                eng.memset(far[0:W, 3, :], FAR).then_inc(pool_const, 1)
                done += 1
                eng.wait_ge(pool_const, done)
                eng.memset(far[W:P, 0, :], FAR).then_inc(pool_const, 1)
                done += 1
                eng.wait_ge(pool_const, done)
                eng.wait_ge(folded, 2)
                for two, whole in ((wqk2, wqk), (wvo2, wvo)):
                    last = eng.tensor_tensor(two[:, 1, :, :], whole[:, :, :], two[:, 0, :, :].bitcast(f32),
                                             ALU.subtract)
                last.then_inc(folded, 1)
                eng.wait_ge(d0, 6)
                eng.tensor_tensor(g2[:, :, :], g2[:, :, :], halves[:, :, 0:NI], ALU.pow).then_inc(roots, 1)
                eng.wait_ge(d0, 9)
                eng.tensor_tensor(g3[:, :, :], g3[:, :, :], halves[:, :, 0:NI], ALU.pow).then_inc(roots, 1)

            @block.tensor
            def _(eng):
                eng.wait_ge(w_in, 16 * 12)
                eng.wait_ge(dve_const, 1)

                def product(bank, cols, lhs, rhs):
                    for d in range(CC):
                        last = eng.matmul(bank[:, cols], lhs(d), rhs(d), start=(d == 0), stop=(d == CC - 1))
                    return last
                for c in range(CC):
                    cs = slice(c * P, c * P + P)
                    product(m_bank[c], slice(0, C), lambda d: wq_s[:, d, cs], lambda d: wk_s[:, d, :])
                    product(m_bank[c], slice(C, C + 1), lambda d: wk_s[:, d, cs], lambda d: bq_s[:, d, :])
                    product(m_bank[c], slice(C + 1, C + 2), lambda d: wq_s[:, d, cs], lambda d: bk_s[:, d, :])
                    product(m_bank[2 + c], slice(0, C), lambda d: wv_s[:, d, cs], lambda d: wo_s[:, d, :])
                    product(m_bank[2 + c], slice(C, C + 1), lambda d: wo_s[:, d, cs], lambda d: bv_s[:, d, :])
                product(s_bank[0], slice(0, 1), lambda d: bqb[:, d, :], lambda d: bk_s[:, d, :]).then_inc(fold, 1)
                eng.wait_ge(pool_const, 22)
                eng.wait_ge(d0, 2)
                eng.matmul(s_bank[1][:, 0:CC * NI], group[:, :], g1[:, :, :].rearrange("p a b -> p (a b)"),
                           start=True, stop=True).then_inc(g_sum, 1)
                eng.wait_ge(d0, 5)
                eng.matmul(s_bank[1][:, 32:32 + CC * NI], group[:, :], g3[:, :, :].rearrange("p a b -> p (a b)"),
                           start=True, stop=True).then_inc(g_sum, 1)

            @block.scalar
            def _(eng):
                eng.wait_ge(w_in, 16 * 12)
                eng.wait_ge(kept, 2)
                eng.wait_ge(fold, 1)
                for c in range(CC):
                    eng.activation(wqk[:, c, :], m_bank[c][:, 0:C], ACT.Copy, scale=-SCALE)
                    eng.activation(r_bias[:, c, :], m_bank[c][:, C:C + 1], ACT.Copy, scale=-SCALE)
                    eng.activation(wvo[:, c, C:C + 1], m_bank[c][:, C + 1:C + 2], ACT.Copy, scale=-SCALE)
                    eng.activation(wvo[:, c, 0:C], m_bank[2 + c][:, 0:C], ACT.Copy)
                    eng.activation(o_bias[:, c, :], m_bank[2 + c][:, C:C + 1], ACT.Identity, bias=bo_s[:, c, :])
                eng.activation(q_const[:, :], s_bank[0][:, 0:1], ACT.Copy, scale=-SCALE).then_inc(folded, 1)
                eng.wait_ge(folded, 1)
                for two, whole in ((wqk2, wqk), (wvo2, wvo)):
                    last = eng.activation(two[:, 0, :, :], whole[:, :, :], ACT.Copy)
                last.then_inc(folded, 1)

            @block.vector
            def _(eng):
                eng.memset(keep[:, :], 1.0).then_inc(kept, 1)
                for c in range(CC):
                    last = eng.memset(wvo[:, c, C + 1:C + 2], 0.0)
                last.then_inc(kept, 1)
                eng.wait_ge(w_in, 16 * 12)
                eng.tensor_copy(bqb[:, :, :], bq_s[:, :, :].broadcast_to([P, CC, P])).then_inc(dve_const, 1)
                for i in range(XR):
                    eng.wait_ge(x_seen[i], 16)
                    for c in range(CC):
                        last = eng.bn_stats(stats[:, c, i, :], xs[:, i, c, :])
                    last.then_inc(x_done[i], 1)
                if NI > 1:
                    with eng.Fori(1, NI) as img:
                        for i in range(XR):
                            eng.wait_ge(x_seen[i], img * 16 + 16)
                            for c in range(CC):
                                last = eng.bn_stats(stats[:, c, bass.ds(img * IB + i, 1), :], xs[:, i, c, :])
                            last.then_inc(x_done[i], 1)
                eng.wait_ge(x_done[XR - 1], NI)
                for c in range(CC):
                    for i in range(NI):
                        last = eng.bn_aggr(mv[:, c, i, :], stats[:, c, i * IB:(i + 1) * IB, :].rearrange("p a b -> p (a b)"))
                last.then_inc(d0, 1)
                eng.wait_ge(d0, 1)
                eng.tensor_copy(g1[:, :, :], mv[:, :, :, 0]).then_inc(d0, 1)
                eng.wait_ge(g_sum, 1)
                gm = s_bank[1][:, 0:CC * NI].rearrange("p (a b) -> p a b", a=CC)
                gv = s_bank[1][:, 32:32 + CC * NI].rearrange("p (a b) -> p a b", a=CC)
                eng.tensor_tensor(g2[:, :, :], g1[:, :, :], gm, ALU.subtract).then_inc(d0, 1)
                eng.wait_ge(d0, 3)
                eng.tensor_tensor(g2[:, :, :], g2[:, :, :], g2[:, :, :], ALU.mult).then_inc(d0, 1)
                eng.wait_ge(d0, 4)
                eng.tensor_tensor(g3[:, :, :], g2[:, :, :], mv[:, :, :, 1], ALU.add).then_inc(d0, 1)
                eng.wait_ge(g_sum, 2)
                eng.tensor_scalar(g2[:, :, :], gv, EPS, None, ALU.add).then_inc(d0, 1)
                eng.wait_ge(roots, 1)
                eng.tensor_tensor(g3[:, :, :], g2[:, :, :], g2[:, :, :], ALU.mult).then_inc(d0, 1)
                eng.wait_ge(d0, 7)
                eng.tensor_tensor(g3[:, :, :], g3[:, :, :], mv[:, :, :, 1], ALU.mult).then_inc(d0, 1)
                eng.wait_ge(d0, 8)
                eng.tensor_scalar(g3[:, :, :], g3[:, :, :], EPS, None, ALU.add).then_inc(d0, 1)
                eng.wait_ge(roots, 2)
                eng.tensor_tensor(s_all[:, :, :], g3[:, :, :], g2[:, :, :], ALU.mult).then_inc(d0, 1)
                eng.wait_ge(d0, 10)
                eng.scalar_tensor_tensor(b_all[:, :, :], g1[:, :, :], -1.0, s_all[:, :, :], ALU.mult, ALU.mult).then_inc(d0, 1)
                eng.wait_ge(d0, 11)
                for c in range(CC):
                    for kind in range(3):
                        for half, src in ((0, s_all), (1, b_all)):
                            last = eng.tensor_copy(
                                tab[:, 2 * kind + half, c, :].rearrange("p (i b) -> p i b", b=IB),
                                src[:, c, :].unsqueeze(2).broadcast_to([P, NI, IB]))
                last.then_inc(d0, 1)
                eng.wait_ge(d0, 12)
                tv = tab[:, :, :, :].rearrange("p k c (i b) -> p k c i b", b=IB)
                for k in range(2):
                    for c in range(CC):
                        eng.memset(tv[:, 2 + k, c, :, 0], 0.0)
                        eng.memset(tv[:, 4 + k, c, :, IB - 1], 0.0)
                eng.wait_ge(kept, 1)
                eng.memset(keep[:, :].rearrange("p (i b) -> p i b", b=IB)[:, :, 0], 0.0)
                eng.wait_ge(pool_const, 22)
                eng.tensor_copy(band_cur[:, :], cur_s[:, :])
                eng.tensor_copy(band_prev[:, :], prev_s[:, :])
                eng.tensor_copy(far2[:, 0:REAL].rearrange("p (a b) -> p a b", b=W), far[:, :, 1:W + 1])
                eng.tensor_copy(far2[:, REAL:REAL + 4], far[:, :, 0])
                eng.tensor_copy(far2[:, REAL + 4:NBR], far[:, :, PW - 1])
                eng.tensor_reduce(edge[:, :], far[:, :, 0:PW:PW - 1], AX.XY, ALU.min)
                eng.wait_ge(folded, 3)
                eng.tensor_scalar(base[:, 0, :], base0[:, 0, :], float(CAP), None, ALU.mult).then_inc(prepared, 1)

        prep.close()
        loop1 = ExitStack()

        def lb(name, shape, dt=f32):
            return loop1.enter_context(nc.sbuf_tensor(name, shape, dt))

        normed = lb("normed", [P, CC, (ROWS + 2) * W])
        band = lb("band", [P, 2, 2, CC, (ROWS + 2) * W], f32r)
        xb = lb("xb", [P, 2, CC, BT])
        rT = lb("rT", [P, 2, 2, CC, BT], f32r)
        vv = lb("vv", [P, 2, VC, C + 2])
        sm = lb("sm", [P, 2, NBR])
        ex = lb("ex", [P, 2, NBR])
        at = lb("at", [P, 2, 2, P])
        edge_norm = lb("edge_norm", [P, 4, CC])
        xt = lb("xt", [P, KT, C])
        lowest = lb("lowest", [P, KT])
        qb = lb("qb", [P, KT])
        shift = lb("shift", [P, KT])
        den = lb("den", [P, KT])
        rden = lb("rden", [P, KT])
        tt = lb("tt", [P, 2, KT, C])
        bn6 = lb("bn6", [P, KT, 6])
        mv4 = lb("mv4", [P, KT, 2])
        ve = lb("ve", [P, KT])
        mean_rs = lb("mean_rs", [P, KT])
        rs = lb("rs", [P, KT])
        xn1 = lb("xn1", [P, KT, C + 2])
        xn1T = lb("xn1T", [P, CC, BT])
        pT = lb("pT", [P, BT])
        eg = lb("eg", [P, KT])
        gg = lb("gg", [P, KT])
        wx = lb("wx", [P, 2, 2, KT, C + 2], f32r)
        wprev = lb("wprev", [P, 2, C + 2], f32r)
        wden = lb("wden", [P, KT])
        tn = lb("tn", [P, 2, KT, C + 2])
        tnT = lb("tnT", [P, CC, BT])
        rsum = lb("rsum", [P, 2, KT, C])
        logit = lb("logit", [P, KT, E])
        best = lb("best", [P, KT, 8])
        besti = lb("besti", [P, KT, 8], u32)
        down = lb("down", [P, KT, 8])
        e8 = lb("e8", [P, KT, 8])
        zsum = lb("zsum", [P, KT, 1])
        p12 = lb("p12", [P, KT, 2])
        psum2 = lb("psum2", [P, KT, 1])
        idf = lb("idf", [P, KT, 2])
        hot = lb("hot", [P, 2, KT, E])
        chosen = lb("chosen", [P, KT, E], bf16)
        where = lb("where", [P, KT, E])
        prod = lb("prod", [P, 2, KT, E])
        slotf = lb("slotf", [P, 2, KT])
        slot_s = lb("slot_s", [P, 2, 2, KT], i32)

        jvec = lb("jvec", [P, NJ])
        count = lb("count", [P, E])
        counti = lb("counti", [P, E], i32)
        tiles_of = lb("tiles_of", [P, E])
        upto = lb("upto", [P, E, E])
        ends = lb("ends", [P, E])
        past = lb("past", [P, NJ, E])
        hop = lb("hop", [P, E])
        hops = lb("hops", [P, NJ, E])
        row_f = lb("row_f", [P, NJ])
        tables = sem("tables")
        tails = sem("tails")
        zeroed = sem("zeroed")
        tailed = sem("tailed")
        jiota = sem("jiota")

        JOBS = ("AV0 AV1 AV2 AV3 BX01 AR0 Dtr01 Dtr23 AR1 Drouter Ctr01 Ctr23 BX23 Cproj Cgate AV4 Dpos "
                "Cwin0 Cwin1 Cwin2 Cwin3").split()
        bank_of = {job: i % 4 for i, job in enumerate(JOBS)}
        orders = [" ".join(j for j in JOBS if bank_of[j] == i) for i in range(4)]
        full = [sig(f"full{i}", orders[i]) for i in range(4)]
        taken = [sig(f"taken{i}", orders[i]) for i in range(4)]
        s_full = [sig(f"s_full{i}", f"BS{i} BS{i + 2}") for i in range(2)]
        s_taken = [sig(f"s_taken{i}", f"BS{i} BS{i + 2}") for i in range(2)]
        tiles = lambda s: " ".join(f"{s}{k}" for k in range(KT))
        at_full = sig("at_full", tiles("BAT"))
        at_taken = sig("at_taken", tiles("BAT"))
        o_full = sig("o_full", tiles("BAV"))
        t_ready = sig("t_ready", tiles("Bt"))
        exp_ready = sig("exp_ready", tiles("BE"))
        qb_ready = sig("qb_ready", "Bqb")
        masked = sig("masked", tiles("BM"))
        rden_ready = sig("rden_ready", tiles("Brd"))
        ln_step = sig("ln_step", "Cst1 Cag1 Cve1 Cms1 Cst2 Cag2 Cve2 Ctn")
        xn1_ready = sig("xn1_ready", "Cxn1")
        root = sig("root", "Crs1 Crs2")
        prev_ready = sig("prev_ready", "Cprev")
        gate_step = sig("gate_step", "Cg1 Cg")
        wx_high = sig("wx_high", tiles("Cwh"))
        wx_ready = sig("wx_ready", tiles("Cwx"))
        high = sig("high", "Ah0 Ah1")
        band_high = sig("band_high", "Nbh")
        band_ready = sig("band_ready", "Nbl")
        wden_ready = sig("wden_ready", tiles("Cwd"))
        sum_ready = sig("sum_ready", "CR")
        route = sig("route", "Dbest Dbesti Ddown Didf Dhot DM Dwhere Dbase Dz Dprod Dzi "
                             "Dslotf Dp Dsl Dps Dpm Dpi Dmix")
        rexp = sig("rexp", "DE")
        main_ready = sig("main_ready", "Nmain")
        halo_ready = sig("halo_ready", "Nhalo")
        edge_ready = sig("edge_ready", "Nedge")
        xb_ready = sig("xb_ready", "Nxb")
        sum_out = [sem(f"sum_out{i}") for i in range(2)]
        scattered = [sem(f"scattered{i}") for i in range(2)]
        cleared = sem("cleared")

        def alone(eng, *waits):
            for s, v in waits:
                eng.wait_ge(s, v)
            eng.sem_inc(passed, 1)

        def iterations(eng, body):
            for off in range(-2, 4):
                body(Iteration(None, off, NB))
            with eng.Fori(2, NB // 2 - 1) as half:
                for off in range(2):
                    body(Iteration(half, off, NB))
            for off in range(NB - 2, NB + 3):
                body(Iteration(None, off, NB))

        def column(ap, at):
            return ap[:, at:at + 1] if isinstance(at, int) else ap[:, bass.ds(at, 1)]

        flat = "p a b -> p (a b)"

        def fill_rows(eng, row, number):
            rows = sent[bass.ds(row, BT), :].rearrange("(p k) c -> p k c", k=KT)
            eng.dma_start(rows[:, :, 0:C], w1_s[:, :, :, :].rearrange("p e c n -> p (e c) n")[:, 0:KT, :])\
               .then_inc(tails, 16)
            eng.dma_start(rows[:, :, C:C + 2], tail_id[:, number, :, :]).then_inc(tails, 16)

        with nc.Block() as block:
            @block.sync
            def _(eng):
                eng.wait_ge(prepared, 1)

                def body(it):
                    if it.runs("N") and (it.base is not None or it.block("N") >= 2):
                        par, blk = it.parity("N"), it.block("N")
                        two = it.before().before()
                        main_ready.wait(eng, two, "Nmain")
                        halo_ready.wait(eng, two, "Nhalo")
                        xb_ready.wait(eng, two, "Nxb")
                        load_rows(eng, par, blk)
                    if it.base is None and it.off == 0:
                        for dst, src in ((w1_s, w1), (w2_s, w2)):
                            for c in range(CC):
                                eng.dma_start(dst[:, :, c, :], src[:, c * P:(c + 1) * P, :].rearrange("e p n -> p e n"))\
                                   .then_inc(w_experts, 16)
                    if it.base is None and it.off == 3:
                        eng.wait_ge(w_experts, 16 * 2 * CC)
                        eng.wait_ge(tailed, 1)
                        for i in range(SPARE):
                            fill_rows(eng, E * CAP + i * BT, E + i)
                    prior = it.before()
                    if prior.runs("C"):
                        par, blk = prior.parity("C"), prior.block("C")
                        sum_ready.wait(eng, prior, "CR")
                        eng.dma_start(residual_v[bass.ds(blk, 1), :, :], rsum[:, par, :, :].rearrange(flat))\
                           .then_inc(sum_out[par], 16)
                iterations(eng, body)
                eng.wait_ge(tables, 1)
                for e in range(E):
                    fill_rows(eng, eng.value_load(tail_i[0:1, e:e + 1], min_val=0, max_val=E * CAP), e)
                for i in range(2):
                    eng.wait_ge(sum_out[i], 16 * (NB // 2))

            @block.tensor
            def _(eng):
                eng.wait_ge(prepared, 1)
                eng.wait_ge(cleared, 5)

                def begin(it, job):
                    taken[bank_of[job]].wait_before(eng, it, job)
                    return m_bank[bank_of[job]]

                def end(last, job):
                    last.then_inc(full[bank_of[job]].sem, 1)

                def moved(it, job):
                    taken[bank_of[job]].wait(eng, it, job)

                def exact(dst, lhs, rhs):
                    passes = [(c, i, j) for c in range(CC) for i, j in ((0, 0), (0, 1), (1, 0))]
                    for n, (c, i, j) in enumerate(passes):
                        last = eng.matmul(dst, lhs(i, c), rhs(j, c), start=(n == 0), stop=(n == len(passes) - 1))
                    return last

                def logits(it, k):
                    par = it.parity("B")
                    if k == 0:
                        moved(it.before(), "AR0")
                        moved(it.before(), "AR1")
                    s_taken[k % 2].wait_before(eng, it, f"BS{k}")
                    bank = s_bank[k % 2]
                    last = exact(bank[:, 0:REAL], lambda h, c: rT[:, par, h, c, k * P:(k + 1) * P],
                                 lambda h, c: band[:, par, h, c, k * P:k * P + REAL])
                    last.then_inc(s_full[k % 2].sem, 1)

                def attend(it, k):
                    par = it.parity("B")
                    exp_ready.wait(eng, it, f"BE{k}")
                    at_taken.wait_before(eng, it, f"BAT{k}")
                    for j in range(2):
                        last = eng.transpose(t_bank[:, j * P:(j + 1) * P], ex[:, k % 2, j * P:(j + 1) * P],
                                             ident[:, :])
                    last.then_inc(at_full.sem, 1)

                def weigh(it, k):
                    par = it.parity("B")
                    at_taken.wait(eng, it, f"BAT{k}")
                    t_ready.wait_before(eng, it, f"Bt{k}")
                    if k == 0:
                        for j in range(VC):
                            moved(it.before(), f"AV{j}")
                    for j in range(2):
                        last = eng.matmul(o_bank[:, 0:C], at[:, k % 2, j, :], vv[:, par, k + j, 0:C],
                                          start=(j == 0), stop=(j == 1))
                    last.then_inc(o_full.sem, 1)

                def transposed(it, job, src, k0, per_tile):
                    bank = begin(it, job)
                    for k in (k0, k0 + 1):
                        for c in range(CC):
                            col = (k - k0) * C + c * P if per_tile else c * 2 * P + (k - k0) * P
                            last = eng.transpose(bank[:, col:col + P], src(k, c), ident[:, :])
                    end(last, job)

                def values(it, j):
                    par = it.parity("A")
                    if j == 0:
                        band_ready.wait(eng, it.before(), "Nbl")
                    bank = begin(it, f"AV{j}")
                    end(exact(bank[:, 0:C + 2], lambda h, c: band[:, par, h, c, j * P:(j + 1) * P],
                              lambda h, c: wvo2[:, h, c, :]), f"AV{j}")

                def queries(it, co):
                    par = it.parity("A")
                    bank = begin(it, f"AR{co}")
                    end(exact(bank[:, :], lambda h, c: wqk2[:, h, c, co * P:(co + 1) * P],
                              lambda h, c: band[:, par, h, c, W:W + BT]), f"AR{co}")

                def window(it, k):
                    par, job = it.parity("C"), f"Cwin{k}"
                    wx_ready.wait(eng, it, f"Cwx{k}")
                    if k == 0:
                        prev_ready.wait(eng, it, "Cprev")
                    bank = begin(it, job)
                    for h in range(2):
                        eng.matmul(bank[:, 0:C + 2], band_cur[:, :], wx[:, par, h, k, :], start=(h == 0), stop=False)
                    for h in range(2):
                        before = wprev[:, h, :] if k == 0 else wx[:, par, h, k - 1, :]
                        last = eng.matmul(bank[:, 0:C + 2], band_prev[:, :], before, start=False, stop=(h == 1))
                    end(last, job)

                def gate_product(it):
                    moved(it, "Ctr01")
                    moved(it, "Ctr23")
                    bank = begin(it, "Cproj")
                    for cc in range(CC):
                        last = eng.matmul(bank[:, :], wp_s[:, cc, :], xn1T[:, cc, :], start=(cc == 0),
                                          stop=(cc == CC - 1))
                    end(last, "Cproj")

                def gates(it):
                    moved(it, "Cproj")
                    bank = begin(it, "Cgate")
                    for k in range(KT):
                        last = eng.matmul(bank[:, k:k + 1], pT[:, k * P:(k + 1) * P], wg_s[:, :], start=True,
                                          stop=True)
                    end(last, "Cgate")

                def router(it):
                    moved(it, "Dtr01")
                    moved(it, "Dtr23")
                    bank = begin(it, "Drouter")
                    for k in range(KT):
                        for cc in range(CC):
                            last = eng.matmul(bank[:, k * E:(k + 1) * E], tnT[:, cc, k * P:(k + 1) * P],
                                              rw_s[:, cc, :], start=(cc == 0), stop=(cc == CC - 1))
                    end(last, "Drouter")

                def positions(it):
                    route.wait(eng, it, "DM")
                    bank = begin(it, "Dpos")
                    for k in range(KT):
                        for j in range(k + 1):
                            eng.matmul(bank[:, k * E:(k + 1) * E], (earlier if j == k else onesb)[:, :],
                                       chosen[:, j, :], start=(j == 0), stop=(j == k))
                    for k in range(KT):
                        last = eng.matmul(bank[:, KT * E:KT * E + E], onesb[:, :], chosen[:, k, :],
                                          start=(k == 0), stop=(k == KT - 1))
                    end(last, "Dpos")

                def x_turned(it, k0):
                    xb_ready.wait(eng, it.before().before(), "Nxb")
                    transposed(it, "BX01" if k0 == 0 else "BX23",
                               lambda k, cc: xb[:, it.parity("B"), cc, k * P:(k + 1) * P], k0, True)

                def gated_turned(it):
                    xn1_ready.wait(eng, it, "Cxn1")
                    for k0 in (0, 2):
                        transposed(it, f"Ctr{k0}{k0 + 1}", lambda k, cc: xn1[:, k, cc * P:(cc + 1) * P], k0, False)

                def tokens_turned(it):
                    ln_step.wait(eng, it.before(), "Ctn")
                    for k0 in (0, 2):
                        transposed(it, f"Dtr{k0}{k0 + 1}",
                                   lambda k, cc: tn[:, it.parity("D"), k, cc * P:(cc + 1) * P], k0, False)

                def body(it):
                    a, b, c, d = (it.runs(s) for s in "ABCD")
                    if b:
                        logits(it, 0)
                        logits(it, 1)
                    if a:
                        for j in range(VC - 1):
                            values(it, j)
                    if b:
                        attend(it, 0)
                        x_turned(it, 0)
                    if a:
                        queries(it, 0)
                    if b:
                        weigh(it, 0)
                    if d:
                        tokens_turned(it)
                    if b:
                        logits(it, 2)
                        attend(it, 1)
                    if a:
                        queries(it, 1)
                    if d:
                        router(it)
                    if b:
                        weigh(it, 1)
                    if c:
                        gated_turned(it)
                    if b:
                        logits(it, 3)
                        attend(it, 2)
                        x_turned(it, 2)
                    if c:
                        gate_product(it)
                    if b:
                        weigh(it, 2)
                        attend(it, 3)
                    if c:
                        gates(it)
                    if a:
                        values(it, 4)
                    if d:
                        positions(it)
                    if b:
                        weigh(it, 3)
                    if c:
                        window(it, 0)
                        window(it, 1)
                        window(it, 2)
                        window(it, 3)
                iterations(eng, body)

            @block.scalar
            def _(eng):
                eng.wait_ge(prepared, 1)
                eng.wait_ge(cleared, 5)

                def take(it, job, out_, in_=None, func=ACT.Copy, **k):
                    i = bank_of[job]
                    full[i].wait(eng, it, job)
                    src = m_bank[i][:, 0:out_.free_size()] if in_ is None else in_
                    eng.activation(out_, src, func, **k).then_inc(taken[i].sem, 1)

                def upper(it, job, event, out_, in_=None, func=ACT.Copy, **k):
                    i = bank_of[job]
                    full[i].wait(eng, it, job)
                    eng.activation(out_, m_bank[i][:, :] if in_ is None else in_, func, **k).then_inc(high.sem, 1)

                def expo(it, k):
                    s_taken[k % 2].wait(eng, it, f"BS{k}")
                    eng.activation(ex[:, k % 2, :], sm[:, k % 2, :], ACT.Exp,
                                   bias=shift[:, k:k + 1], scale=-1.0,
                                   accum_out=den[:, k:k + 1]).then_inc(exp_ready.sem, 1)

                def take_at(it, k):
                    at_full.wait(eng, it, f"BAT{k}")
                    eng.activation(at[:, k % 2, :, :].rearrange(flat), t_bank[:, 0:2 * P], ACT.Copy)\
                       .then_inc(at_taken.sem, 1)

                def pair_of(dst, k0):
                    return dst[:, :, k0 * P:(k0 + 2) * P]

                def bank2(job):
                    return m_bank[bank_of[job]][:, :].rearrange("p (a b) -> p a b", a=CC)

                def body(it):
                    a, b, c, d, n = (it.runs(s) for s in "ABCDN")
                    pa, pn, par = it.parity("A"), it.parity("N"), it.parity("C")
                    if b:
                        expo(it, 0)
                    if a:
                        for j in range(VC - 1):
                            take(it, f"AV{j}", vv[:, pa, j, :])
                    if b:
                        take_at(it, 0)
                        expo(it, 1)
                    if b:
                        t_ready.wait(eng, it.before(), "Bt3")
                        take(it, "BX01", xt[:, 0:2, :].rearrange(flat))
                    if a:
                        upper(it, "AR0", "Ah0", rT[:, pa, 0, 0, :], func=ACT.Identity, bias=r_bias[:, 0, :])
                    if d:
                        take(it, "Dtr01", pair_of(tnT, 0), bank2("Dtr01"))
                        take(it, "Dtr23", pair_of(tnT, 2), bank2("Dtr23"))
                    if b:
                        take_at(it, 1)
                    if c:
                        ln_step.wait(eng, it, "Cms1")
                        wx_ready.wait(eng, it.before(), "Cwx3")
                        for k in range(KT):
                            last = eng.activation(xn1[:, k, 0:C], tt[:, par, k, :], ACT.Identity,
                                                  bias=mean_rs[:, k:k + 1], scale=rs[:, k:k + 1])
                        last.then_inc(xn1_ready.sem, 1)
                    if a:
                        upper(it, "AR1", "Ah1", rT[:, pa, 0, 1, :], func=ACT.Identity, bias=r_bias[:, 1, :])
                    if b:
                        expo(it, 2)
                    if n:
                        blk = it.block("N")
                        eng.wait_ge(x_in[pn], it.pair("N") * 48 + 48)
                        band_ready.wait(eng, it.before(), "Nbl")
                        for cc in range(CC):
                            last = eng.activation(
                                normed[:, cc, W:W + BT], raw[:, pn, cc, W:W + BT], ACT.Identity,
                                bias=column(tab[:, 1, cc, :], blk), scale=column(tab[:, 0, cc, :], blk))
                        last.then_inc(main_ready.sem, 1)
                    if c:
                        take(it, "Ctr01", pair_of(xn1T, 0), bank2("Ctr01"))
                        take(it, "Ctr23", pair_of(xn1T, 2), bank2("Ctr23"))
                    if b:
                        take_at(it, 2)
                        expo(it, 3)
                        take(it, "BX23", xt[:, 2:4, :].rearrange(flat))
                    if c:
                        take(it, "Cproj", pT[:, :], func=ACT.Tanh, bias=bp_s[:, :])
                    if n:
                        if b:
                            s_taken[1].wait(eng, it, "BS3")
                        main_ready.wait(eng, it, "Nmain")
                        halo_ready.wait(eng, it, "Nhalo")
                        eng.activation(band[:, pn, 0, :, :], normed[:, :, :], ACT.Copy).then_inc(band_high.sem, 1)
                    if b:
                        take_at(it, 3)
                    if c:
                        take(it, "Cgate", eg[:, :], func=ACT.Exp, scale=-1.0)
                    if a:
                        take(it, f"AV{VC - 1}", vv[:, pa, VC - 1, :])
                    if c:
                        gate_step.wait(eng, it, "Cg")
                        for k in range(KT):
                            eng.activation(wx[:, par, 0, k, :], xn1[:, k, :], ACT.Copy, scale=gg[:, k:k + 1])\
                               .then_inc(wx_high.sem, 1)
                    if d:
                        route.wait(eng, it, "Ddown")
                        eng.activation(e8[:, :, :].rearrange(flat), down[:, :, :].rearrange(flat), ACT.Exp)\
                           .then_inc(rexp.sem, 1)
                    if n:
                        for cc in range(CC):
                            last = eng.activation(xb[:, pn, cc, :], raw[:, pn, cc, W:W + BT], ACT.Identity,
                                                  bias=o_bias[:, cc, :])
                        last.then_inc(xb_ready.sem, 1)
                iterations(eng, body)

            @block.vector
            def _(eng):
                eng.wait_ge(prepared, 1)
                eng.memset(xn1[:, :, :], 0.0).then_inc(cleared, 1)
                eng.memset(tail_id[:, :, :, :], 0.0).then_inc(zeroed, 1)
                eng.wait_ge(cleared, 1)
                for i in range(2):
                    eng.tensor_copy(sm[:, i, REAL:NBR], far2[:, REAL:NBR])
                    eng.tensor_copy(wx[:, i, :, KT - 1, :], xn1[:, 0:2, :]).then_inc(cleared, 1)
                eng.wait_ge(cleared, 3)
                eng.memset(xn1[:, :, C:C + 1], 1.0).then_inc(cleared, 1)
                eng.memset(besti[:, :, :].rearrange(flat), 0).then_inc(cleared, 1)

                def done(sgn, last):
                    last.then_inc(sgn.sem, 1)

                def step(it, sgn, event, last):
                    last.then_inc(sgn.sem, 1)
                    sgn.wait(eng, it, event)

                def normal(it, n):
                    par = it.parity("C")
                    for k in range(KT):
                        last = eng.bn_stats(bn6[:, k, :], tt[:, par, k, :])
                    last.then_inc(ln_step.sem, 1)
                    alone(eng, (ln_step.sem, ln_step.count(it, f"Cst{n}")))
                    for k in range(KT):
                        last = eng.bn_aggr(mv4[:, k, :], bn6[:, k, :])
                    step(it, ln_step, f"Cag{n}", last)
                    done(ln_step, eng.tensor_scalar(ve[:, :], mv4[:, :, 1], TOKEN_EPS, None, ALU.add))

                def scaled(it, n, dst):
                    par = it.parity("C")
                    root.wait(eng, it, f"Crs{n}")
                    for k in range(KT):
                        last = eng.tensor_scalar(dst(k), tt[:, par, k, :], mv4[:, k, 0:1], rs[:, k:k + 1],
                                                 ALU.subtract, ALU.mult)
                    done(ln_step, last)

                def bias_terms(it):
                    par = it.parity("B")
                    for j in range(VC):
                        i = bank_of[f"AV{j}"]
                        taken[i].wait(eng, it.before(), f"AV{j}")
                    for i in range(2):
                        s_taken[i].wait(eng, it.before(), f"BS{i + 2}")
                    eng.tensor_scalar(qb[0:W, :], vv[W:P, par, 0:KT, C], q_const[0:W, :], None, ALU.add)
                    done(qb_ready, eng.tensor_scalar(qb[W:P, :], vv[0:W, par, 1:VC, C], q_const[W:P, :], None,
                                                     ALU.add))

                def mask(it, k):
                    bank = s_bank[k % 2]
                    waits = [(s_full[k % 2].sem, s_full[k % 2].count(it, f"BS{k}"))]
                    user = it if k >= 2 else it.before()
                    if user.runs("B"):
                        waits.append((exp_ready.sem, exp_ready.count(user, f"BE{(k - 2) % KT}")))
                    if k == 0:
                        waits.append((qb_ready.sem, qb_ready.count(it, "Bqb")))
                    alone(eng, *waits)
                    step(it, masked, f"BM{k}",
                         eng.tensor_tensor_reduce(out=sm[:, k % 2, 0:REAL], in0=bank[:, 0:REAL],
                                                  in1=far2[:, 0:REAL], scale=1.0, scalar=edge[:, :],
                                                  op0=ALU.add, op1=ALU.min, accum_out=lowest[:, k:k + 1]))
                    eng.scalar_tensor_tensor(shift[:, k:k + 1], lowest[:, k:k + 1], qb[:, k:k + 1], qb[:, k:k + 1],
                                             ALU.add, ALU.subtract).then_inc(s_taken[k % 2].sem, 1)

                def sum_turned(it, k):
                    exp_ready.wait(eng, it, f"BE{k}")
                    done(rden_ready, eng.reciprocal(rden[:, k:k + 1], den[:, k:k + 1]))

                def tokens(it, k):
                    par = it.parity("B")
                    rden_ready.wait(eng, it, f"Brd{k}")
                    if k == 0:
                        sum_ready.wait(eng, it.before(), "CR")
                    if k % 2 == 0:
                        job = "BX01" if k == 0 else "BX23"
                        taken[bank_of[job]].wait(eng, it, job)
                    o_full.wait(eng, it, f"BAV{k}")
                    eng.scalar_tensor_tensor(tt[:, par, k, :], o_bank[:, 0:C], rden[:, k:k + 1], xt[:, k, :],
                                             ALU.mult, ALU.add).then_inc(t_ready.sem, 1)

                def lower_part(it, job, event, dst, upper_, src, bias=None):
                    high.wait(eng, it, event)
                    if bias is None:
                        last = eng.tensor_tensor(dst, src, upper_.bitcast(f32), ALU.subtract)
                    else:
                        last = eng.scalar_tensor_tensor(dst, src, bias, upper_.bitcast(f32), ALU.add, ALU.subtract)
                    last.then_inc(taken[bank_of[job]].sem, 1)

                def query_part(it, co):
                    pa, job = it.parity("A"), f"AR{co}"
                    lower_part(it, job, f"Ah{co}", rT[:, pa, 1, co, :], rT[:, pa, 0, co, :],
                               m_bank[bank_of[job]][:, :], r_bias[:, co, :])

                def gated_part(it, k):
                    par = it.parity("C")
                    wx_high.wait(eng, it, f"Cwh{k}")
                    eng.scalar_tensor_tensor(wx[:, par, 1, k, :], xn1[:, k, :], gg[:, k:k + 1],
                                             wx[:, par, 0, k, :].bitcast(f32), ALU.mult, ALU.subtract)\
                       .then_inc(wx_ready.sem, 1)

                def gates_turned(it, k):
                    i = bank_of[f"Cwin{k}"]
                    full[i].wait(eng, it, f"Cwin{k}")
                    done(wden_ready, eng.reciprocal(wden[:, k:k + 1], m_bank[i][:, C:C + 1]))

                def windowed(it, k):
                    par, i = it.parity("C"), bank_of[f"Cwin{k}"]
                    wden_ready.wait(eng, it, f"Cwd{k}")
                    eng.scalar_tensor_tensor(tt[:, par, k, :], m_bank[i][:, 0:C], wden[:, k:k + 1],
                                             tt[:, par, k, :], ALU.mult, ALU.add).then_inc(taken[i].sem, 1)

                def body(it):
                    a, b, c, d, n = (it.runs(s) for s in "ABCDN")
                    pc = it.parity("C")
                    prior = it.before()
                    if n:
                        halo_ready.wait(eng, prior, "Nhalo")
                        done(edge_ready, eng.tensor_copy(edge_norm[:, :, :], (
                            tab[:, 2:6, :, it.block("N")] if it.base is None else
                            tab[:, 2:6, :, bass.ds(it.block("N"), 1)].rearrange("p a b c -> p a (b c)"))))
                    if b:
                        bias_terms(it)
                        mask(it, 0)
                    if prior.runs("C"):
                        taken[bank_of["Cwin3"]].wait(eng, prior, "Cwin3")
                        normal(prior, 2)
                    if b:
                        mask(it, 1)
                    if prior.runs("C"):
                        pp = prior.parity("C")
                        if prior.base is not None or prior.block("C") >= 2:
                            eng.wait_ge(scattered[pp], prior.pair("C") * (32 * KT))
                        scaled(prior, 2, lambda k: tn[:, pp, k, 0:C])
                    if c:
                        t_ready.wait(eng, it.before(), "Bt3")
                        normal(it, 1)
                    if a:
                        query_part(it, 0)
                    if b:
                        sum_turned(it, 0)
                    if c:
                        wx_ready.wait(eng, it.before(), "Cwx3")
                        done(prev_ready, eng.tensor_scalar(wprev[:, :, :], wx[:, 1 - pc, :, KT - 1, :].bitcast(f32),
                                                           column(keep[:, :], it.block("C")), None, ALU.mult))
                        root.wait(eng, it, "Crs1")
                        done(ln_step, eng.scalar_tensor_tensor(mean_rs[:, :], mv4[:, :, 0], -1.0, rs[:, :],
                                                               ALU.mult, ALU.mult))
                    if b:
                        tokens(it, 0)
                        mask(it, 2)
                    if prior.runs("D"):
                        rexp.wait(eng, prior, "DE")
                        done(route, eng.reduce_sum(zsum[:, :, 0], e8[:, :, :], AX.X))
                        for j in range(2):
                            last = eng.tensor_tensor(prod[:, j, :, :], hot[:, j, :, :], where[:, :, :], ALU.mult)
                        done(route, last)
                        route.wait(eng, prior, "Dz")
                        done(route, eng.reciprocal(zsum[:, :, :], zsum[:, :, :]))
                        route.wait(eng, prior, "Dprod")
                        done(route, eng.reduce_sum(slotf[:, :, :], prod[:, :, :, :], AX.X))
                        route.wait(eng, prior, "Dzi")
                        done(route, eng.tensor_tensor(p12[:, :, :], e8[:, :, 0:2],
                                                      zsum[:, :, :].broadcast_to([P, KT, 2]), ALU.mult))
                        if prior.base is not None or prior.block("D") >= 2:
                            eng.wait_ge(scattered[prior.parity("D")], prior.pair("D") * (32 * KT))
                        route.wait(eng, prior, "Dslotf")
                        eng.tensor_copy(tn[:, prior.parity("D"), :, C], places[:, bass.ds(prior.block("D") * KT, KT)])
                        eng.tensor_copy(tn[:, prior.parity("D"), :, C + 1], idf[:, :, 0])
                        done(route, eng.tensor_copy(slot_s[:, prior.parity("D"), :, :], slotf[:, :, :]))
                        route.wait(eng, prior, "Dp")
                        step(prior, route, "Dps", eng.tensor_tensor(psum2[:, :, :], p12[:, :, 0:1], p12[:, :, 1:2],
                                                                 ALU.add))
                        step(prior, route, "Dpm", eng.tensor_scalar(psum2[:, :, :], psum2[:, :, :], 1e-12, None,
                                                                 ALU.max))
                        step(prior, route, "Dpi", eng.reciprocal(psum2[:, :, :], psum2[:, :, :]))
                        done(route, eng.tensor_tensor(mix[:, bass.ds(prior.block("D") * KT, KT), :], p12[:, :, :],
                                                      psum2[:, :, :].broadcast_to([P, KT, 2]), ALU.mult))
                    if a:
                        query_part(it, 1)
                    if d:
                        i = bank_of["Drouter"]
                        full[i].wait(eng, it, "Drouter")
                        eng.tensor_copy(logit[:, :, :].rearrange(flat), m_bank[i][:, 0:KT * E])\
                           .then_inc(taken[i].sem, 1)
                        alone(eng, (taken[i].sem, taken[i].count(it, "Drouter")))
                        for k in range(KT):
                            last = eng.max(best[:, k, :], logit[:, k, :])
                        last.then_inc(route.sem, 1)
                        alone(eng, (route.sem, route.count(it, "Dbest")))
                        for k in range(KT):
                            last = eng.max_index(besti[:, k, :], best[:, k, :], logit[:, k, :])
                        done(route, last)
                        done(route, eng.tensor_tensor(down[:, :, :], best[:, :, :],
                                                      best[:, :, 0:1].broadcast_to([P, KT, 8]), ALU.subtract))
                    if b:
                        sum_turned(it, 1)
                    if b:
                        tokens(it, 1)
                    if b:
                        mask(it, 3)
                        sum_turned(it, 2)
                    if d:
                        route.wait(eng, it, "Dbesti")
                        step(it, route, "Didf", eng.tensor_copy(idf[:, :, :], besti[:, :, 0:2]))
                        for j in range(2):
                            last = eng.tensor_tensor(hot[:, j, :, :],
                                                     expert_ids[:, :].unsqueeze(1).broadcast_to([P, KT, E]),
                                                     idf[:, :, j:j + 1].broadcast_to([P, KT, E]), ALU.is_equal)
                        step(it, route, "Dhot", last)
                        done(route, eng.tensor_tensor(chosen[:, :, :], hot[:, 0, :, :], hot[:, 1, :, :], ALU.add))
                    if b:
                        tokens(it, 2)
                        sum_turned(it, 3)
                    if c:
                        taken[bank_of["Cgate"]].wait(eng, it, "Cgate")
                        step(it, gate_step, "Cg1", eng.tensor_scalar(gg[:, :], eg[:, :], 1.0, None, ALU.add))
                        done(gate_step, eng.reciprocal(gg[:, :], gg[:, :]))
                    if d:
                        i = bank_of["Dpos"]
                        full[i].wait(eng, it, "Dpos")
                        step(it, route, "Dwhere", eng.tensor_tensor(where[:, :, :],
                                                      m_bank[i][:, 0:KT * E].rearrange("p (a b) -> p a b", b=E),
                                                      base[:, :, :].broadcast_to([P, KT, E]), ALU.add))
                        eng.tensor_tensor(base[:, 0, :], base[:, 0, :], m_bank[i][:, KT * E:KT * E + E],
                                          ALU.add).then_inc(route.sem, 1)
                        route.wait(eng, it, "Dbase")
                        eng.sem_inc(taken[i].sem, 1)
                    if c:
                        gated_part(it, 0)
                        gated_part(it, 1)
                    if b:
                        tokens(it, 3)
                    if c:
                        gated_part(it, 2)
                        gated_part(it, 3)
                        gates_turned(it, 0)
                        for k in range(KT):
                            if k + 1 < KT:
                                gates_turned(it, k + 1)
                            windowed(it, k)
                iterations(eng, body)
                n = [0]

                def follow(ins):
                    n[0] += 1
                    ins.then_inc(tables, 1)
                    eng.wait_ge(tables, n[0])

                follow(eng.tensor_copy(tail_i[:, :], base[:, 0, :]))
                follow(eng.scalar_tensor_tensor(count[:, :], base0[:, 0, :], -float(CAP), base[:, 0, :],
                                              ALU.mult, ALU.add))
                follow(eng.tensor_scalar(count[:, :], count[:, :], float(BT - 1), None, ALU.add))
                follow(eng.tensor_copy(counti[:, :], count[:, :]))
                follow(eng.tensor_scalar(counti[:, :], counti[:, :], BT.bit_length() - 1, None,
                                       ALU.arith_shift_right))
                follow(eng.tensor_copy(tiles_of[:, :], counti[:, :]))
                follow(eng.tensor_tensor(upto[:, :, :], expert_ids[:, :].unsqueeze(2).broadcast_to([P, E, E]),
                                       expert_ids[:, :].unsqueeze(1).broadcast_to([P, E, E]), ALU.is_ge))
                follow(eng.tensor_tensor(upto[:, :, :], upto[:, :, :],
                                       tiles_of[:, :].unsqueeze(1).broadcast_to([P, E, E]), ALU.mult))
                follow(eng.reduce_sum(ends[:, :], upto[:, :, :], AX.X))
                eng.wait_ge(jiota, 1)
                follow(eng.tensor_tensor(past[:, :, :], jvec[:, :].unsqueeze(2).broadcast_to([P, NJ, E]),
                                       ends[:, :].unsqueeze(1).broadcast_to([P, NJ, E]), ALU.is_ge))
                follow(eng.tensor_scalar(hop[:, :], tiles_of[:, :], -float(BT), float(CAP), ALU.mult, ALU.add))
                follow(eng.tensor_tensor(hops[:, :, :], past[:, :, :],
                                       hop[:, :].unsqueeze(1).broadcast_to([P, NJ, E]), ALU.mult))
                eng.reduce_sum(expert_f[:, :], past[:, :, :], AX.X)
                follow(eng.reduce_sum(row_f[:, :], hops[:, :, :], AX.X))
                follow(eng.scalar_tensor_tensor(row_f[:, :], jvec[:, :], float(BT), row_f[:, :], ALU.mult, ALU.add))
                follow(eng.tensor_scalar(expert_f[:, :], expert_f[:, :], float(E - 1), None, ALU.min))
                eng.tensor_copy(expert_i[:, :], expert_f[:, :])
                follow(eng.tensor_copy(row_i[:, :], row_f[:, :]))

            @block.gpsimd
            def _(eng):
                eng.wait_ge(prepared, 1)
                eng.wait_ge(cleared, 5)
                eng.iota(jvec[:, :], pattern=[[1, NJ]], base=0, channel_multiplier=0,
                         allow_small_or_imprecise_dtypes=True).then_inc(jiota, 1)
                eng.wait_ge(zeroed, 1)
                eng.iota(tail_id[:, :, :, 0], pattern=[[2 * BT, E + SPARE], [2, KT]], base=2 * NT,
                         channel_multiplier=2 * KT, allow_small_or_imprecise_dtypes=True).then_inc(tailed, 1)

                def power(it, n):
                    ln_step.wait(eng, it, f"Cve{n}")
                    eng.tensor_tensor(rs[:, :], ve[:, :], halves[:, 0, 0:KT], ALU.pow).then_inc(root.sem, 1)

                def body(it):
                    prior = it.before()
                    if prior.runs("C"):
                        power(prior, 2)
                        par = prior.parity("C")
                        if prior.base is not None or prior.block("C") >= 2:
                            eng.wait_ge(sum_out[par], prior.pair("C") * 16)
                        ln_step.wait(eng, prior, "Ctn")
                        eng.tensor_tensor(rsum[:, par, :, :], tt[:, par, :, :], tn[:, par, :, 0:C], ALU.add).then_inc(sum_ready.sem, 1)
                    if it.runs("C"):
                        power(it, 1)
                    if it.runs("N"):
                        pn = it.parity("N")
                        waits = [(x_in[pn], it.pair("N") * 48 + 48)]
                        if it.before().runs("N"):
                            waits.append((band_ready.sem, band_ready.count(it.before(), "Nbl")))
                        waits.append((edge_ready.sem, edge_ready.count(it, "Nedge")))
                        alone(eng, *waits)
                        for kind, at_ in ((0, 0), (2, W + BT)):
                            for cc in range(CC):
                                last = eng.tensor_scalar(
                                    normed[:, cc, at_:at_ + W], raw[:, pn, cc, at_:at_ + W],
                                    edge_norm[:, kind, cc:cc + 1], edge_norm[:, kind + 1, cc:cc + 1],
                                    ALU.mult, ALU.add)
                        last.then_inc(halo_ready.sem, 1)
                    if it.runs("S"):
                        par = it.parity("S")
                        alone(eng, (route.sem, route.count(it.before(), "Dsl")))
                        for k in range(KT):
                            for j in range(2):
                                eng.indirect_dma_start(
                                    sent, bass.IndirectOffsetOnAxis(slot_s[:, par, j, k:k + 1], 0),
                                    tn[:, par, k, :], None).then_inc(scattered[par], 16)
                    if it.runs("N"):
                        pn = it.parity("N")
                        band_high.wait(eng, it, "Nbh")
                        for cc in range(CC):
                            last = eng.tensor_tensor(band[:, pn, 1, cc, :], normed[:, cc, :],
                                                     band[:, pn, 0, cc, :].bitcast(f32), ALU.subtract)
                        last.then_inc(band_ready.sem, 1)
                iterations(eng, body)
                for i in range(2):
                    eng.wait_ge(scattered[i], 32 * KT * (NB // 2))
        loop1.close()

        loop2 = ExitStack()

        def eb(name, shape, dt=f32):
            return loop2.enter_context(nc.sbuf_tensor(name, shape, dt))

        w1h = eb("w1h", [P, E, CC, C], f32r)
        w1l = eb("w1l", [P, E, CC, C], f32r)
        w2h = eb("w2h", [P, E, CC, C], f32r)
        w2l = eb("w2l", [P, E, CC, C], f32r)
        b2_all = eb("b2_all", [P, E, C])
        b1_all = eb("b1_all", [P, E, CC])
        xin = eb("xin", [P, 2, KT, C + 2])
        dest = eb("dest", [P, 2, KT])
        dest_i = eb("dest_i", [P, 2, KT], i32)
        xh = eb("xh", [P, CC, BT], f32r)
        xl = eb("xl", [P, CC, BT], f32r)
        hid = eb("hid", [P, CC, BT])
        hh = eb("hh", [P, 2, CC, BT], f32r)
        hl = eb("hl", [P, 2, CC, BT], f32r)
        yy = eb("yy", [P, 2, KT, C])
        w1hs = eb("w1hs", [P, 2, CC, C], f32r)
        w1ls = eb("w1ls", [P, 2, CC, C], f32r)
        b1s = eb("b1s", [P, 2, CC])

        split = sem("split")
        split_h = sem("split_h")
        w_late = sem("w_late")

        def lower_parts(eng, e):
            eng.tensor_tensor(w1l[:, e, :, :], w1_s[:, e, :, :], w1h[:, e, :, :].bitcast(f32), ALU.subtract)
            eng.tensor_tensor(w2l[:, e, :, :], w2_s[:, e, :, :], w2h[:, e, :, :].bitcast(f32), ALU.subtract)\
               .then_inc(split, 1)

        with nc.Block() as block:
            @block.sync
            def _(eng):
                eng.dma_start(b2_all[:, :, :].rearrange("p e c -> p (e c)"),
                              b2.rearrange("e c -> (e c)").partition_broadcast(P)).then_inc(w_late, 16)
                eng.dma_start(b1_all[:, :, :], b1).then_inc(w_late, 16)
                eng.wait_ge(w_late, 32)

            @block.gpsimd
            def _(eng):
                for e in range(E // 2, E):
                    eng.wait_ge(split_h, e + 1)
                    lower_parts(eng, e)

            @block.scalar
            def _(eng):
                eng.wait_ge(w_experts, 16 * 2 * CC)
                for e in range(E):
                    eng.activation(w1h[:, e, :, :].rearrange(flat), w1_s[:, e, :, :].rearrange(flat), ACT.Copy)
                    eng.activation(w2h[:, e, :, :].rearrange(flat), w2_s[:, e, :, :].rearrange(flat), ACT.Copy)\
                       .then_inc(split_h, 1)

            @block.vector
            def _(eng):
                for e in range(E // 2):
                    eng.wait_ge(split_h, e + 1)
                    lower_parts(eng, e)

        LAG.update(L=-2, X=-1, H=0, Y=1)
        xT_full = [sig(f"xT_full{i}", f"Xt{i}") for i in range(2)]
        xh_ready = [sig(f"xh_ready{i}", f"Xh{i}") for i in range(2)]
        xl_ready = [sig(f"xl_ready{i}", f"Xl{i}") for i in range(2)]
        h_full = [sig(f"h_full{i}", f"Hf{i}") for i in range(2)]
        hid_ready = [sig(f"hid_ready{i}", f"Hg{i}") for i in range(2)]
        hh_ready = [sig(f"hh_ready{i}", f"Hh{i}") for i in range(2)]
        hl_ready = [sig(f"hl_ready{i}", f"Hl{i}") for i in range(2)]
        y_full = [sig(f"y_full{i}", f"Yf{i}") for i in range(2)]
        y_taken = [sig(f"y_taken{i}", f"Yt{i}") for i in range(2)]
        w_ready = sig("w_ready", "Xw")
        dest_ready = sig("dest_ready", "Yd Xd")
        rows_in = [sem(f"rows_in{i}") for i in range(2)]
        rows_out = [sem(f"rows_out{i}") for i in range(2)]
        xT_bank, h_bank, y_bank = m_bank[0:2], m_bank[2:4], s_bank

        def tiles_loop(eng, n, body):
            for off in range(-2, 4):
                body(Iteration(None, off, n))
            with eng.Fori(2, n // 2 - 1) as half:
                for off in range(2):
                    body(Iteration(half, off, n))
            for off in range(n - 2, n + 2):
                body(Iteration(None, off, n))

        def entry(eng, table, at, top):
            src = table[0:1, at:at + 1] if isinstance(at, int) else table[0:1, bass.ds(at, 1)]
            return eng.value_load(src, min_val=0, max_val=top)

        def rows_of(dram, row):
            return dram[bass.ds(row, BT), :].rearrange("(p k) c -> p (k c)", k=KT)

        with nc.Block() as block:
            @block.sync
            def _(eng):
                eng.wait_ge(tails, 32 * (E + SPARE))

                def body(it):
                    if it.runs("L"):
                        par = it.parity("L")
                        row = entry(eng, row_i, it.block("L"), ROOM - BT)
                        if it.before().runs("X"):
                            alone(eng, (dest_ready.sem, dest_ready.count(it.before(), "Xd")))
                        xT_full[0].wait(eng, it.before(), "Xt0")
                        xT_full[1].wait(eng, it.before(), "Xt1")
                        eng.dma_start(xin[:, par, :, :].rearrange(flat), rows_of(sent, row))\
                           .then_inc(rows_in[par], 16)
                tiles_loop(eng, NJ, body)

            @block.gpsimd
            def _(eng):
                def body(it):
                    if it.runs("Y"):
                        par = it.parity("Y")
                        alone(eng, (dest_ready.sem, dest_ready.count(it, "Yd")),
                              *((y.sem, y.count(it, f"Yt{i}")) for i, y in enumerate(y_taken)))
                        for k in range(KT):
                            eng.indirect_dma_start(
                                answers, bass.IndirectOffsetOnAxis(dest_i[:, par, k:k + 1], 0),
                                yy[:, par, k, :], None).then_inc(rows_out[par], 16)
                tiles_loop(eng, NJ, body)
                for i in range(2):
                    eng.wait_ge(rows_out[i], 16 * KT * (NJ // 2))

            @block.tensor
            def _(eng):
                eng.wait_ge(split, E)

                def turn(it):
                    par = it.parity("X")
                    eng.wait_ge(rows_in[par], it.pair("X") * 16 + 16)
                    for c in range(CC):
                        xl_ready[c].wait_before(eng, it, f"Xl{c}")
                        for k in range(KT):
                            last = eng.transpose(xT_bank[c][:, k * P:(k + 1) * P],
                                                 xin[:, par, k, c * P:(c + 1) * P], ident[:, :])
                        last.then_inc(xT_full[c].sem, 1)

                def first(it, f):
                    par = it.parity("H")
                    if f == 0:
                        w_ready.wait(eng, it.before(), "Xw")
                        for c in range(CC):
                            xl_ready[c].wait(eng, it.before(), f"Xl{c}")
                    hid_ready[f].wait_before(eng, it, f"Hg{f}")
                    fs = slice(f * P, (f + 1) * P)
                    n = 0
                    for c in range(CC):
                        for w, xx in ((w1hs, xh), (w1hs, xl), (w1ls, xh)):
                            last = eng.matmul(h_bank[f][:, :], w[:, par, c, fs], xx[:, c, :],
                                              start=(n == 0), stop=(n == 3 * CC - 1))
                            n += 1
                    last.then_inc(h_full[f].sem, 1)

                def second(it, half, e):
                    par = it.parity("Y")
                    if half == 0:
                        for f in range(CC):
                            hl_ready[f].wait(eng, it.before(), f"Hl{f}")
                    y_taken[half].wait_before(eng, it, f"Yt{half}")
                    for k in range(2):
                        ts = slice((2 * half + k) * P, (2 * half + k + 1) * P)
                        n = 0
                        for f in range(CC):
                            for hx, w in ((hh, w2h), (hh, w2l), (hl, w2h)):
                                rhs = w[:, bass.ds(e, 1), f, :].rearrange("p e c -> p (e c)")
                                last = eng.matmul(y_bank[half][:, k * C:(k + 1) * C], hx[:, par, f, ts], rhs,
                                                  start=(n == 0), stop=(n == 3 * CC - 1))
                                n += 1
                    last.then_inc(y_full[half].sem, 1)

                def body(it):
                    h, y, x_ = it.runs("H"), it.runs("Y"), it.runs("X")
                    if h:
                        first(it, 0)
                        first(it, 1)
                    if x_:
                        turn(it)
                    if y:
                        e = entry(eng, expert_i, it.block("Y"), E - 1)
                        second(it, 0, e)
                        second(it, 1, e)
                tiles_loop(eng, NJ, body)

            @block.scalar
            def _(eng):
                eng.wait_ge(split, E)
                eng.wait_ge(w_late, 32)

                def body(it):
                    if it.runs("X"):
                        par = it.parity("X")
                        e = entry(eng, expert_i, it.block("X"), E - 1)
                        hid_ready[1].wait(eng, it.before(), "Hg1")
                        eng.activation(w1hs[:, par, :, :].rearrange(flat),
                                       w1h[:, bass.ds(e, 1), :, :].rearrange("p e a b -> p (e a b)"), ACT.Copy)
                        eng.activation(w1ls[:, par, :, :].rearrange(flat),
                                       w1l[:, bass.ds(e, 1), :, :].rearrange("p e a b -> p (e a b)"), ACT.Copy)
                        eng.activation(b1s[:, par, :], b1_all[:, bass.ds(e, 1), :].rearrange("p e a -> p (e a)"),
                                       ACT.Copy).then_inc(w_ready.sem, 1)
                    if it.runs("H"):
                        par = it.parity("H")
                        w_ready.wait(eng, it.before(), "Xw")
                        for f in range(CC):
                            h_full[f].wait(eng, it, f"Hf{f}")
                            hl_ready[f].wait(eng, it.before(), f"Hl{f}")
                            eng.activation(hid[:, f, :], h_bank[f][:, :], ACT.Gelu, bias=b1s[:, par, f:f + 1])\
                               .then_inc(hid_ready[f].sem, 1)
                    if it.runs("X"):
                        for c in range(CC):
                            xT_full[c].wait(eng, it, f"Xt{c}")
                            eng.activation(xh[:, c, :], xT_bank[c][:, :], ACT.Copy).then_inc(xh_ready[c].sem, 1)
                    if it.runs("H"):
                        for f in range(CC):
                            hid_ready[f].wait(eng, it, f"Hg{f}")
                            eng.activation(hh[:, it.parity("H"), f, :], hid[:, f, :], ACT.Copy)\
                               .then_inc(hh_ready[f].sem, 1)
                tiles_loop(eng, NJ, body)

            @block.vector
            def _(eng):
                eng.wait_ge(w_late, 32)

                def body(it):
                    if it.runs("Y"):
                        par = it.parity("Y")
                        if it.base is not None or it.block("Y") >= 2:
                            eng.wait_ge(rows_out[par], it.pair("Y") * 16 * KT)
                        dest_ready.wait(eng, it.before().before(), "Xd")
                        eng.tensor_copy(dest_i[:, par, :], dest[:, par, :]).then_inc(dest_ready.sem, 1)
                    if it.runs("X"):
                        par, at_ = it.parity("X"), it.block("X")
                        eng.wait_ge(rows_in[par], it.pair("X") * 16 + 16)
                        dest_ready.wait(eng, it, "Yd")
                        eng.scalar_tensor_tensor(dest[:, par, :], xin[:, par, :, C + 1], column(expert_f, at_),
                                                 xin[:, par, :, C], ALU.not_equal, ALU.add)\
                           .then_inc(dest_ready.sem, 1)
                        for c in range(CC):
                            xh_ready[c].wait(eng, it, f"Xh{c}")
                            eng.tensor_tensor(xl[:, c, :], xT_bank[c][:, :], xh[:, c, :].bitcast(f32),
                                              ALU.subtract).then_inc(xl_ready[c].sem, 1)
                    if it.runs("H"):
                        for f in range(CC):
                            hh_ready[f].wait(eng, it, f"Hh{f}")
                            eng.tensor_tensor(hl[:, it.parity("H"), f, :], hid[:, f, :],
                                              hh[:, it.parity("H"), f, :].bitcast(f32),
                                              ALU.subtract).then_inc(hl_ready[f].sem, 1)
                    if it.runs("Y"):
                        par = it.parity("Y")
                        e = entry(eng, expert_i, it.block("Y"), E - 1)
                        if it.base is not None or it.block("Y") >= 2:
                            eng.wait_ge(rows_out[par], it.pair("Y") * 16 * KT)
                        for half in range(2):
                            y_full[half].wait(eng, it, f"Yf{half}")
                            eng.tensor_tensor(yy[:, par, 2 * half:2 * half + 2, :],
                                              y_bank[half][:, :].rearrange("p (k c) -> p k c", k=2),
                                              b2_all[:, bass.ds(e, 1), :].broadcast_to([P, 2, C]),
                                              ALU.add).then_inc(y_taken[half].sem, 1)
                tiles_loop(eng, NJ, body)
        loop2.close()

        LAG.update(G=-1, K=0)
        loop3 = ExitStack()

        def cb(name, shape, dt=f32):
            return loop3.enter_context(nc.sbuf_tensor(name, shape, dt))

        share = cb("share", [P, KT, 2])
        got = cb("got", [P, 2, KT, 2, C])
        res = cb("res", [P, 2, KT, C])
        part = cb("part", [P, KT, C])
        tot = cb("tot", [P, 2, KT, C])
        fin = cb("fin", [P, 2, CC, BT])
        part_ready = sig("part_ready", "Kp")
        tot_ready = sig("tot_ready", "Kt")
        share_ready = sig("share_ready", "Ks")
        f_full = [sig(f"f_full{i}", f"Kf{i}") for i in range(2)]
        f_taken = [sig(f"f_taken{i}", f"Kk{i}") for i in range(2)]
        got_in = [sem(f"got_in{i}") for i in range(2)]
        res_in = [sem(f"res_in{i}") for i in range(2)]
        fin_out = [sem(f"fin_out{i}") for i in range(2)]

        with nc.Block() as block:
            @block.sync
            def _(eng):
                def body(it):
                    if it.runs("G"):
                        par = it.parity("G")
                        if it.before().runs("K"):
                            alone(eng, (part_ready.sem, part_ready.count(it.before(), "Kp")),
                                  (tot_ready.sem, tot_ready.count(it.before(), "Kt")))
                        at_ = it.block("G")
                        eng.dma_start(got[:, par, :, :, :].rearrange("p k j c -> p (k j c)"),
                                      answers[bass.ds(at_ * (2 * BT), 2 * BT), :].rearrange(
                                          "(p n) c -> p (n c)", p=P)).then_inc(got_in[par], 16)
                        eng.dma_start(res[:, par, :, :].rearrange(flat),
                                      residual_v[bass.ds(it.block("G"), 1), :, :]).then_inc(res_in[par], 16)
                tiles_loop(eng, NB, body)

            @block.vector
            def _(eng):
                def body(it):
                    if it.runs("K"):
                        par, at_ = it.parity("K"), it.block("K") * KT
                        tot_ready.wait(eng, it.before(), "Kt")
                        share_ready.wait(eng, it.before(), "Ks")
                        eng.tensor_copy(share[:, :, :], mix[:, bass.ds(at_, KT), :]).then_inc(share_ready.sem, 1)
                        share_ready.wait(eng, it, "Ks")
                        eng.wait_ge(res_in[par], it.pair("K") * 16 + 16)
                        eng.wait_ge(got_in[par], it.pair("K") * 16 + 16)
                        for k in range(KT):
                            last = eng.scalar_tensor_tensor(part[:, k, :], got[:, par, k, 0, :],
                                                            share[:, k, 0:1], res[:, par, k, :],
                                                            ALU.mult, ALU.add)
                        last.then_inc(part_ready.sem, 1)
                        part_ready.wait(eng, it, "Kp")
                        for i in range(CC):
                            f_full[i].wait(eng, it.before(), f"Kf{i}")
                        for k in range(KT):
                            last = eng.scalar_tensor_tensor(tot[:, par, k, :], got[:, par, k, 1, :],
                                                            share[:, k, 1:2], part[:, k, :],
                                                            ALU.mult, ALU.add)
                        last.then_inc(tot_ready.sem, 1)
                tiles_loop(eng, NB, body)

            @block.tensor
            def _(eng):
                def body(it):
                    if it.runs("K"):
                        par = it.parity("K")
                        tot_ready.wait(eng, it, "Kt")
                        for c in range(CC):
                            f_taken[c].wait_before(eng, it, f"Kk{c}")
                            for k in range(KT):
                                last = eng.transpose(m_bank[c][:, k * P:(k + 1) * P],
                                                     tot[:, par, k, c * P:(c + 1) * P], ident[:, :])
                            last.then_inc(f_full[c].sem, 1)
                tiles_loop(eng, NB, body)

            @block.scalar
            def _(eng):
                def body(it):
                    if it.runs("K"):
                        par = it.parity("K")
                        if it.base is not None or it.block("K") >= 2:
                            eng.wait_ge(fin_out[par], it.pair("K") * 16)
                        for c in range(CC):
                            f_full[c].wait(eng, it, f"Kf{c}")
                            eng.activation(fin[:, par, c, :], m_bank[c][:, :], ACT.Copy).then_inc(f_taken[c].sem, 1)
                        blk = it.block("K")
                        for i in range(CC):
                            f_taken[i].wait(eng, it, f"Kk{i}")
                        dst = ov[:, :, bass.ds(blk // IB, 1), bass.ds(blk % IB * BT, BT)]
                        eng.dma_start(dst, fin[:, par, :, :]).then_inc(fin_out[par], 16)
                tiles_loop(eng, NB, body)
                for i in range(2):
                    eng.wait_ge(fin_out[i], 16 * (NB // 2))
        loop3.close()


_INS = ["x", "wqT", "wkT", "wvT", "wo", "bq", "bk", "bv", "bo", "wpT", "bp", "wg", "rwT", "w1", "b1", "w2", "b2"]


def kernel(x, L0_conv_Wq, L0_conv_bq, L0_conv_Wk, L0_conv_bk, L0_conv_Wv, L0_conv_bv, L0_conv_Wo, L0_conv_bo,
           L1_attn_Wp, L1_attn_bp, L1_attn_Wg, L1_ffn_router_w, L1_ffn_w1, L1_ffn_b1, L1_ffn_w2, L1_ffn_b2):
    import numpy as np
    import concourse.bacc as bacc
    from concourse.bass_utils import run_bass_kernel_spmd

    def turned(a):
        return np.asarray(a).T

    def by_partition(a):
        a = np.asarray(a)
        a = a.reshape(a.shape[:-1] + (-1, 128))
        return np.moveaxis(a, -1, 0)

    given = dict(
        x=x, wqT=turned(L0_conv_Wq), wkT=turned(L0_conv_Wk), wvT=turned(L0_conv_Wv), wo=L0_conv_Wo,
        bq=by_partition(L0_conv_bq), bk=by_partition(L0_conv_bk), bv=by_partition(L0_conv_bv),
        bo=by_partition(L0_conv_bo), wpT=turned(L1_attn_Wp), bp=by_partition(L1_attn_bp), wg=turned(L1_attn_Wg),
        rwT=turned(L1_ffn_router_w), w1=L1_ffn_w1, b1=by_partition(L1_ffn_b1), w2=L1_ffn_w2, b2=L1_ffn_b2)
    nc = bacc.Bacc("TRN2", target_bir_lowering=False, num_devices=1)
    arrays, args = {}, {}
    for name in _INS:
        a = np.ascontiguousarray(given[name])
        arrays[f"in_{name}"] = a
        args[name] = nc.dram_tensor(f"in_{name}", a.shape, mybir.dt.from_np(a.dtype), kind="ExternalInput").ap()
    shape = arrays["in_x"].shape
    args["out"] = nc.dram_tensor("out_x", shape, mybir.dt.float32, kind="ExternalOutput").ap()
    hybrid(nc, **args)
    r = run_bass_kernel_spmd(nc, [arrays], core_ids=[0])
    return r.results[0]["out_x"]
```
